# Optimizing a Trainium2 kernel written in Bass

```python
import numpy as np
import jax
import jax.numpy as jnp

def _softmax(x, axis=-1):
    return jax.nn.softmax(x, axis=axis)

def _gelu(x):
    return jax.nn.gelu(x, approximate=True)

def _silu(x):
    return jax.nn.silu(x)

def _sigmoid(x):
    return jax.nn.sigmoid(x)

def _layernorm(x, axis=-1, eps=1e-05):
    m = jnp.mean(x, axis=axis, keepdims=True)
    v = jnp.var(x, axis=axis, keepdims=True)
    return (x - m) / jnp.sqrt(v + eps)

def _scatter_add(tgt, idx, src, axis=0):
    return tgt.at[idx].add(src)

def _segment_sum(src, seg, n):
    return jax.ops.segment_sum(src, seg, n)
kernel_name = 'mk_gnn_resnorm_d4_gnn_r32_2a44a5'

def setup_inputs(seed: int=0):
    np.random.seed(seed)
    _w = jnp.asarray

    def _rec_inputs():
        import jax
        import jax.numpy as jnp
        _gk = jax.random.key(seed)
        x = -0.0003713 + 1 * jax.random.normal(jax.random.fold_in(_gk, 1), (3125, 128), jnp.float32)
        _s = jax.random.randint(jax.random.fold_in(_gk, 2), (25000,), 0, 3125, jnp.int32)
        _d = jax.random.randint(jax.random.fold_in(_gk, 3), (25000,), 0, 3125, jnp.int32)
        _loop = jnp.arange(3125, dtype=jnp.int32)
        src = jnp.concatenate([_s, _d, _loop])
        dst = jnp.concatenate([_d, _s, _loop])
        _o = jnp.argsort(dst, stable=True)
        src = src[_o]
        dst = dst[_o]
        edge_type_8 = jax.random.randint(jax.random.fold_in(_gk, 12), (53125,), 0, 8, jnp.int32)
        return (x, src, dst, edge_type_8)
    x, src, dst, edge_type_8 = _rec_inputs()

    def _L0_gnn_setup():
        import jax, jax.numpy as jnp
        import numpy as np
        N_NODES = 3125
        N_EDGES = 18750
        HID = 128
        N_ETYPES = 8
        key = jax.random.key(seed)
        ks = jax.random.split(key, 10)
        s = 1.0 / np.sqrt(HID)
        return {'h': jax.random.normal(ks[0], (N_NODES, HID), dtype=jnp.float32), 'edge_index': jax.random.randint(ks[1], (2, N_EDGES), 0, N_NODES, dtype=jnp.int64), 'edge_type': jax.random.randint(ks[2], (N_EDGES,), 0, N_ETYPES, dtype=jnp.int64), 'message_W': jax.random.uniform(ks[3], (N_ETYPES, HID, HID), jnp.float32, -s, s), 'message_b': jax.random.uniform(ks[4], (N_ETYPES, HID), jnp.float32, -s, s), 'gru_w_ih': jax.random.uniform(ks[5], (3 * HID, HID), jnp.float32, -s, s), 'gru_w_hh': jax.random.uniform(ks[6], (3 * HID, HID), jnp.float32, -s, s), 'gru_b_ih': jax.random.uniform(ks[7], (3 * HID,), jnp.float32, -s, s), 'gru_b_hh': jax.random.uniform(ks[8], (3 * HID,), jnp.float32, -s, s)}
    _L0_gnn_all = _L0_gnn_setup()
    _L0_gnn_in = {k: v for k, v in _L0_gnn_all.items() if k in ('message_W', 'message_b', 'gru_w_ih', 'gru_w_hh', 'gru_b_ih', 'gru_b_hh')}
    del _L0_gnn_all

    def _L1_gnn_setup():
        import jax, jax.numpy as jnp
        import numpy as np
        N = 3125
        E = 50000
        D_IN = 128
        D_H = 128

        def _glorot(key, shape):
            fan_in, fan_out = (shape[1], shape[0])
            lim = np.sqrt(6.0 / (fan_in + fan_out))
            return jax.random.uniform(key, shape, jnp.float32, -lim, lim)

        def _sage_conv(h, src, dst, Wl, bl, Wr, num_nodes):
            msgs = h[src]
            agg = jax.ops.segment_sum(msgs, dst, num_segments=num_nodes)
            deg = jax.ops.segment_sum(jnp.ones((src.shape[0],), h.dtype), dst, num_segments=num_nodes)
            mean = agg / jnp.maximum(deg, 1.0)[:, None]
            return mean @ Wl.T + bl + h @ Wr.T
        key = jax.random.key(seed)
        ks = jax.random.split(key, 12)
        x = jax.random.normal(ks[0], (N, D_IN), jnp.float32)
        edge_index = jax.random.randint(ks[1], (2, E), 0, N, jnp.int64)
        return {'x': x, 'edge_index': edge_index, 'W1': _glorot(ks[2], (D_H, D_IN)), 'b1': jnp.zeros((D_H,), jnp.float32), 'W2': _glorot(ks[3], (D_H, D_H)), 'b2': jnp.zeros((D_H,), jnp.float32), 'c1_Wl': _glorot(ks[4], (D_H, D_H)), 'c1_bl': jnp.zeros((D_H,), jnp.float32), 'c1_Wr': _glorot(ks[5], (D_H, D_H)), 'c2_Wl': _glorot(ks[6], (D_H, D_H)), 'c2_bl': jnp.zeros((D_H,), jnp.float32), 'c2_Wr': _glorot(ks[7], (D_H, D_H))}
    _L1_gnn_all = _L1_gnn_setup()
    _L1_gnn_in = {k: v for k, v in _L1_gnn_all.items() if k in ('W1', 'b1', 'W2', 'b2', 'c1_Wl', 'c1_bl', 'c1_Wr', 'c2_Wl', 'c2_bl', 'c2_Wr')}
    del _L1_gnn_all

    def _L2_gnn_setup():
        import jax, jax.numpy as jnp
        import numpy as np
        IN_DIM = 128
        OUT_DIM = 128
        NUM_RELS = 8
        N_NODES = 50000
        N_EDGES = 15625
        key = jax.random.key(seed)
        k_x, k_ei_s, k_ei_d, k_et, k_w, k_sw = jax.random.split(key, 6)
        x = jax.random.normal(k_x, (N_NODES, IN_DIM), dtype=jnp.float32)
        src = jax.random.randint(k_ei_s, (N_EDGES,), 0, N_NODES)
        dst = jax.random.randint(k_ei_d, (N_EDGES,), 0, N_NODES)
        edge_index = jnp.stack([src, dst], axis=0).astype(jnp.int64)
        edge_type = jax.random.randint(k_et, (N_EDGES,), 0, NUM_RELS).astype(jnp.int64)
        bw = float(np.sqrt(6.0 / (IN_DIM + OUT_DIM)))
        weight = jax.random.uniform(k_w, (NUM_RELS, IN_DIM, OUT_DIM), dtype=jnp.float32, minval=-bw, maxval=bw)
        self_loop_weight = jax.random.uniform(k_sw, (IN_DIM, OUT_DIM), dtype=jnp.float32, minval=-bw, maxval=bw)
        bias = jnp.zeros((OUT_DIM,), dtype=jnp.float32)
        return {'x': x, 'weight': weight, 'self_loop_weight': self_loop_weight, 'bias': bias, 'edge_index': edge_index, 'edge_type': edge_type, 'num_entities': N_NODES}
    _L2_gnn_all = _L2_gnn_setup()
    _L2_gnn_in = {k: v for k, v in _L2_gnn_all.items() if k in ('weight', 'self_loop_weight', 'bias')}
    del _L2_gnn_all

    def _L3_gnn_setup():
        import jax, jax.numpy as jnp
        import numpy as np
        N_NODES = 50000
        N_EDGES = 25000
        IN_CH = 128
        HEADS = 4
        OUT_CH = 32
        key = jax.random.key(seed)
        k1, k2, k3, k4 = jax.random.split(key, 4)
        x = jax.random.normal(k1, (N_NODES, IN_CH), dtype=jnp.float32)
        edge_index = jax.random.randint(k2, (2, N_EDGES), 0, N_NODES, dtype=jnp.int64)
        limW = float(np.sqrt(6.0 / (IN_CH + HEADS * OUT_CH)))
        W = jax.random.uniform(k3, (HEADS * OUT_CH, IN_CH), minval=-limW, maxval=limW, dtype=jnp.float32)
        lima = float(np.sqrt(6.0 / (HEADS + 2 * OUT_CH)))
        att = jax.random.uniform(k4, (HEADS, 2 * OUT_CH), minval=-lima, maxval=lima, dtype=jnp.float32)
        bias = jnp.zeros((HEADS * OUT_CH,), dtype=jnp.float32)
        return {'x': x, 'edge_index': edge_index, 'W': W, 'att': att, 'bias': bias}
    _L3_gnn_all = _L3_gnn_setup()
    _L3_gnn_in = {k: v for k, v in _L3_gnn_all.items() if k in ('W', 'att', 'bias')}
    del _L3_gnn_all
    return {'x': x, 'src': src, 'dst': dst, 'edge_type_8': edge_type_8, 'L0_gnn_message_W': _L0_gnn_in['message_W'], 'L0_gnn_message_b': _L0_gnn_in['message_b'], 'L0_gnn_gru_w_ih': _L0_gnn_in['gru_w_ih'], 'L0_gnn_gru_w_hh': _L0_gnn_in['gru_w_hh'], 'L0_gnn_gru_b_ih': _L0_gnn_in['gru_b_ih'], 'L0_gnn_gru_b_hh': _L0_gnn_in['gru_b_hh'], 'L1_gnn_W1': _L1_gnn_in['W1'], 'L1_gnn_b1': _L1_gnn_in['b1'], 'L1_gnn_W2': _L1_gnn_in['W2'], 'L1_gnn_b2': _L1_gnn_in['b2'], 'L1_gnn_c1_Wl': _L1_gnn_in['c1_Wl'], 'L1_gnn_c1_bl': _L1_gnn_in['c1_bl'], 'L1_gnn_c1_Wr': _L1_gnn_in['c1_Wr'], 'L1_gnn_c2_Wl': _L1_gnn_in['c2_Wl'], 'L1_gnn_c2_bl': _L1_gnn_in['c2_bl'], 'L1_gnn_c2_Wr': _L1_gnn_in['c2_Wr'], 'L2_gnn_weight': _L2_gnn_in['weight'], 'L2_gnn_self_loop_weight': _L2_gnn_in['self_loop_weight'], 'L2_gnn_bias': _L2_gnn_in['bias'], 'L3_gnn_W': _L3_gnn_in['W'], 'L3_gnn_att': _L3_gnn_in['att'], 'L3_gnn_bias': _L3_gnn_in['bias']}

def reference(x, src, dst, edge_type_8, L0_gnn_message_W, L0_gnn_message_b, L0_gnn_gru_w_ih, L0_gnn_gru_w_hh, L0_gnn_gru_b_ih, L0_gnn_gru_b_hh, L1_gnn_W1, L1_gnn_b1, L1_gnn_W2, L1_gnn_b2, L1_gnn_c1_Wl, L1_gnn_c1_bl, L1_gnn_c1_Wr, L1_gnn_c2_Wl, L1_gnn_c2_bl, L1_gnn_c2_Wr, L2_gnn_weight, L2_gnn_self_loop_weight, L2_gnn_bias, L3_gnn_W, L3_gnn_att, L3_gnn_bias):
    import jax
    import jax.numpy as jnp

    def _L0_gnn_ref(h, edge_index, edge_type, message_W, message_b, gru_w_ih, gru_w_hh, gru_b_ih, gru_b_hh):
        import jax, jax.numpy as jnp
        import numpy as np
        N_NODES = 3125
        N_EDGES = 18750
        HID = 128
        N_ETYPES = 8
        num_nodes = h.shape[0]
        src, dst = (edge_index[0], edge_index[1])
        all_msgs = jnp.einsum('nh,thd->ntd', h, message_W) + message_b
        msg = all_msgs[src, edge_type]
        messages = jax.ops.segment_sum(msg, dst, num_segments=num_nodes)
        gi = messages @ gru_w_ih.T + gru_b_ih
        gh = h @ gru_w_hh.T + gru_b_hh
        i_r, i_z, i_n = jnp.split(gi, 3, axis=-1)
        h_r, h_z, h_n = jnp.split(gh, 3, axis=-1)
        r = jax.nn.sigmoid(i_r + h_r)
        z = jax.nn.sigmoid(i_z + h_z)
        n = jnp.tanh(i_n + r * h_n)
        return (1.0 - z) * n + z * h

    def _L1_gnn_ref(x, edge_index, W1, b1, W2, b2, c1_Wl, c1_bl, c1_Wr, c2_Wl, c2_bl, c2_Wr):
        import jax, jax.numpy as jnp
        import numpy as np
        N = 3125
        E = 50000
        D_IN = 128
        D_H = 128

        def _glorot(key, shape):
            fan_in, fan_out = (shape[1], shape[0])
            lim = np.sqrt(6.0 / (fan_in + fan_out))
            return jax.random.uniform(key, shape, jnp.float32, -lim, lim)

        def _sage_conv(h, src, dst, Wl, bl, Wr, num_nodes):
            msgs = h[src]
            agg = jax.ops.segment_sum(msgs, dst, num_segments=num_nodes)
            deg = jax.ops.segment_sum(jnp.ones((src.shape[0],), h.dtype), dst, num_segments=num_nodes)
            mean = agg / jnp.maximum(deg, 1.0)[:, None]
            return mean @ Wl.T + bl + h @ Wr.T
        src, dst = (edge_index[0], edge_index[1])
        n = x.shape[0]
        h = jax.nn.relu(x @ W1.T + b1)
        h = jax.nn.relu(_sage_conv(h, src, dst, c1_Wl, c1_bl, c1_Wr, n))
        h = jax.nn.relu(h @ W2.T + b2)
        h = jax.nn.relu(_sage_conv(h, src, dst, c2_Wl, c2_bl, c2_Wr, n))
        return h

    def _L2_gnn_ref(x, weight, self_loop_weight, bias, edge_index, edge_type, num_entities):
        import jax, jax.numpy as jnp
        import numpy as np
        IN_DIM = 128
        OUT_DIM = 128
        NUM_RELS = 8
        N_NODES = 50000
        N_EDGES = 15625
        hr = jnp.einsum('nd,rdo->rno', x, weight)
        src, dst = (edge_index[0], edge_index[1])
        msg = hr[edge_type, src]
        agg = jax.ops.segment_sum(msg, dst, num_segments=num_entities)
        out = agg + x @ self_loop_weight + bias
        return jax.nn.relu(out)

    def _L3_gnn_ref(x, edge_index, W, att, bias):
        import jax, jax.numpy as jnp
        import numpy as np
        N_NODES = 50000
        N_EDGES = 25000
        IN_CH = 128
        HEADS = 4
        OUT_CH = 32
        n = x.shape[0]
        heads, two_c = att.shape
        out_ch = two_c // 2
        loop = jnp.arange(n, dtype=edge_index.dtype)
        src = jnp.concatenate([edge_index[0], loop])
        dst = jnp.concatenate([edge_index[1], loop])
        h = (x @ W.T).reshape(n, heads, out_ch)
        h_src = h[src]
        h_dst = h[dst]
        e = jnp.einsum('ehc,hc->eh', h_src, att[:, :out_ch]) + jnp.einsum('ehc,hc->eh', h_dst, att[:, out_ch:])
        e = jax.nn.leaky_relu(e, negative_slope=0.2)
        e_max = jax.ops.segment_max(e, dst, num_segments=n)
        alpha = jnp.exp(e - e_max[dst])
        a_sum = jax.ops.segment_sum(alpha, dst, num_segments=n)
        alpha = alpha / jnp.maximum(a_sum[dst], 1e-10)
        weighted = h_src * alpha[..., None]
        out = jax.ops.segment_sum(weighted, dst, num_segments=n)
        out = out.reshape(n, heads * out_ch)
        return out + bias
    edge_index = jnp.stack([src, dst])
    x = _layernorm(x + _L0_gnn_ref(x, edge_index, edge_type_8, L0_gnn_message_W, L0_gnn_message_b, L0_gnn_gru_w_ih, L0_gnn_gru_w_hh, L0_gnn_gru_b_ih, L0_gnn_gru_b_hh), axis=-1)
    x = _layernorm(x + _L1_gnn_ref(x, edge_index, L1_gnn_W1, L1_gnn_b1, L1_gnn_W2, L1_gnn_b2, L1_gnn_c1_Wl, L1_gnn_c1_bl, L1_gnn_c1_Wr, L1_gnn_c2_Wl, L1_gnn_c2_bl, L1_gnn_c2_Wr), axis=-1)
    x = _layernorm(x + _L2_gnn_ref(x, L2_gnn_weight, L2_gnn_self_loop_weight, L2_gnn_bias, edge_index, edge_type_8, 3125), axis=-1)
    x = _layernorm(x + _L3_gnn_ref(x, edge_index, L3_gnn_W, L3_gnn_att, L3_gnn_bias), axis=-1)
    return x

_drawn_inputs = setup_inputs


def setup_inputs(seed=0):
    import zlib

    import numpy as np

    out = dict(_drawn_inputs(seed))
    spreads = {'L1_gnn_b1': (0.0, 0.1),
     'L1_gnn_b2': (0.0, 0.1),
     'L1_gnn_c1_bl': (0.0, 0.1),
     'L1_gnn_c2_bl': (0.0, 0.1),
     'L2_gnn_bias': (0.0, 0.271),
     'L3_gnn_bias': (0.0, 0.1)}
    factors = {'L0_gnn_gru_b_ih': 2.93, 'L0_gnn_gru_b_hh': 4.294}
    for name, (base, spread) in spreads.items():
        noise = np.random.default_rng([zlib.crc32(name.encode()), seed]).standard_normal(out[name].shape)
        drawn = base * np.exp(spread * noise) if base else spread * noise
        out[name] = jnp.asarray(drawn.astype(out[name].dtype))
    for name, factor in factors.items():
        out[name] = (out[name] * factor).astype(out[name].dtype)
    return out
```

```python
import concourse.bass as bass
from concourse import mybir
from concourse.alu_op_type import AluOpType as ALU
from contextlib import ExitStack

F32 = mybir.dt.float32
BF16 = mybir.dt.bfloat16
I32 = mybir.dt.int32
ACT = mybir.ActivationFunctionType
AX = mybir.AxisListType
ds = bass.ds

P = 128
NODES, EDGES, FEAT, TYPES = 3125, 53125, 128, 8
HEADS, HEAD_F = 4, 32
TILES = -(-NODES // P)
PADN = TILES * P
FULL = NODES // P
LASTN = NODES - FULL * P
ROWS = -(-EDGES // P)
PADE = ROWS * P
PER = ROWS
LASTP = EDGES - (P - 1) * PER
PAIRS = ROWS + TILES - 1
PQ = PAIRS // 4
SLOTS = 8
TURNS = PAIRS // SLOTS
GROUP = 5
GROUPS = TILES // GROUP
GW = GROUP * P
AW = 132
TROW = FEAT + HEADS + 6
FAR = 2.0 ** 100
EPS = 1e-5
LAG_TURN, LAG_MASK, LAG_MAX, LAG_SPREAD, LAG_LOGIT, LAG_EXP, LAG_WEIGHT, LAG_SUM, LAG_ADD = 1, 2, 2, 3, 4, 4, 5, 5, 6
LAG_LAST = 6
assert PQ * 4 == PAIRS and TURNS * SLOTS == PAIRS and GROUPS * GROUP == TILES and 0 < LASTP <= PER


class Chunk:

    def __init__(self, turn, at):
        self.n = turn * SLOTS + at
        self.slot = at % SLOTS
        self.round = turn + at // SLOTS

    def count(self, more=0, k=0):
        return self.n + (1 + more + k * PAIRS)

    def within(self):
        return not isinstance(self.n, int) or 0 <= self.n < PAIRS


def over_chunks(eng, step, lag, peeled):
    for turn in range(peeled):
        for b in range(SLOTS):
            step(lambda delay: Chunk(turn, b - delay))
    with eng.Fori(peeled, TURNS) as turn:
        for b in range(SLOTS):
            step(lambda delay: Chunk(turn, b - delay))
    for b in range(lag):
        step(lambda delay: Chunk(TURNS, b - delay))


def build(nc, x, src, dst, etype, L0W, L0b, w_ih, w_hh, b_ih, b_hh, W1, b1, W2, b2, c1l, c1b, c1r,
          c2l, c2b, c2r, L2W, L2S, L2b, L3W, L3a, L3b, out):
    with ExitStack() as ctx:
        def sb(name, shape, dt=F32):
            return ctx.enter_context(nc.sbuf_tensor(name, shape, dt))

        def sem(name):
            return ctx.enter_context(nc.semaphore(name))

        typed_table = nc.dram_tensor("typed_table", (PADN * TYPES, FEAT), F32, kind="Internal").ap()
        node_table = nc.dram_tensor("node_table", (PADN, FEAT), F32, kind="Internal").ap()
        gat_table = nc.dram_tensor("gat_table", (PADN, TROW), F32, kind="Internal").ap()
        list_code = nc.dram_tensor("list_code", (PADE, 1), I32, kind="Internal").ap()
        list_dst = nc.dram_tensor("list_dst", (PADE, 1), I32, kind="Internal").ap()
        pair_tiles = nc.dram_tensor("pair_tiles", (PAIRS, 1), I32, kind="Internal").ap()

        PS = ctx.enter_context(nc.psum_tensor("PS", [P, 8 * 512], F32))

        xn = sb("xn", [P, PADN])
        xT = sb("xT", [P, PADN])
        hT = sb("hT", [P, PADN])
        rows = sb("rows", [P, TILES * TROW])
        acc = sb("acc", [P, (TILES + 1) * AW])
        typed_out = sb("typed_out", [P, GROUP, TYPES * FEAT])
        L0W_sb = sb("L0W_sb", [P, TYPES, FEAT])
        L2W_sb = sb("L2W_sb", [P, TYPES, FEAT])
        L0b_bc = sb("L0b_bc", [P, TYPES * FEAT])
        L3b_bc = sb("L3b_bc", [P, FEAT])
        wraw = sb("wraw", [P, 13, FEAT])
        wT = sb("wT", [P, 12, FEAT])
        w3a = sb("w3a", [P, FEAT + 2 * HEADS])
        att = sb("att", [P, 2 * HEADS])
        selfw = sb("selfw", [P, FEAT])
        bcol = sb("bcol", [P, 12])
        identf = sb("identf", [P, P])
        identb = sb("identb", [P, P], BF16)
        ident4 = sb("ident4", [P, HEADS, P], BF16)
        headsel = sb("headsel", [12, HEADS, P], BF16)
        onesf = sb("onesf", [P, P])
        below = sb("below", [P, P])
        lane_i = sb("lane_i", [P, P], I32)
        lane = sb("lane", [P, P])
        epst = sb("epst", [P, 1])
        rdeg = sb("rdeg", [P, TILES])

        e_dst = sb("e_dst", [P, PER], I32)
        e_next = sb("e_next", [P, PER], I32)
        e_code = sb("e_code", [P, PER], I32)
        e_type = sb("e_type", [P, PER], I32)
        e_bkt = sb("e_bkt", [P, PER], I32)
        e_f = sb("e_f", [P, PER])
        e_g = sb("e_g", [P, PER])
        e_pos = sb("e_pos", [P, PER])
        e_cum = sb("e_cum", [P, PER])
        e_zero = sb("e_zero", [P, PER])
        rowtot = sb("rowtot", [P, TILES + 1])
        bk = sb("bk", [P, 12, TILES + 1])
        bki = sb("bki", [P, 4, TILES + 1], I32)
        bad = sb("bad", [P, 2])
        flag = sb("flag", [P, 1], I32)
        base = sb("base", [P, TILES + 1])
        scat = sb("scat", [P, 3], I32)
        pr = sb("pr", [PQ, 6, 4])
        prc = sb("prc", [PQ, 4, TILES])
        prd = sb("prd", [PQ, 4, TILES])
        pair_no = sb("pair_no", [PQ, 4], I32)
        pair_row = sb("pair_row", [PQ, 4], I32)
        pair_tile = sb("pair_tile", [PQ, 4], I32)
        got_i = sb("got_i", [PQ, 8, P], I32)
        got_f = sb("got_f", [PQ, 8, P])
        chunk_code = sb("chunk_code", [P, PAIRS], I32)
        chunk_src = sb("chunk_src", [P, PAIRS], I32)
        chunk_dst = sb("chunk_dst", [P, PAIRS])
        tile_at = sb("tile_at", [1, PAIRS], I32)

        ix = sb("ix", [P, SLOTS], I32)
        g = sb("g", [P, SLOTS, TROW])
        oh = sb("oh", [P, SLOTS, P])
        ohm = sb("ohm", [P, SLOTS, P], BF16)
        ohT = sb("ohT", [P, SLOTS, P])
        aT = sb("aT", [12, SLOTS, P], BF16)
        cm = sb("cm", [P, SLOTS, 12])
        bm = sb("bm", [P, SLOTS, 8])
        state = sb("state", [P, TILES + 1, 8])
        wd = sb("wd", [P, SLOTS, 8])
        rescale = sb("rescale", [P, SLOTS, HEADS])
        wm = sb("wm", [P, SLOTS, HEADS, HEAD_F + 1])

        mT = sb("mT", [P, GW])
        cT = sb("cT", [P, GW])
        mn = sb("mn", [P, GW])
        gr = sb("gr", [P, GW])
        gz = sb("gz", [P, GW])
        gn = sb("gn", [P, GW])
        u1 = sb("u1", [P, GW])
        u2 = sb("u2", [P, GW])
        stats = sb("stats", [P, GROUP, 6])
        mv = sb("mv", [P, GROUP, 2])
        sd = sb("sd", [P, GROUP])
        rs = sb("rs", [P, GROUP])
        den = sb("den", [P, TILES, HEADS])
        spl = sb("spl", [P, 2, TILES, HEADS])

        loaded_x, loaded_w, loaded_e = sem("loaded_x"), sem("loaded_w"), sem("loaded_e")
        pool_seq, const_ready = sem("pool_seq"), sem("const_ready")
        dve_seq, dve_pace = sem("dve_seq"), sem("dve_pace")
        code_ready, order_known = sem("code_ready"), sem("order_known")
        bucket_sums, bucket_base, bad_sum = sem("bucket_sums"), sem("bucket_base"), sem("bad_sum")
        rowtot_ready, bad_ready = sem("rowtot_ready"), sem("bad_ready")
        place_ready, scattered, list_ready = sem("place_ready"), sem("scattered"), sem("list_ready")
        pairs_ready, pair_dma = sem("pairs_ready"), sem("pair_dma")
        rows_got, rows_float, rows_turned, chunks_ready = sem("rows_got"), sem("rows_float"), sem("rows_turned"), sem("chunks_ready")
        weights_turned, weights_ready, att_zeroed = sem("weights_turned"), sem("weights_ready"), sem("att_zeroed")
        tiles_loaded, sort_seq = sem("tiles_loaded"), sem("sort_seq")
        x_padded, x_turned, xT_ready = sem("x_padded"), sem("x_turned"), sem("xT_ready")
        pace = sem("pace")
        typed_done = [sem(f"typed_done{k}") for k in range(2)]
        typed_evac = [sem(f"typed_evac{k}") for k in range(2)]
        typed_written = [[sem(f"typed_written{k}_{j}") for j in range(GROUP)] for k in range(2)]
        table_written = {k: sem(f"table_written{k}") for k in (1, 2, 4,)}
        arrived = [sem(f"arrived{b}") for b in range(SLOTS)]
        ix_ready = sem("ix_ready")
        oh_ready = sem("oh_ready")
        product = sem("product")
        acc_done = sem("acc_done")
        acc_zero = sem("acc_zero")
        agg_turned = {k: sem(f"agg_turned{k}") for k in (0, 1, 2,)}
        agg_T = {k: sem(f"agg_T{k}") for k in (0, 1, 2,)}
        mean_ready = [sem(f"mean_ready{k}") for k in range(4)]
        linear_done = {k: sem(f"linear_done{k}") for k in (0, 1, 2, 3,)}
        hidden_T = {k: sem(f"hidden_T{k}") for k in (0, 1, 2, 3,)}
        linear2_done = {k: sem(f"linear2_done{k}") for k in (1,)}
        hidden2_T = {k: sem(f"hidden2_T{k}") for k in (1,)}
        rows_turned_back = {k: sem(f"rows_turned_back{k}") for k in (0, 1, 3,)}
        rows_ready = [sem(f"rows_ready{k}") for k in range(4)]
        gates_done, gates_rz, n_pre, n_ready = sem("gates_done"), sem("gates_rz"), sem("n_pre"), sem("n_ready")
        y_T = {k: sem(f"y_T{k}") for k in (0, 2, 3,)}
        y_turned = {k: sem(f"y_turned{k}") for k in (0, 2, 3,)}
        var_ready = [sem(f"var_ready{k}") for k in range(5)]
        std_ready = [sem(f"std_ready{k}") for k in range(5)]
        x_ready = [sem(f"x_ready{k}") for k in range(5)]
        x_again = {k: sem(f"x_again{k}") for k in (0, 2, 3,)}
        x_T = {k: sem(f"x_T{k}") for k in (0, 2, 3,)}
        gat_rows, gat_state = sem("gat_rows"), sem("gat_state")
        turned, turned_sb, masked, seg_max = sem("turned"), sem("turned_sb"), sem("masked"), sem("seg_max")
        spread, logits, weights, weighted = sem("spread"), sem("logits"), sem("weights"), sem("weighted")
        out_rows, out_written = sem("out_rows"), sem("out_written")

        block = ctx.enter_context(nc.Block())

        IH, HH, W1i, W2i, C1L, C1R, C2L, C2R = 0, 3, 6, 7, 8, 9, 10, 11
        L3i = 12
        B_IH, B_HH, B1, B2, B_C1, B_C2, B_L2, B_R, B_Z = 0, 3, 6, 7, 8, 9, 10, 11, 0

        def region(r, width=GW):
            return PS[:, 1024 * r:1024 * r + width]

        def bank(b, n=512, p=P):
            return PS[0:p, 512 * b:512 * b + n]

        def acc_cols(tile, n):
            return acc[:, ds(tile * AW, n)]

        @block.sync
        def _(sp):
            sp.wait_ge(x_padded, 1)
            sp.dma_start(xn[:, 0:FULL * P].rearrange("p (t d) -> p t d", d=FEAT),
                         x[0:FULL * P, :].rearrange("(t p) d -> p t d", p=P)).then_inc(loaded_x, 16)
            sp.dma_start(xn[0:LASTN, FULL * P:PADN], x[FULL * P:NODES, :]).then_inc(loaded_x, 16)
            sp.wait_ge(x_padded, 2)
            for tile, arr in ((e_dst, dst), (e_code, src), (e_type, etype)):
                sp.dma_start(tile[0:P - 1, :], arr[0:(P - 1) * PER].rearrange("(p t) -> p t", t=PER)).then_inc(loaded_e, 16)
                sp.dma_start(tile[P - 1:P, 0:LASTP], arr[(P - 1) * PER:EDGES].rearrange("(a t) -> a t", a=1)).then_inc(loaded_e, 16)
            sp.dma_start(e_next[0:P - 1, :], dst[1:1 + (P - 1) * PER].rearrange("(p t) -> p t", t=PER)).then_inc(loaded_e, 16)
            sp.dma_start(e_next[P - 1:P, 0:LASTP - 1], dst[(P - 1) * PER + 1:EDGES].rearrange("(a t) -> a t", a=1)).then_inc(loaded_e, 16)

            def typed(k):
                with sp.Fori(0, GROUPS) as i:
                    for j in range(GROUP):
                        sp.wait_ge(typed_evac[k], i * (2 * GROUP) + 2 * j + 2)
                        sp.dma_start(typed_table[ds(i * (GW * TYPES) + j * P * TYPES, P * TYPES), :].rearrange("(p t) d -> p (t d)", t=TYPES),
                                     typed_out[:, j, :]).then_inc(typed_written[k][j], 16)

            def plain(k):
                with sp.Fori(0, GROUPS) as i:
                    sp.wait_ge(rows_ready[k], i + 1)
                    sp.dma_start(node_table[ds(i * GW, GW), :].rearrange("(j p) d -> p j d", p=P),
                                 rows[:, ds(i * GW, GW)].rearrange("p (j d) -> p j d", d=FEAT)).then_inc(table_written[k + 1], 16)

            sp.wait_ge(pairs_ready, 1)
            sp.dma_start(pair_tiles.rearrange("(j p) a -> p (j a)", p=PQ), pair_tile[:, :], allow_slow_non_contiguous=True).then_inc(pair_dma, 16)
            sp.wait_ge(pair_dma, 16)
            sp.dma_start(tile_at[:, :], pair_tiles.rearrange("n a -> a n")).then_inc(tiles_loaded, 16)
            typed(0)
            plain(0)
            plain(1)
            typed(1)
            sp.wait_ge(gat_rows, 1)
            sp.dma_start(gat_table.rearrange("(t p) d -> p t d", p=P),
                         rows[:, :].rearrange("p (t d) -> p t d", d=TROW)).then_inc(table_written[4], 16)
            with sp.Fori(0, GROUPS - 1) as i:
                sp.wait_ge(out_rows, i + 1)
                sp.dma_start(out[ds(i * GW, GW), :].rearrange("(j p) d -> p j d", p=P),
                             rows[:, ds(i * GW, GW)].rearrange("p (j d) -> p j d", d=FEAT)).then_inc(out_written, 16)
            sp.wait_ge(out_rows, GROUPS)
            sp.dma_start(out[(GROUPS - 1) * GW:FULL * P, :].rearrange("(j p) d -> p j d", p=P),
                         rows[:, (GROUPS - 1) * GW:FULL * P].rearrange("p (j d) -> p j d", d=FEAT)).then_inc(out_written, 16)
            sp.dma_start(out[FULL * P:NODES, :], rows[0:LASTN, FULL * P:PADN]).then_inc(out_written, 16)
            sp.wait_ge(out_written, 16 * (GROUPS + 1))

        @block.gpsimd
        def _(pool):
            steps = [0]

            def link(ins):
                steps[0] += 1
                ins.then_inc(pool_seq, 1)
                pool.wait_ge(pool_seq, steps[0])

            pool.memset(xn[:, FULL * P:PADN], 0.0).then_inc(x_padded, 1)
            pool.memset(e_dst[:, :], PADN)
            pool.memset(e_next[:, :], PADN)
            pool.memset(e_code[:, :], 0)
            pool.memset(e_type[:, :], 0).then_inc(x_padded, 1)
            link(pool.memset(identf[:, :], 0.0))
            link(pool.affine_select(out=identf[:, :], in_=identf[:, :], compare_op=ALU.not_equal, fill=1.0,
                                    base=0, pattern=[[-1, P]], channel_multiplier=1))
            link(pool.tensor_copy(identb[:, :], identf[:, :]))
            link(pool.memset(ident4[:, :, :], 0.0))
            link(pool.affine_select(out=ident4[:, :, :], in_=ident4[:, :, :], compare_op=ALU.not_equal, fill=FAR,
                                    base=0, pattern=[[0, HEADS], [-1, P]], channel_multiplier=1))
            link(pool.memset(onesf[:, :], 1.0))
            link(pool.affine_select(out=below[:, :], in_=onesf[:, :], compare_op=ALU.is_gt, fill=0.0,
                                    base=0, pattern=[[1, P]], channel_multiplier=-1))
            link(pool.memset(headsel[:, :, :], 1.0))
            link(pool.affine_select(out=headsel[:, :, :], in_=headsel[:, :, :], compare_op=ALU.is_ge, fill=0.0,
                                    base=0, pattern=[[-3, HEADS], [0, P]], channel_multiplier=1))
            link(pool.affine_select(out=headsel[:, :, :], in_=headsel[:, :, :], compare_op=ALU.is_ge, fill=0.0,
                                    base=2, pattern=[[3, HEADS], [0, P]], channel_multiplier=-1))
            link(pool.iota(lane_i[:, :], pattern=[[1, P]], base=0, channel_multiplier=0))
            link(pool.tensor_copy(lane[:, :], lane_i[:, :]))
            link(pool.iota(pair_no[:, :], pattern=[[PQ, 4]], base=0, channel_multiplier=1))
            link(pool.memset(epst[:, :], EPS))
            pool.memset(g[:, :, :], 1.0).then_inc(const_ready, 1)

            pool.wait_ge(code_ready, 1)
            pool.wait_ge(order_known, 1)
            disorder = pool.value_load(flag[0:1, 0:1], min_val=0, max_val=1)
            with pool.If(disorder > 0):
                pool.wait_ge(place_ready, 1)
                with pool.Fori(0, PER) as t:
                    pool.tensor_copy(scat[:, 0:1], e_pos[:, ds(t, 1)])
                    pool.tensor_copy(scat[:, 1:2], e_code[:, ds(t, 1)])
                    pool.tensor_copy(scat[:, 2:3], e_dst[:, ds(t, 1)]).then_inc(place_ready, 1)
                    pool.wait_ge(place_ready, t + 2)
                    pool.sem_inc(pace, 1)
                    pool.indirect_dma_start(list_code, bass.IndirectOffsetOnAxis(ap=scat[:, 0:1], axis=0),
                                            scat[:, 1:2], None).then_inc(scattered, 16)
                    pool.indirect_dma_start(list_dst, bass.IndirectOffsetOnAxis(ap=scat[:, 0:1], axis=0),
                                            scat[:, 2:3], None).then_inc(scattered, 16)
                    pool.wait_ge(scattered, t * 32 + 32)
                    pool.sem_inc(pace, 1)
            with pool.Else():
                pool.dma_start(list_code.rearrange("(p t) a -> p (t a)", t=PER), e_code[:, :]).then_inc(scattered, 16)
                pool.dma_start(list_dst.rearrange("(p t) a -> p (t a)", t=PER), e_dst[:, :]).then_inc(scattered, 16)
                pool.wait_ge(scattered, 32)
                pool.sem_inc(pace, 1)

            pool.wait_ge(pairs_ready, 1)
            code_rows = list_code.rearrange("(r e) a -> r (e a)", e=P)
            dst_rows = list_dst.rearrange("(r e) a -> r (e a)", e=P)
            for j in range(4):
                where = bass.IndirectOffsetOnAxis(ap=pair_row[:, j:j + 1], axis=0)
                pool.indirect_dma_start(got_i[:, j, :], None, code_rows, where).then_inc(rows_got, 16)
                pool.indirect_dma_start(got_i[:, 4 + j, :], None, dst_rows, where).then_inc(rows_got, 16)

            def gathers(k, table, width, written, total):
                for s in written:
                    pool.wait_ge(s, total)

                def beat(c):
                    c = c(0)
                    if c.within():
                        pool.wait_ge(ix_ready, c.count(0, k))
                        pool.sem_inc(pace, 1)
                        pool.indirect_dma_start(g[:, c.slot, 0:width], None, table,
                                                bass.IndirectOffsetOnAxis(ap=ix[:, c.slot:c.slot + 1], axis=0))\
                            .then_inc(arrived[c.slot], 16)
                over_chunks(pool, beat, 0, 1)

            gathers(0, typed_table, FEAT, typed_written[0], 16 * GROUPS)
            gathers(1, node_table, FEAT, [table_written[1]], 16 * GROUPS)
            gathers(2, node_table, FEAT, [table_written[2]], 16 * GROUPS)
            gathers(3, typed_table, FEAT, typed_written[1], 16 * GROUPS)
            gathers(4, gat_table, TROW, [table_written[4]], 16)

        @block.scalar
        def _(act):
            for n, w in ((W1i, W1), (W2i, W2), (C1L, c1l), (C1R, c1r), (C2L, c2l), (C2R, c2r), (L3i, L3W)):
                act.dma_start(wraw[:, n, :], w).then_inc(loaded_w, 16)
            for n, w in ((IH, w_ih), (HH, w_hh)):
                act.dma_start(wraw[:, n:n + 3, :], w.rearrange("(k p) d -> p k d", p=P)).then_inc(loaded_w, 16)
            act.dma_start(L0W_sb[:, :, :], L0W.rearrange("t h d -> h t d")).then_inc(loaded_w, 16)
            act.dma_start(L2W_sb[:, :, :], L2W.rearrange("t h d -> h t d")).then_inc(loaded_w, 16)
            act.dma_start(selfw[:, :], L2S).then_inc(loaded_w, 16)
            act.dma_start(L0b_bc[:, :], L0b.rearrange("t d -> (t d)").partition_broadcast(P)).then_inc(loaded_w, 16)
            act.dma_start(L3b_bc[:, :], L3b.partition_broadcast(P)).then_inc(loaded_w, 16)
            for n, b in ((B_IH, b_ih), (B_HH, b_hh)):
                act.dma_start(bcol[:, n:n + 3], b.rearrange("(k p) -> p k", p=P), allow_slow_non_contiguous=True).then_inc(loaded_w, 16)
            for n, b in ((B1, b1), (B2, b2), (B_C1, c1b), (B_C2, c2b), (B_L2, L2b)):
                act.dma_start(bcol[:, n:n + 1], b.rearrange("(p a) -> p a", a=1), allow_slow_non_contiguous=True).then_inc(loaded_w, 16)
            act.wait_ge(att_zeroed, 1)
            for h in range(HEADS):
                for side in range(2):
                    act.dma_start(att[h * HEAD_F:(h + 1) * HEAD_F, side * HEADS + h:side * HEADS + h + 1],
                                  L3a[h, side * HEAD_F:(side + 1) * HEAD_F].rearrange("(p a) -> p a", a=1), allow_slow_non_contiguous=True).then_inc(loaded_w, 16)
            act.wait_ge(weights_turned, 1)
            act.activation(wT[:, :, :].rearrange("p k d -> p (k d)"), PS[:, 0:12 * FEAT], ACT.Copy).then_inc(weights_ready, 1)
            act.activation(w3a[:, :], bank(4, FEAT + 2 * HEADS), ACT.Copy).then_inc(weights_ready, 1)
            with act.Fori(0, GROUPS) as i:
                act.wait_ge(x_turned, i + 1)
                act.activation(xT[:, ds(i * GW, GW)], region(3), ACT.Copy).then_inc(xT_ready, 1)
            act.wait_ge(rows_turned, 1)
            act.activation(chunk_code[:, :], bank(0, PAIRS), ACT.Copy).then_inc(chunks_ready, 1)
            act.activation(chunk_dst[:, :], bank(1, PAIRS), ACT.Copy).then_inc(chunks_ready, 1)

            def columns(k, cols):
                def beat(c):
                    c = c(0)
                    if not c.within():
                        return
                    if not isinstance(c.n, int) or c.n >= SLOTS:
                        act.wait_ge(product, c.count(-SLOTS, k))
                    act.activation(ix[:, c.slot:c.slot + 1], cols[:, ds(c.n, 1)], ACT.Copy).then_inc(ix_ready, 1)
                over_chunks(act, beat, 0, 1)

            def norm(k, i):
                act.wait_ge(var_ready[k], i + 1)
                act.activation(sd[:, :], mv[:, :, 1], ACT.Sqrt, bias=epst[:, 0:1]).then_inc(std_ready[k], 1)

            act.wait_ge(chunks_ready, 3)
            columns(0, chunk_code)

            with act.Fori(0, GROUPS) as i:
                act.wait_ge(agg_turned[0], i + 1)
                act.activation(mT[:, :], region(0), ACT.Copy).then_inc(agg_T[0], 1)
                act.wait_ge(gates_done, i * 4 + 1)
                act.activation(gr[:, :], region(1), ACT.Sigmoid, bias=bcol[:, B_R:B_R + 1]).then_inc(gates_rz, 1)
                act.wait_ge(gates_done, i * 4 + 2)
                act.activation(gz[:, :], region(2), ACT.Sigmoid, bias=bcol[:, B_Z:B_Z + 1]).then_inc(gates_rz, 1)
                act.wait_ge(n_pre, i + 1)
                act.activation(gn[:, :], u2[:, :], ACT.Tanh, bias=bcol[:, B_IH + 2:B_IH + 3]).then_inc(n_ready, 1)
                norm(0, i)
                act.wait_ge(x_again[0], i + 1)
                act.activation(xT[:, ds(i * GW, GW)], region(2), ACT.Copy).then_inc(x_T[0], 1)
                act.wait_ge(linear_done[0], i + 1)
                act.activation(hT[:, ds(i * GW, GW)], region(3), ACT.Relu, bias=bcol[:, B1:B1 + 1]).then_inc(hidden_T[0], 1)
            columns(1, chunk_src)

            with act.Fori(0, GROUPS) as i:
                act.wait_ge(agg_turned[1], i + 1)
                act.activation(mT[:, :], region(0), ACT.Copy).then_inc(agg_T[1], 1)
                act.wait_ge(linear_done[1], i + 1)
                act.activation(cT[:, :], region(1), ACT.Relu, bias=bcol[:, B_C1:B_C1 + 1]).then_inc(hidden_T[1], 1)
                act.wait_ge(linear2_done[1], i + 1)
                act.activation(hT[:, ds(i * GW, GW)], region(2), ACT.Relu, bias=bcol[:, B2:B2 + 1]).then_inc(hidden2_T[1], 1)
            columns(2, chunk_src)

            with act.Fori(0, GROUPS) as i:
                act.wait_ge(agg_turned[2], i + 1)
                act.activation(mT[:, :], region(0), ACT.Copy).then_inc(agg_T[2], 1)
                act.wait_ge(linear_done[2], i + 1)
                act.activation(cT[:, :], region(1), ACT.Relu, bias=bcol[:, B_C2:B_C2 + 1]).then_inc(hidden_T[2], 1)
                norm(2, i)
                act.wait_ge(x_again[2], i + 1)
                act.activation(xT[:, ds(i * GW, GW)], region(3), ACT.Copy).then_inc(x_T[2], 1)
            columns(3, chunk_code)

            with act.Fori(0, GROUPS) as i:
                act.wait_ge(linear_done[3], i + 1)
                act.activation(cT[:, :], region(0), ACT.Relu, bias=bcol[:, B_L2:B_L2 + 1]).then_inc(hidden_T[3], 1)
                norm(3, i)
                act.wait_ge(x_again[3], i + 1)
                act.activation(xT[:, ds(i * GW, GW)], region(2), ACT.Copy).then_inc(x_T[3], 1)

            def beat(c):
                now = c(0)
                if now.within():
                    if not isinstance(now.n, int) or now.n >= SLOTS:
                        act.wait_ge(product, now.count(-SLOTS, 4))
                    act.activation(ix[:, now.slot:now.slot + 1], chunk_src[:, ds(now.n, 1)], ACT.Copy).then_inc(ix_ready, 1)
                t = c(LAG_TURN)
                if t.within():
                    act.wait_ge(turned, t.count())
                    act.activation(ohT[:, t.slot, :], bank(t.slot % 2, P), ACT.Identity, bias=onesf[:, 0:1])
                    act.activation(aT[:, t.slot, :], PS[0:12, 512 * (t.slot % 2) + P:512 * (t.slot % 2) + 2 * P],
                                   ACT.Copy).then_inc(turned_sb, 1)
                w = c(LAG_EXP)
                if w.within():
                    act.wait_ge(logits, w.count())
                    act.activation(rescale[:, w.slot, :], wd[:, w.slot, 4:8], ACT.Exp)
                    act.activation(wm[:, w.slot, :, HEAD_F], wd[:, w.slot, 0:4], ACT.Exp).then_inc(weights, 1)
            over_chunks(act, beat, LAG_LAST, 2)

            with act.Fori(0, GROUPS) as i:
                norm(4, i)

        @block.tensor
        def _(pe):
            def turn_group(r, source, i):
                for j in range(GROUP):
                    last = pe.transpose(PS[:, 1024 * r + j * P:1024 * r + (j + 1) * P],
                                        source(i, j), identf[:, :])
                return last

            def linear(r, parts):
                for c0, n in ((0, 512), (512, GW - 512)):
                    for q, (w, feats) in enumerate(parts):
                        last = pe.matmul(PS[:, 1024 * r + c0:1024 * r + c0 + n], w, feats(c0, n),
                                         start=(q == 0), stop=(q == len(parts) - 1))
                return last

            def whole(tile):
                return lambda c0, n: tile[:, c0:c0 + n]

            def of(tile, i):
                return lambda c0, n: tile[:, ds(i * GW + c0, n)]

            def node_tile(i, j):
                return xn[:, ds(i * GW + j * P, P)]

            pe.wait_ge(const_ready, 1)
            pe.wait_ge(rowtot_ready, 1)
            pe.matmul(bank(6, TILES + 1), onesf[:, :], rowtot[:, :], start=True, stop=True).then_inc(bucket_sums, 1)
            pe.matmul(bank(7, TILES + 1), below[:, :], rowtot[:, :], start=True, stop=True).then_inc(bucket_base, 1)
            pe.wait_ge(bad_ready, 1)
            pe.matmul(bank(5, 1), onesf[:, :], bad[:, 0:1], start=True, stop=True).then_inc(bad_sum, 1)
            pe.wait_ge(loaded_w, 16 * 29)
            for n in range(12):
                pe.transpose(PS[:, n * P:(n + 1) * P], wraw[:, n, :], identf[:, :])
            pe.transpose(PS[:, 2048:2048 + P], wraw[:, L3i, :], identf[:, :])
            pe.matmul(PS[:, 2048 + P:2048 + P + 2 * HEADS], wraw[:, L3i, :], att[:, :], start=True, stop=True).then_inc(weights_turned, 1)
            pe.wait_ge(loaded_x, 32)
            pe.wait_ge(pairs_ready, 1)
            for i in range(GROUPS):
                turn_group(3, node_tile, i).then_inc(x_turned, 1)
                pe.wait_ge(xT_ready, i + 1)

            def typed(k, w):
                def unit(i, j, half, first):
                    u = 2 * j + half
                    if not (first and u < 5):
                        pe.wait_ge(typed_evac[k], i * (2 * GROUP) + u - 4)
                    pe.matmul(bank(u % 5), xT[:, ds(i * GW + j * P, P)],
                              w[:, 4 * half:4 * half + 4, :].rearrange("p t d -> p (t d)"), start=True, stop=True)\
                        .then_inc(typed_done[k], 1)
                for i in range(GROUPS):
                    for j in range(GROUP):
                        for half in range(2):
                            unit(i, j, half, i == 0)

            pe.wait_ge(weights_ready, 2)
            pe.wait_ge(xT_ready, GROUPS)
            typed(0, L0W_sb)
            pe.wait_ge(typed_evac[0], 10 * GROUPS)
            pe.wait_ge(rows_float, 1)
            for j in range(4):
                pe.transpose(PS[:, j * PQ:(j + 1) * PQ], got_f[:, j, :], identf[0:PQ, 0:PQ])
            for j in range(4):
                last = pe.transpose(PS[:, 512 + j * PQ:512 + (j + 1) * PQ], got_f[:, 4 + j, :], identf[0:PQ, 0:PQ])
            last.then_inc(rows_turned, 1)
            pe.wait_ge(chunks_ready, 2)

            def sums(k, width):
                def beat(c):
                    c = c(0)
                    if not c.within():
                        return
                    pe.wait_ge(oh_ready, c.count(0, k))
                    pe.wait_ge(arrived[c.slot], (c.round + (1 + k * TURNS)) * 16)
                    if not isinstance(c.n, int) or c.n >= 4:
                        pe.wait_ge(acc_done, c.count(-4, k))
                    pe.matmul(bank(c.slot % 4, width), oh[:, c.slot, :], g[:, c.slot, 0:width],
                              start=True, stop=True).then_inc(product, 1)
                over_chunks(pe, beat, 0, 1)

            sums(0, FEAT + 1)

            pe.wait_ge(acc_done, 1 * PAIRS)
            for i in range(GROUPS):
                turn_group(0, lambda i, j: acc[:, ds(i * (GROUP * AW) + j * AW, P)], i).then_inc(agg_turned[0], 1)
                pe.wait_ge(agg_T[0], i + 1)
                linear(1, [(wT[:, IH, :], whole(mT)), (wT[:, HH, :], of(xT, i))]).then_inc(gates_done, 1)
                linear(2, [(wT[:, IH + 1, :], whole(mT)), (wT[:, HH + 1, :], of(xT, i))]).then_inc(gates_done, 1)
                linear(3, [(wT[:, HH + 2, :], of(xT, i))]).then_inc(gates_done, 1)
                linear(0, [(wT[:, IH + 2, :], whole(mT))]).then_inc(gates_done, 1)
                pe.wait_ge(y_T[0], i + 1)
                turn_group(1, lambda i, j: u1[:, j * P:(j + 1) * P], i).then_inc(y_turned[0], 1)
                pe.wait_ge(x_ready[0], i + 1)
                turn_group(2, node_tile, i).then_inc(x_again[0], 1)
                pe.wait_ge(x_T[0], i + 1)
                linear(3, [(wT[:, W1i, :], of(xT, i))]).then_inc(linear_done[0], 1)
                pe.wait_ge(hidden_T[0], i + 1)
                turn_group(0, lambda i, j: hT[:, ds(i * GW + j * P, P)], i).then_inc(rows_turned_back[0], 1)
                pe.wait_ge(rows_ready[0], i + 1)
            sums(1, FEAT)

            pe.wait_ge(acc_done, 2 * PAIRS)
            for i in range(GROUPS):
                pe.wait_ge(mean_ready[1], i + 1)
                turn_group(0, lambda i, j: mn[:, j * P:(j + 1) * P], i).then_inc(agg_turned[1], 1)
                pe.wait_ge(agg_T[1], i + 1)
                linear(1, [(wT[:, C1L, :], whole(mT)), (wT[:, C1R, :], of(hT, i))]).then_inc(linear_done[1], 1)
                pe.wait_ge(hidden_T[1], i + 1)
                linear(2, [(wT[:, W2i, :], whole(cT))]).then_inc(linear2_done[1], 1)
                pe.wait_ge(hidden2_T[1], i + 1)
                turn_group(3, lambda i, j: hT[:, ds(i * GW + j * P, P)], i).then_inc(rows_turned_back[1], 1)
                pe.wait_ge(rows_ready[1], i + 1)
            sums(2, FEAT)

            pe.wait_ge(acc_done, 3 * PAIRS)
            for i in range(GROUPS):
                pe.wait_ge(mean_ready[2], i + 1)
                turn_group(0, lambda i, j: mn[:, j * P:(j + 1) * P], i).then_inc(agg_turned[2], 1)
                pe.wait_ge(agg_T[2], i + 1)
                linear(1, [(wT[:, C2L, :], whole(mT)), (wT[:, C2R, :], of(hT, i))]).then_inc(linear_done[2], 1)
                pe.wait_ge(y_T[2], i + 1)
                turn_group(2, lambda i, j: u1[:, j * P:(j + 1) * P], i).then_inc(y_turned[2], 1)
                pe.wait_ge(x_ready[2], i + 1)
                turn_group(3, node_tile, i).then_inc(x_again[2], 1)
                pe.wait_ge(x_T[2], i + 1)
            typed(1, L2W_sb)
            pe.wait_ge(typed_evac[1], 10 * GROUPS)
            sums(3, FEAT)

            pe.wait_ge(acc_done, 4 * PAIRS)
            for i in range(GROUPS):
                for j in range(GROUP):
                    pe.matmul(PS[:, j * P:(j + 1) * P], selfw[:, :], xT[:, ds(i * GW + j * P, P)], start=True, stop=False)
                    last = pe.matmul(PS[:, j * P:(j + 1) * P], acc[:, ds(i * (GROUP * AW) + j * AW, P)], identf[:, :],
                                     start=False, stop=True)
                last.then_inc(linear_done[3], 1)
                pe.wait_ge(y_T[3], i + 1)
                turn_group(1, lambda i, j: u1[:, j * P:(j + 1) * P], i).then_inc(y_turned[3], 1)
                pe.wait_ge(x_ready[3], i + 1)
                turn_group(2, node_tile, i).then_inc(x_again[3], 1)
                pe.wait_ge(x_T[3], i + 1)
                WA = FEAT + 2 * HEADS
                for j in range(GROUP):
                    at = 3072 + (j * WA if j < 3 else 512 + (j - 3) * WA)
                    last = pe.matmul(PS[:, at:at + WA], xT[:, ds(i * GW + j * P, P)], w3a[:, :], start=True, stop=True)
                last.then_inc(rows_turned_back[3], 1)
                pe.wait_ge(rows_ready[3], i + 1)

            def beat(c):
                t = c(LAG_TURN)
                if t.within():
                    pe.wait_ge(oh_ready, t.count(0, 4))
                    pe.wait_ge(arrived[t.slot], (t.round + (1 + 4 * TURNS)) * 16)
                    if not isinstance(t.n, int) or t.n >= 2:
                        pe.wait_ge(turned_sb, t.count(-2))
                    pe.matmul(bank(t.slot % 2, P), ohm[:, t.slot, :], identb[:, :], start=True, stop=True)
                    pe.matmul(PS[0:12, 512 * (t.slot % 2) + P:512 * (t.slot % 2) + 2 * P],
                              g[:, t.slot, FEAT + HEADS:TROW].bitcast(BF16), identb[:, :], start=True, stop=True).then_inc(turned, 1)
                m = c(LAG_MASK)
                if m.within():
                    pe.wait_ge(turned_sb, m.count())
                    if not isinstance(m.n, int) or m.n >= 2:
                        pe.wait_ge(seg_max, m.count(-2))
                    b = 2 + m.slot % 2
                    for h in range(HEADS):
                        here = PS[:, 512 * b + h * P:512 * b + (h + 1) * P]
                        pe.matmul(here, ohm[:, m.slot, :], ident4[:, h, :], start=True, stop=False)
                        last = pe.matmul(here, headsel[:, h, :], aT[:, m.slot, :], start=False, stop=True)
                    last.then_inc(masked, 1)
                f = c(LAG_SPREAD)
                if f.within():
                    pe.wait_ge(seg_max, f.count())
                    if not isinstance(f.n, int) or f.n >= 2:
                        pe.wait_ge(logits, f.count(-2))
                    pe.matmul(bank(4 + f.slot % 2, 8), ohT[:, f.slot, :], bm[:, f.slot, :], start=True, stop=True).then_inc(spread, 1)
                s = c(LAG_SUM)
                if s.within():
                    pe.wait_ge(weighted, s.count())
                    if not isinstance(s.n, int) or s.n >= 2:
                        pe.wait_ge(acc_done, s.count(-2, 4))
                    pe.matmul(bank(6 + s.slot % 2, AW), oh[:, s.slot, :], wm[:, s.slot, :, :].rearrange("p h f -> p (h f)"),
                              start=True, stop=True).then_inc(product, 1)
            over_chunks(pe, beat, LAG_LAST, 2)

        @block.vector
        def _(dve):
            steps = [0]

            def link(ins):
                steps[0] += 1
                ins.then_inc(dve_seq, 1)
                dve.wait_ge(dve_seq, steps[0])

            dve.memset(att[:, :], 0.0).then_inc(att_zeroed, 1)
            dve.wait_ge(const_ready, 1)
            dve.wait_ge(loaded_e, 16 * 8)
            dve.scalar_tensor_tensor(out=e_code[:, :], in0=e_code[:, :], scalar=float(TYPES), in1=e_type[:, :],
                                     op0=ALU.mult, op1=ALU.add).then_inc(code_ready, 1)
            link(dve.tensor_single_scalar(e_bkt[:, :], e_dst[:, :], 7, ALU.arith_shift_right))
            link(dve.tensor_single_scalar(e_next[:, :], e_next[:, :], 7, ALU.arith_shift_right))
            link(dve.tensor_tensor(e_f[:, :], e_bkt[:, :], e_next[:, :], ALU.is_gt))
            dve.tensor_reduce(bad[:, 0:1], e_f[:, :], AX.X, ALU.max).then_inc(bad_ready, 1)
            link(dve.tensor_copy(e_g[:, :], e_bkt[:, :]))
            for b in range(TILES + 1):
                link(dve.tensor_scalar(e_f[:, :], e_g[:, :], float(b), None, ALU.is_equal))
                ins = dve.tensor_reduce(rowtot[:, b:b + 1], e_f[:, :], AX.X, ALU.add)
                if b < TILES:
                    link(ins)
            ins.then_inc(rowtot_ready, 1)
            dve.wait_ge(bad_sum, 1)
            dve.tensor_scalar(flag[:, :], bank(5, 1), 1.0, None, ALU.min).then_inc(order_known, 1)
            CNT, END, START, FIRST, LAST, NUM, PEND, PSTART, SHIFT, HAS, ZERO = range(11)
            dve.wait_ge(bucket_base, 1)
            link(dve.tensor_copy(bk[:, CNT, :], bank(6, TILES + 1)))
            link(dve.memset(bk[:, ZERO, :], 0.0))
            link(dve.tensor_tensor_scan(bk[:, END, :], bk[:, CNT, :], bk[:, ZERO, :], 0.0, ALU.add, ALU.add))
            link(dve.tensor_tensor(bk[:, START, :], bk[:, END, :], bk[:, CNT, :], ALU.subtract))
            link(dve.tensor_tensor(base[:, :], bank(7, TILES + 1), bk[:, START, :], ALU.add))
            link(dve.tensor_scalar(base[:, :], base[:, :], -1.0, None, ALU.add))
            link(dve.tensor_copy(bki[:, 0, :], bk[:, START, :]))
            link(dve.tensor_scalar(bki[:, 1, :], bk[:, END, :], -1.0, 0.0, ALU.add, ALU.max))
            link(dve.tensor_single_scalar(bki[:, 2, :], bki[:, 0, :], 7, ALU.arith_shift_right))
            link(dve.tensor_single_scalar(bki[:, 3, :], bki[:, 1, :], 7, ALU.arith_shift_right))
            link(dve.tensor_copy(bk[:, FIRST, :], bki[:, 2, :]))
            link(dve.tensor_copy(bk[:, LAST, :], bki[:, 3, :]))
            link(dve.tensor_scalar(bk[:, HAS, :], bk[:, CNT, :], 1.0, None, ALU.min))
            link(dve.tensor_tensor(bk[:, NUM, :], bk[:, LAST, :], bk[:, FIRST, :], ALU.subtract))
            link(dve.scalar_tensor_tensor(out=bk[:, NUM, :], in0=bk[:, NUM, :], scalar=1.0, in1=bk[:, HAS, :],
                                          op0=ALU.add, op1=ALU.mult))
            link(dve.tensor_tensor_scan(bk[:, PEND, :], bk[:, NUM, :], bk[:, ZERO, :], 0.0, ALU.add, ALU.add))
            link(dve.tensor_tensor(bk[:, PSTART, :], bk[:, PEND, :], bk[:, NUM, :], ALU.subtract))
            link(dve.tensor_tensor(bk[:, SHIFT, :], bk[:, FIRST, :], bk[:, PSTART, :], ALU.subtract))
            NO, TILE, ROW = range(3)
            link(dve.tensor_copy(pr[:, NO, :], pair_no[:, :]))
            shape = [PQ, 4, TILES]

            def per_tile(ap):
                return ap.unsqueeze(1).broadcast_to(shape)

            def per_pair(ap):
                return ap.unsqueeze(2).broadcast_to(shape)

            link(dve.tensor_tensor(prc[:, :, :], per_pair(pr[:, NO, :]), per_tile(bk[0:PQ, PEND, 0:TILES]), ALU.is_ge))
            link(dve.tensor_reduce(pr[:, TILE, :], prc[:, :, :], AX.X, ALU.add))
            link(dve.tensor_tensor(prd[:, :, :], per_pair(pr[:, TILE, :]), per_tile(lane[0:PQ, 0:TILES]), ALU.is_equal))
            link(dve.tensor_tensor(prd[:, :, :], prd[:, :, :], per_tile(bk[0:PQ, SHIFT, 0:TILES]), ALU.mult))
            link(dve.tensor_reduce(pr[:, ROW, :], prd[:, :, :], AX.X, ALU.add))
            link(dve.tensor_tensor(pr[:, ROW, :], pr[:, ROW, :], pr[:, NO, :], ALU.add))
            link(dve.tensor_copy(pair_tile[:, :], pr[:, TILE, :]))
            dve.tensor_scalar(pair_row[:, :], pr[:, ROW, :], float(ROWS - 1), None, ALU.min).then_inc(pairs_ready, 1)

            disorder = dve.value_load(flag[0:1, 0:1], min_val=0, max_val=1)
            with dve.If(disorder > 0):
                dve.memset(e_pos[:, :], 0.0).then_inc(sort_seq, 1)
                dve.memset(e_zero[:, :], 0.0).then_inc(sort_seq, 1)
                dve.wait_ge(sort_seq, 2)
                with dve.Fori(0, TILES + 1) as b:
                    dve.tensor_scalar(e_f[:, :], e_g[:, :], lane[:, ds(b, 1)], None, ALU.is_equal).then_inc(sort_seq, 1)
                    dve.wait_ge(sort_seq, b * 4 + 3)
                    dve.tensor_tensor_scan(e_cum[:, :], e_f[:, :], e_zero[:, :], 0.0, ALU.add, ALU.add).then_inc(sort_seq, 1)
                    dve.wait_ge(sort_seq, b * 4 + 4)
                    dve.scalar_tensor_tensor(out=e_cum[:, :], in0=e_cum[:, :], scalar=base[:, ds(b, 1)], in1=e_f[:, :],
                                             op0=ALU.add, op1=ALU.mult).then_inc(sort_seq, 1)
                    dve.wait_ge(sort_seq, b * 4 + 5)
                    dve.tensor_tensor(e_pos[:, :], e_pos[:, :], e_cum[:, :], ALU.add).then_inc(sort_seq, 1)
                    dve.wait_ge(sort_seq, b * 4 + 6)
                dve.memset(bad[:, 1:2], 0.0).then_inc(place_ready, 1)
            with dve.Else():
                dve.memset(bad[:, 1:2], 0.0).then_inc(place_ready, 1)

            dve.wait_ge(loaded_w, 16 * 29)
            link(dve.tensor_tensor(bcol[:, B_R:B_R + 1], bcol[:, B_IH:B_IH + 1], bcol[:, B_HH:B_HH + 1], ALU.add))
            link(dve.tensor_tensor(bcol[:, B_Z:B_Z + 1], bcol[:, B_IH + 1:B_IH + 2], bcol[:, B_HH + 1:B_HH + 2], ALU.add))

            def typed(k, finish):
                def unit(i, j, half, first):
                    u = 2 * j + half
                    dve.wait_ge(typed_done[k], i * (2 * GROUP) + u + 1)
                    if not first and half == 0:
                        dve.wait_ge(typed_written[k][j], i * 16)
                    finish(typed_out[:, j, 512 * half:512 * half + 512], bank(u % 5), half).then_inc(typed_evac[k], 1)
                for j in range(GROUP):
                    for half in range(2):
                        unit(0, j, half, True)
                with dve.Fori(1, GROUPS) as i:
                    for j in range(GROUP):
                        for half in range(2):
                            unit(i, j, half, False)

            typed(0, lambda o, p, half: dve.tensor_tensor(o, p, L0b_bc[:, 512 * half:512 * half + 512], ALU.add))

            dve.wait_ge(rows_got, 16 * 8)
            link(dve.tensor_copy(got_f[:, 0:4, :], got_i[:, 0:4, :]))
            link(dve.tensor_scalar(pr[:, TILE, :], pr[:, TILE, :], float(-P), None, ALU.mult))
            for j in range(4):
                ins = dve.tensor_scalar(got_f[:, 4 + j, :], got_i[:, 4 + j, :], pr[:, TILE, j:j + 1], None, ALU.add)
            ins.then_inc(rows_float, 1)
            dve.wait_ge(chunks_ready, 2)
            dve.tensor_single_scalar(chunk_src[:, :], chunk_code[:, :], 3, ALU.arith_shift_right).then_inc(chunks_ready, 1)
            dve.wait_ge(tiles_loaded, 16)

            def one_hot(k, c):
                if not isinstance(c.n, int) or c.n >= SLOTS:
                    dve.wait_ge(product, c.count(-SLOTS, k))
                return dve.tensor_scalar(oh[:, c.slot, :], lane[:, :], chunk_dst[:, ds(c.n, 1)], None, ALU.is_equal)

            def tile_of(c):
                return dve.value_load(tile_at[0:1, ds(c.n, 1)], min_val=0, max_val=TILES)

            def sums(k, width):
                dve.memset(acc[:, :], 0.0).then_inc(acc_zero, 1)
                dve.wait_ge(acc_zero, k + 1)

                def beat(c):
                    now, add = c(0), c(4)
                    if now.within():
                        one_hot(k, now).then_inc(oh_ready, 1)
                    if add.within():
                        tile = tile_of(add)
                        dve.wait_ge(product, add.count(0, k))
                        if not isinstance(add.n, int) or add.n >= 1:
                            dve.wait_ge(acc_done, add.count(-1, k))
                        dve.tensor_tensor(acc_cols(tile, width), acc_cols(tile, width), bank(add.slot % 4, width),
                                          ALU.add).then_inc(acc_done, 1)
                over_chunks(dve, beat, 4, 1)

            class Seq:

                def __init__(self, s, per):
                    self.s, self.per, self.i, self.n = s, per, 0, 0

                def begin(self, i):
                    self.i, self.n = i, 0

                def __call__(self, ins):
                    self.n += 1
                    ins.then_inc(self.s, 1)
                    dve.wait_ge(self.s, self.i * self.per + self.n)

                def end(self):
                    assert self.n == self.per, self.n

            def norm(k, i, seq, source, target):
                for j in range(GROUP):
                    ins = dve.bn_stats(stats[:, j, :], source(j))
                seq(ins)
                dve.sem_inc(dve_pace, 1)
                for j in range(GROUP):
                    ins = dve.bn_aggr(mv[:, j, :], stats[:, j, :])
                ins.then_inc(var_ready[k], 1)
                dve.wait_ge(std_ready[k], i + 1)
                seq(dve.reciprocal(rs[:, :], sd[:, :]))
                for j in range(GROUP):
                    ins = dve.tensor_scalar(target(i, j), source(j), mv[:, j, 0:1], rs[:, j:j + 1], ALU.subtract, ALU.mult)
                return ins

            def new_x(i, j):
                return xn[:, ds(i * GW + j * P, P)]

            sums(0, FEAT + 1)
            dve.wait_ge(acc_done, 1 * PAIRS)
            degree = acc[:, :].rearrange("p (t a) -> p t a", a=AW)[:, 0:TILES, FEAT]
            link(dve.tensor_scalar(rdeg[:, :], degree, 1.0, None, ALU.max))
            link(dve.reciprocal(rdeg[:, :], rdeg[:, :]))
            seq = Seq(sem("dve_gru"), 6)
            with dve.Fori(0, GROUPS) as i:
                seq.begin(i)
                cols = ds(i * GW, GW)
                dve.wait_ge(gates_rz, i * 2 + 1)
                dve.wait_ge(gates_done, i * 4 + 3)
                seq(dve.scalar_tensor_tensor(out=u1[:, :], in0=region(3), scalar=bcol[:, B_HH + 2:B_HH + 3], in1=gr[:, :],
                                             op0=ALU.add, op1=ALU.mult))
                dve.wait_ge(gates_done, i * 4 + 4)
                dve.tensor_tensor(u2[:, :], u1[:, :], region(0), ALU.add).then_inc(n_pre, 1)
                dve.wait_ge(n_ready, i + 1)
                seq(dve.tensor_tensor(u1[:, :], xT[:, cols], gn[:, :], ALU.subtract))
                dve.wait_ge(gates_rz, i * 2 + 2)
                seq(dve.tensor_tensor(u1[:, :], u1[:, :], gz[:, :], ALU.mult))
                seq(dve.tensor_tensor(u1[:, :], u1[:, :], gn[:, :], ALU.add))
                dve.tensor_tensor(u1[:, :], u1[:, :], xT[:, cols], ALU.add).then_inc(y_T[0], 1)
                dve.wait_ge(y_turned[0], i + 1)
                norm(0, i, seq, lambda j: PS[:, 1024 + j * P:1024 + (j + 1) * P], new_x).then_inc(x_ready[0], 1)
                dve.wait_ge(rows_turned_back[0], i + 1)
                dve.tensor_copy(rows[:, cols], region(0)).then_inc(rows_ready[0], 1)
                seq.end()

            def mean(k, i):
                dve.tensor_tensor(mn[:, :].rearrange("p (j d) -> p j d", d=P),
                                  acc[:, ds(i * (GROUP * AW), GROUP * AW)].rearrange("p (j a) -> p j a", a=AW)[:, :, 0:P],
                                  rdeg[:, ds(i * GROUP, GROUP)].unsqueeze(2).broadcast_to([P, GROUP, P]), ALU.mult)\
                    .then_inc(mean_ready[k], 1)

            sums(1, FEAT)
            dve.wait_ge(acc_done, 2 * PAIRS)
            with dve.Fori(0, GROUPS) as i:
                mean(1, i)
                dve.wait_ge(rows_turned_back[1], i + 1)
                dve.tensor_copy(rows[:, ds(i * GW, GW)], region(3)).then_inc(rows_ready[1], 1)
            sums(2, FEAT)
            dve.wait_ge(acc_done, 3 * PAIRS)
            seq = Seq(sem("dve_sage"), 2)
            with dve.Fori(0, GROUPS) as i:
                seq.begin(i)
                mean(2, i)
                dve.wait_ge(hidden_T[2], i + 1)
                dve.tensor_tensor(u1[:, :], xT[:, ds(i * GW, GW)], cT[:, :], ALU.add).then_inc(y_T[2], 1)
                dve.wait_ge(y_turned[2], i + 1)
                norm(2, i, seq, lambda j: PS[:, 2048 + j * P:2048 + (j + 1) * P], new_x).then_inc(x_ready[2], 1)
                seq.end()

            typed(1, lambda o, p, half: dve.tensor_copy(o, p))
            sums(3, FEAT)
            dve.wait_ge(acc_done, 4 * PAIRS)
            seq = Seq(sem("dve_rel"), 2)
            rows_t = rows[:, :].rearrange("p (t d) -> p t d", d=TROW)
            with dve.Fori(0, GROUPS) as i:
                seq.begin(i)
                dve.wait_ge(hidden_T[3], i + 1)
                dve.tensor_tensor(u1[:, :], xT[:, ds(i * GW, GW)], cT[:, :], ALU.add).then_inc(y_T[3], 1)
                dve.wait_ge(y_turned[3], i + 1)
                norm(3, i, seq, lambda j: PS[:, 1024 + j * P:1024 + (j + 1) * P], new_x).then_inc(x_ready[3], 1)
                dve.wait_ge(rows_turned_back[3], i + 1)
                WA = FEAT + 2 * HEADS
                for at, t0, n in ((3072, 0, 3), (3584, 3, 2)):
                    p = PS[:, at:at + n * WA].rearrange("p (t d) -> p t d", d=WA)
                    dve.tensor_copy(rows[:, ds(i * (GROUP * TROW) + t0 * TROW, n * TROW)].rearrange("p (t d) -> p t d", d=TROW)[:, :, 0:FEAT + HEADS],
                                    p[:, :, 0:FEAT + HEADS])
                    ins = dve.tensor_copy(state[:, ds(i * GROUP + t0, n), 0:HEADS], p[:, :, FEAT + HEADS:WA])
                ins.then_inc(rows_ready[3], 1)
                seq.end()

            dve.wait_ge(rows_ready[3], GROUPS)
            score = rows_t[:, :, FEAT:FEAT + HEADS]
            part = [rows[:, :].bitcast(BF16).rearrange("p (t d) -> p t d", d=2 * TROW)[:, :, 2 * (FEAT + HEADS) + j:2 * TROW:3] for j in range(3)]
            link(dve.tensor_copy(part[0], score))
            link(dve.tensor_tensor(spl[:, 0, :, :], score, part[0], ALU.subtract))
            link(dve.tensor_copy(part[1], spl[:, 0, :, :]))
            link(dve.tensor_tensor(spl[:, 1, :, :], spl[:, 0, :, :], part[1], ALU.subtract))
            dve.tensor_copy(part[2], spl[:, 1, :, :]).then_inc(gat_rows, 1)
            dve.memset(state[:, TILES, :], 0.0)
            link(dve.tensor_tensor(spl[:, 0, :, :], score, state[:, 0:TILES, 0:HEADS], ALU.add))
            link(dve.scalar_tensor_tensor(out=state[:, 0:TILES, HEADS:2 * HEADS], in0=spl[:, 0, :, :], scalar=0.2,
                                          in1=spl[:, 0, :, :], op0=ALU.mult, op1=ALU.max))
            dve.memset(acc[:, TILES * AW:], 0.0)
            acc_f = acc[:, 0:TILES * AW].rearrange("p (t h f) -> p t h f", t=TILES, h=HEADS)
            dve.memset(acc_f[:, :, :, HEAD_F:HEAD_F + 1].rearrange("p t h f -> p (t h) f"), 1.0)
            dve.tensor_copy(acc_f[:, :, :, 0:HEAD_F], rows_t[:, :, 0:FEAT].rearrange("p t (h f) -> p t h f", h=HEADS))\
                .then_inc(acc_zero, 1)
            dve.wait_ge(acc_zero, 5)

            max_step, max_kept, logit_step, rescaled = sem("max_step"), sem("max_kept"), sem("logit_step"), sem("rescaled")

            def beat(c):
                now = c(0)
                if now.within():
                    one_hot(4, now)
                    dve.tensor_scalar(ohm[:, now.slot, :], lane[:, :], chunk_dst[:, ds(now.n, 1)], 1.0,
                                      ALU.is_equal, ALU.subtract).then_inc(oh_ready, 1)
                m = c(LAG_MAX)
                if m.within():
                    s = m.slot
                    tile = tile_of(m)
                    dve.wait_ge(masked, m.count())
                    dve.tensor_reduce(cm[:, s, 0:4], bank(2 + s % 2).rearrange("p (h e) -> p h e", h=HEADS), AX.X, ALU.max)\
                        .then_inc(max_step, 1)
                    if not isinstance(m.n, int) or m.n >= 1:
                        dve.wait_ge(max_kept, m.count(-1))
                    dve.wait_ge(max_step, m.n * 5 + 1)
                    here = state[:, ds(tile, 1), :].rearrange("p a b -> p (a b)")
                    dve.tensor_tensor(cm[:, s, 4:8], cm[:, s, 0:4], here[:, 0:4], ALU.add).then_inc(max_step, 1)
                    dve.wait_ge(max_step, m.n * 5 + 2)
                    dve.scalar_tensor_tensor(out=cm[:, s, 8:12], in0=cm[:, s, 4:8], scalar=0.2, in1=cm[:, s, 4:8],
                                             op0=ALU.mult, op1=ALU.max).then_inc(max_step, 1)
                    dve.wait_ge(max_step, m.n * 5 + 3)
                    dve.tensor_tensor(bm[:, s, 4:8], cm[:, s, 8:12], here[:, 4:8], ALU.max).then_inc(max_step, 1)
                    dve.wait_ge(max_step, m.n * 5 + 4)
                    dve.tensor_tensor(wd[:, s, 4:8], here[:, 4:8], bm[:, s, 4:8], ALU.subtract).then_inc(max_step, 1)
                    dve.tensor_copy(bm[:, s, 0:4], here[:, 0:4]).then_inc(seg_max, 1)
                    dve.wait_ge(max_step, m.n * 5 + 5)
                    dve.tensor_scalar(here[:, 4:8], bm[:, s, 4:8], 1.0, None, ALU.mult).then_inc(max_kept, 1)
                e = c(LAG_LOGIT)
                if e.within():
                    s = e.slot
                    f = bank(4 + s % 2, 8)
                    dve.wait_ge(spread, e.count())
                    dve.tensor_tensor(cm[:, s, 0:4], g[:, s, FEAT:FEAT + HEADS], f[:, 0:4], ALU.add).then_inc(logit_step, 1)
                    dve.wait_ge(logit_step, e.n * 3 + 1)
                    dve.scalar_tensor_tensor(out=cm[:, s, 4:8], in0=cm[:, s, 0:4], scalar=0.2, in1=cm[:, s, 0:4],
                                             op0=ALU.mult, op1=ALU.max).then_inc(logit_step, 1)
                    dve.wait_ge(logit_step, e.n * 3 + 2)
                    dve.tensor_tensor(cm[:, s, 8:12], cm[:, s, 4:8], f[:, 4:8], ALU.subtract).then_inc(logit_step, 1)
                    dve.wait_ge(logit_step, e.n * 3 + 3)
                    dve.tensor_scalar(wd[:, s, 0:4], cm[:, s, 8:12], 0.0, None, ALU.min).then_inc(logits, 1)
                w = c(LAG_WEIGHT)
                if w.within():
                    s = w.slot
                    dve.wait_ge(weights, w.count())
                    dve.tensor_tensor(wm[:, s, :, 0:HEAD_F], g[:, s, 0:FEAT].rearrange("p (h f) -> p h f", h=HEADS),
                                      wm[:, s, :, HEAD_F:HEAD_F + 1].broadcast_to([P, HEADS, HEAD_F]), ALU.mult)\
                        .then_inc(weighted, 1)
                a = c(LAG_ADD)
                if a.within():
                    s = a.slot
                    tile = tile_of(a)
                    sums_here = acc_cols(tile, AW)
                    if not isinstance(a.n, int) or a.n >= 1:
                        dve.wait_ge(acc_done, a.count(-1, 4))
                    dve.tensor_tensor(sums_here.rearrange("p (h f) -> p h f", h=HEADS), sums_here.rearrange("p (h f) -> p h f", h=HEADS),
                                      rescale[:, s, :].unsqueeze(2).broadcast_to([P, HEADS, HEAD_F + 1]), ALU.mult)\
                        .then_inc(rescaled, 1)
                    dve.wait_ge(rescaled, a.count())
                    dve.wait_ge(product, a.count(0, 4))
                    dve.tensor_tensor(sums_here, sums_here, bank(6 + s % 2, AW), ALU.add).then_inc(acc_done, 1)
            over_chunks(dve, beat, LAG_LAST, 2)

            dve.wait_ge(acc_done, 5 * PAIRS)
            accv = acc[:, 0:TILES * AW].rearrange("p (t h f) -> p t h f", t=TILES, h=HEADS)
            link(dve.tensor_scalar(den[:, :, :], accv[:, :, :, HEAD_F], 1e-10, None, ALU.max))
            link(dve.reciprocal(den[:, :, :], den[:, :, :]))
            seq = Seq(sem("dve_out"), 5)
            with dve.Fori(0, GROUPS) as i:
                seq.begin(i)
                here = acc[:, ds(i * (GROUP * AW), GROUP * AW)].rearrange("p (q f) -> p q f", f=HEAD_F + 1)
                seq(dve.tensor_tensor(u1[:, :].rearrange("p (q f) -> p q f", f=HEAD_F), here[:, :, 0:HEAD_F],
                                      den[:, ds(i * GROUP, GROUP), :].rearrange("p t h -> p (t h)").unsqueeze(2)
                                      .broadcast_to([P, GROUP * HEADS, HEAD_F]), ALU.mult))
                seq(dve.tensor_tensor(u1[:, :].rearrange("p (j d) -> p j d", d=P), u1[:, :].rearrange("p (j d) -> p j d", d=P),
                                      L3b_bc[:, :].unsqueeze(1).broadcast_to([P, GROUP, P]), ALU.add))
                seq(dve.tensor_tensor(u1[:, :], u1[:, :], xn[:, ds(i * GW, GW)], ALU.add))
                norm(4, i, seq, lambda j: u1[:, j * P:(j + 1) * P],
                     lambda i, j: rows[:, ds(i * GW + j * P, P)]).then_inc(out_rows, 1)
                dve.wait_ge(out_rows, i + 1)
                seq.end()


_INS = ['x', 'src', 'dst', 'edge_type_8', 'L0_gnn_message_W', 'L0_gnn_message_b', 'L0_gnn_gru_w_ih', 'L0_gnn_gru_w_hh',
        'L0_gnn_gru_b_ih', 'L0_gnn_gru_b_hh', 'L1_gnn_W1', 'L1_gnn_b1', 'L1_gnn_W2', 'L1_gnn_b2', 'L1_gnn_c1_Wl',
        'L1_gnn_c1_bl', 'L1_gnn_c1_Wr', 'L1_gnn_c2_Wl', 'L1_gnn_c2_bl', 'L1_gnn_c2_Wr', 'L2_gnn_weight',
        'L2_gnn_self_loop_weight', 'L2_gnn_bias', 'L3_gnn_W', 'L3_gnn_att', 'L3_gnn_bias']


def kernel(**inputs):
    import numpy as _np
    import concourse.bacc as _bacc
    from concourse import mybir as _mybir
    from concourse.bass_utils import run_bass_kernel_spmd as _run

    nc = _bacc.Bacc("TRN2", target_bir_lowering=False, num_devices=1)
    arrays, args = {}, []
    for name in _INS:
        a = _np.ascontiguousarray(inputs[name])
        arrays[f"in_{name}_dram"] = a
        args.append(nc.dram_tensor(f"in_{name}_dram", a.shape, _mybir.dt.from_np(a.dtype), kind="ExternalInput").ap())
    args.append(nc.dram_tensor("out_0_dram", (NODES, FEAT), F32, kind="ExternalOutput").ap())
    build(nc, *args)
    r = _run(nc, [arrays], core_ids=[0])
    return r.results[0]["out_0_dram"]
```

```python
import concourse.bass as bass
from concourse import mybir
from concourse.alu_op_type import AluOpType as ALU
from contextlib import ExitStack

F32 = mybir.dt.float32
BF16 = mybir.dt.bfloat16
I32 = mybir.dt.int32
ACT = mybir.ActivationFunctionType
AX = mybir.AxisListType
ds = bass.ds

P = 128
NODES, EDGES, FEAT, TYPES = 3125, 53125, 128, 8
HEADS, HEAD_F = 4, 32
TILES = -(-NODES // P)
PADN = TILES * P
FULL = NODES // P
LASTN = NODES - FULL * P
HALVES = 2
UNIT = HALVES * P
ROWS = -(-EDGES // UNIT)
PADE = ROWS * UNIT
PER = PADE // P
LASTP = EDGES - (P - 1) * PER
UNITS = ROWS + TILES - 1
UJ = 2
UQ = UNITS // UJ
P_BITS, UNIT_BITS, TYPE_BITS = P.bit_length() - 1, UNIT.bit_length() - 1, TYPES.bit_length() - 1
SLOTS = 8
TURNS = UNITS // SLOTS
GROUP = 5
GROUPS = TILES // GROUP
GW = GROUP * P
AW = 132
TROW = FEAT + HEADS + 6
FAR = 2.0 ** 100
EPS = 1e-5
LAG_TURN, LAG_MASK, LAG_MAX, LAG_SPREAD, LAG_LOGIT, LAG_EXP, LAG_WEIGHT, LAG_SUM, LAG_ADD = 0, 1, 2, 3, 3, 4, 4, 5, 6
LAG_LAST = 6
LEAD = 3
assert UQ * UJ == UNITS and TURNS * SLOTS == UNITS and GROUPS * GROUP == TILES and 0 < LASTP <= PER


class Unit:

    def __init__(self, turn, at):
        self.n = turn * SLOTS + at
        self.slot = at % SLOTS
        self.round = turn + at // SLOTS

    def count(self, more=0, k=0):
        return self.n + (1 + more + k * UNITS)

    def within(self):
        return not isinstance(self.n, int) or 0 <= self.n < UNITS

    def after(self, n):
        return not isinstance(self.n, int) or self.n >= n


def over_units(eng, step, lag):
    for b in range(SLOTS):
        step(lambda delay: Unit(0, b - delay))
    with eng.Fori(1, TURNS) as turn:
        for b in range(SLOTS):
            step(lambda delay: Unit(turn, b - delay))
    for b in range(lag):
        step(lambda delay: Unit(TURNS, b - delay))


def build(nc, x, src, dst, etype, L0W, L0b, w_ih, w_hh, b_ih, b_hh, W1, b1, W2, b2, c1l, c1b, c1r,
          c2l, c2b, c2r, L2W, L2S, L2b, L3W, L3a, L3b, out):
    with ExitStack() as ctx:
        def sb(name, shape, dt=F32):
            return ctx.enter_context(nc.sbuf_tensor(name, shape, dt))

        def sem(name):
            return ctx.enter_context(nc.semaphore(name))

        typed_table = nc.dram_tensor("typed_table", (PADN * TYPES, FEAT), F32, kind="Internal").ap()
        node_table = nc.dram_tensor("node_table", (PADN, FEAT), F32, kind="Internal").ap()
        gat_table = nc.dram_tensor("gat_table", (PADN, TROW), F32, kind="Internal").ap()
        list_code = nc.dram_tensor("list_code", (PADE, 1), I32, kind="Internal").ap()
        list_dst = nc.dram_tensor("list_dst", (PADE, 1), I32, kind="Internal").ap()
        unit_tiles = nc.dram_tensor("unit_tiles", (UNITS, 1), I32, kind="Internal").ap()

        PS = ctx.enter_context(nc.psum_tensor("PS", [P, 8 * 512], F32))

        xn = sb("xn", [P, PADN])
        xT = sb("xT", [P, PADN])
        hT = sb("hT", [P, PADN])
        rows = sb("rows", [P, TILES * TROW])
        acc = sb("acc", [P, (TILES + 1) * AW])
        work = sb("work", [P, GROUP * TYPES * FEAT])
        typed_out = work[:, :].rearrange("p (j n) -> p j n", j=GROUP)
        mT, cT, mn, gr, gz, gn, u1, u2 = (work[:, q * GW:(q + 1) * GW] for q in range(8))
        L0W_sb = sb("L0W_sb", [P, TYPES, FEAT])
        L2W_sb = sb("L2W_sb", [P, TYPES, FEAT])
        L0b_parts = sb("L0b_parts", [96, TYPES * FEAT], BF16)
        L0b_raw = rows[0:96, 0:2 * TYPES * FEAT].rearrange("p (a n) -> p a n", a=2)
        L3b_bc = sb("L3b_bc", [P, FEAT])
        wraw = sb("wraw", [P, 13, FEAT])
        wT = sb("wT", [P, 12, FEAT])
        w3a = sb("w3a", [P, FEAT + 2 * HEADS])
        att = sb("att", [P, 2 * HEADS])
        selfw = sb("selfw", [P, FEAT])
        bcol = sb("bcol", [P, 12])
        identf = sb("identf", [P, P])
        identb = sb("identb", [P, P], BF16)
        ident4 = sb("ident4", [P, HEADS, P], BF16)
        headsel = sb("headsel", [12, HEADS, P], BF16)
        onesf = sb("onesf", [P, P])
        onesb = sb("onesb", [96, P], BF16)
        below = sb("below", [P, P])
        lane_i = sb("lane_i", [P, P], I32)
        lane = sb("lane", [P, P])
        laneb = sb("laneb", [P, P], BF16)
        epst = sb("epst", [P, 1])
        rdeg = sb("rdeg", [P, TILES])

        e_dst = sb("e_dst", [P, PER], I32)
        e_next = sb("e_next", [P, PER], I32)
        e_code = sb("e_code", [P, PER], I32)
        e_type = sb("e_type", [P, PER], I32)
        e_bkt = sb("e_bkt", [P, PER], I32)
        e_f = sb("e_f", [P, PER])
        e_g = sb("e_g", [P, PER])
        e_pos = sb("e_pos", [P, PER])
        e_cum = sb("e_cum", [P, PER])
        e_zero = sb("e_zero", [P, PER])
        rowtot = sb("rowtot", [P, TILES + 1])
        bk = sb("bk", [P, 12, TILES + 1])
        bki = sb("bki", [P, 4, TILES + 1], I32)
        bad = sb("bad", [P, 2])
        flag = sb("flag", [P, 1], I32)
        base = sb("base", [P, TILES + 1])
        scat = sb("scat", [P, 3], I32)
        pr = sb("pr", [UQ, 6, UJ])
        prc = sb("prc", [UQ, UJ, TILES])
        prd = sb("prd", [UQ, UJ, TILES])
        unit_no = sb("unit_no", [UQ, UJ], I32)
        unit_row = sb("unit_row", [UQ, UJ], I32)
        unit_tile = sb("unit_tile", [UQ, UJ], I32)
        got_i = sb("got_i", [UQ, 2 * UJ, UNIT], I32)
        got_f = sb("got_f", [UQ, 2 * UJ, UNIT])
        chunk_code = sb("chunk_code", [P, HALVES, UNITS], I32)
        chunk_src = sb("chunk_src", [P, HALVES, UNITS], I32)
        chunk_dst = sb("chunk_dst", [P, HALVES, UNITS])
        tile_at = sb("tile_at", [1, UNITS], I32)

        ix = sb("ix", [P, SLOTS, HALVES], I32)
        g = sb("g", [P, SLOTS, HALVES, TROW])
        oh = sb("oh", [P, SLOTS, HALVES, P])
        ohm = sb("ohm", [P, SLOTS, HALVES, P], BF16)
        ohT = sb("ohT", [P, SLOTS, HALVES, P])
        aT = sb("aT", [12, SLOTS, HALVES, P], BF16)
        cm = sb("cm", [P, SLOTS, 12])
        lg = sb("lg", [P, SLOTS, 3, HALVES, HEADS])
        bm = sb("bm", [P, SLOTS, 8])
        state = sb("state", [P, TILES + 1, 8])
        wd = sb("wd", [P, SLOTS, HALVES, HEADS])
        dm = sb("dm", [P, SLOTS, HEADS])
        rescale = sb("rescale", [P, SLOTS, HEADS])
        wm = sb("wm", [P, SLOTS, HALVES, HEADS, HEAD_F + 1])

        stats = sb("stats", [P, GROUP, 6])
        mv = sb("mv", [P, GROUP, 2])
        sd = sb("sd", [P, GROUP])
        rs = sb("rs", [P, GROUP])
        den = sb("den", [P, TILES, HEADS])
        spl = sb("spl", [P, 2, TILES, HEADS])

        loaded_x, loaded_w, loaded_e = sem("loaded_x"), sem("loaded_w"), sem("loaded_e")
        pool_seq, const_ready = sem("pool_seq"), sem("const_ready")
        dve_seq, dve_pace = sem("dve_seq"), sem("dve_pace")
        code_ready, order_known = sem("code_ready"), sem("order_known")
        bucket_sums, bucket_base, bad_sum = sem("bucket_sums"), sem("bucket_base"), sem("bad_sum")
        rowtot_ready, bad_ready = sem("rowtot_ready"), sem("bad_ready")
        place_ready, scattered, list_ready = sem("place_ready"), sem("scattered"), sem("list_ready")
        units_ready, unit_dma = sem("units_ready"), sem("unit_dma")
        rows_got, rows_float, rows_turned, chunks_ready = sem("rows_got"), sem("rows_float"), sem("rows_turned"), sem("chunks_ready")
        weights_turned, weights_ready, att_zeroed = sem("weights_turned"), sem("weights_ready"), sem("att_zeroed")
        tiles_loaded, sort_seq, bias_split, oh_float = sem("tiles_loaded"), sem("sort_seq"), sem("bias_split"), sem("oh_float")
        x_padded, x_turned, xT_ready = sem("x_padded"), sem("x_turned"), sem("xT_ready")
        pace = sem("pace")
        typed_done = [sem(f"typed_done{k}") for k in range(2)]
        typed_evac = [sem(f"typed_evac{k}") for k in range(2)]
        typed_written = [[sem(f"typed_written{k}_{j}") for j in range(GROUP)] for k in range(2)]
        table_written = {k: sem(f"table_written{k}") for k in (1, 2, 4,)}
        arrived = [sem(f"arrived{b}") for b in range(SLOTS)]
        ix_ready = sem("ix_ready")
        oh_ready = sem("oh_ready")
        product = sem("product")
        acc_done = sem("acc_done")
        acc_zero = sem("acc_zero")
        agg_turned = {k: sem(f"agg_turned{k}") for k in (0, 1, 2,)}
        agg_T = {k: sem(f"agg_T{k}") for k in (0, 1, 2,)}
        mean_ready = [sem(f"mean_ready{k}") for k in range(4)]
        linear_done = {k: sem(f"linear_done{k}") for k in (0, 1, 2, 3,)}
        hidden_T = {k: sem(f"hidden_T{k}") for k in (0, 1, 2, 3,)}
        linear2_done = {k: sem(f"linear2_done{k}") for k in (1,)}
        hidden2_T = {k: sem(f"hidden2_T{k}") for k in (1,)}
        rows_turned_back = {k: sem(f"rows_turned_back{k}") for k in (0, 1, 3,)}
        rows_ready = [sem(f"rows_ready{k}") for k in range(4)]
        gates_done, gates_rz, n_pre, n_ready = sem("gates_done"), sem("gates_rz"), sem("n_pre"), sem("n_ready")
        y_T = {k: sem(f"y_T{k}") for k in (0, 2, 3,)}
        y_turned = {k: sem(f"y_turned{k}") for k in (0, 2, 3,)}
        var_ready = [sem(f"var_ready{k}") for k in range(5)]
        std_ready = [sem(f"std_ready{k}") for k in range(5)]
        x_ready = [sem(f"x_ready{k}") for k in range(5)]
        x_again = {k: sem(f"x_again{k}") for k in (0, 2, 3,)}
        x_T = {k: sem(f"x_T{k}") for k in (0, 2, 3,)}
        gat_rows, gat_state = sem("gat_rows"), sem("gat_state")
        turned, turned_sb, masked, seg_max = sem("turned"), sem("turned_sb"), sem("masked"), sem("seg_max")
        spread, logits, weights, weighted = sem("spread"), sem("logits"), sem("weights"), sem("weighted")
        out_rows, out_written = sem("out_rows"), sem("out_written")

        block = ctx.enter_context(nc.Block())

        IH, HH, W1i, W2i, C1L, C1R, C2L, C2R = 0, 3, 6, 7, 8, 9, 10, 11
        L3i = 12
        B_IH, B_HH, B1, B2, B_C1, B_C2, B_L2, B_R, B_Z = 0, 3, 6, 7, 8, 9, 10, 11, 0

        def region(r, width=GW):
            return PS[:, 1024 * r:1024 * r + width]

        def bank(b, n=512, p=P):
            return PS[0:p, 512 * b:512 * b + n]

        def acc_cols(tile, n):
            return acc[:, ds(tile * AW, n)]

        @block.sync
        def _(sp):
            sp.wait_ge(x_padded, 1)
            sp.dma_start(xn[:, 0:FULL * P].rearrange("p (t d) -> p t d", d=FEAT),
                         x[0:FULL * P, :].rearrange("(t p) d -> p t d", p=P)).then_inc(loaded_x, 16)
            sp.dma_start(xn[0:LASTN, FULL * P:PADN], x[FULL * P:NODES, :]).then_inc(loaded_x, 16)
            sp.wait_ge(x_padded, 2)
            for tile, arr in ((e_dst, dst), (e_code, src), (e_type, etype)):
                sp.dma_start(tile[0:P - 1, :], arr[0:(P - 1) * PER].rearrange("(p t) -> p t", t=PER)).then_inc(loaded_e, 16)
                sp.dma_start(tile[P - 1:P, 0:LASTP], arr[(P - 1) * PER:EDGES].rearrange("(a t) -> a t", a=1)).then_inc(loaded_e, 16)
            sp.dma_start(e_next[0:P - 1, :], dst[1:1 + (P - 1) * PER].rearrange("(p t) -> p t", t=PER)).then_inc(loaded_e, 16)
            sp.dma_start(e_next[P - 1:P, 0:LASTP - 1], dst[(P - 1) * PER + 1:EDGES].rearrange("(a t) -> a t", a=1)).then_inc(loaded_e, 16)

            def typed(k):
                with sp.Fori(0, GROUPS) as i:
                    for j in range(GROUP):
                        sp.wait_ge(typed_evac[k], i * (2 * GROUP) + 2 * j + 2)
                        sp.dma_start(typed_table[ds(i * (GW * TYPES) + j * P * TYPES, P * TYPES), :].rearrange("(p t) d -> p (t d)", t=TYPES),
                                     typed_out[:, j, :]).then_inc(typed_written[k][j], 16)

            def plain(k):
                with sp.Fori(0, GROUPS) as i:
                    sp.wait_ge(rows_ready[k], i + 1)
                    sp.dma_start(node_table[ds(i * GW, GW), :].rearrange("(j p) d -> p j d", p=P),
                                 rows[:, ds(i * GW, GW)].rearrange("p (j d) -> p j d", d=FEAT)).then_inc(table_written[k + 1], 16)

            typed(0)
            plain(0)
            plain(1)
            typed(1)
            sp.wait_ge(gat_rows, 1)
            sp.dma_start(gat_table.rearrange("(t p) d -> p t d", p=P),
                         rows[:, :].rearrange("p (t d) -> p t d", d=TROW)).then_inc(table_written[4], 16)
            with sp.Fori(0, GROUPS - 1) as i:
                sp.wait_ge(out_rows, i + 1)
                sp.dma_start(out[ds(i * GW, GW), :].rearrange("(j p) d -> p j d", p=P),
                             rows[:, ds(i * GW, GW)].rearrange("p (j d) -> p j d", d=FEAT)).then_inc(out_written, 16)
            sp.wait_ge(out_rows, GROUPS)
            sp.dma_start(out[(GROUPS - 1) * GW:FULL * P, :].rearrange("(j p) d -> p j d", p=P),
                         rows[:, (GROUPS - 1) * GW:FULL * P].rearrange("p (j d) -> p j d", d=FEAT)).then_inc(out_written, 16)
            sp.dma_start(out[FULL * P:NODES, :], rows[0:LASTN, FULL * P:PADN]).then_inc(out_written, 16)
            sp.wait_ge(out_written, 16 * (GROUPS + 1))

        @block.gpsimd
        def _(pool):
            steps = [0]

            def link(ins):
                steps[0] += 1
                ins.then_inc(pool_seq, 1)
                pool.wait_ge(pool_seq, steps[0])

            pool.memset(xn[:, FULL * P:PADN], 0.0).then_inc(x_padded, 1)
            pool.memset(e_dst[:, :], PADN)
            pool.memset(e_next[:, :], PADN)
            pool.memset(e_code[:, :], 0)
            pool.memset(e_type[:, :], 0).then_inc(x_padded, 1)
            link(pool.memset(identf[:, :], 0.0))
            link(pool.affine_select(out=identf[:, :], in_=identf[:, :], compare_op=ALU.not_equal, fill=1.0,
                                    base=0, pattern=[[-1, P]], channel_multiplier=1))
            link(pool.tensor_copy(identb[:, :], identf[:, :]))
            link(pool.memset(ident4[:, :, :], 0.0))
            link(pool.affine_select(out=ident4[:, :, :], in_=ident4[:, :, :], compare_op=ALU.not_equal, fill=FAR,
                                    base=0, pattern=[[0, HEADS], [-1, P]], channel_multiplier=1))
            link(pool.memset(onesf[:, :], 1.0))
            link(pool.affine_select(out=below[:, :], in_=onesf[:, :], compare_op=ALU.is_gt, fill=0.0,
                                    base=0, pattern=[[1, P]], channel_multiplier=-1))
            link(pool.memset(headsel[:, :, :], 1.0))
            link(pool.affine_select(out=headsel[:, :, :], in_=headsel[:, :, :], compare_op=ALU.is_ge, fill=0.0,
                                    base=0, pattern=[[-3, HEADS], [0, P]], channel_multiplier=1))
            link(pool.affine_select(out=headsel[:, :, :], in_=headsel[:, :, :], compare_op=ALU.is_ge, fill=0.0,
                                    base=2, pattern=[[3, HEADS], [0, P]], channel_multiplier=-1))
            link(pool.iota(lane_i[:, :], pattern=[[1, P]], base=0, channel_multiplier=0))
            link(pool.tensor_copy(lane[:, :], lane_i[:, :]))
            link(pool.tensor_copy(laneb[:, :], lane_i[:, :]))
            link(pool.iota(unit_no[:, :], pattern=[[UQ, UJ]], base=0, channel_multiplier=1))
            link(pool.memset(epst[:, :], EPS))
            link(pool.memset(onesb[:, :], 1.0))
            pool.memset(g[:, :, :, :], 1.0).then_inc(const_ready, 1)

            pool.wait_ge(code_ready, 1)
            pool.wait_ge(order_known, 1)
            disorder = pool.value_load(flag[0:1, 0:1], min_val=0, max_val=1)
            with pool.If(disorder > 0):
                pool.wait_ge(place_ready, 1)
                with pool.Fori(0, PER) as t:
                    pool.tensor_copy(scat[:, 0:1], e_pos[:, ds(t, 1)])
                    pool.tensor_copy(scat[:, 1:2], e_code[:, ds(t, 1)])
                    pool.tensor_copy(scat[:, 2:3], e_dst[:, ds(t, 1)]).then_inc(place_ready, 1)
                    pool.wait_ge(place_ready, t + 2)
                    pool.sem_inc(pace, 1)
                    pool.indirect_dma_start(list_code, bass.IndirectOffsetOnAxis(ap=scat[:, 0:1], axis=0),
                                            scat[:, 1:2], None).then_inc(scattered, 16)
                    pool.indirect_dma_start(list_dst, bass.IndirectOffsetOnAxis(ap=scat[:, 0:1], axis=0),
                                            scat[:, 2:3], None).then_inc(scattered, 16)
                    pool.wait_ge(scattered, t * 32 + 32)
                    pool.sem_inc(pace, 1)
            with pool.Else():
                pool.dma_start(list_code.rearrange("(p t) a -> p (t a)", t=PER), e_code[:, :]).then_inc(scattered, 16)
                pool.dma_start(list_dst.rearrange("(p t) a -> p (t a)", t=PER), e_dst[:, :]).then_inc(scattered, 16)
                pool.wait_ge(scattered, 32)
                pool.sem_inc(pace, 1)

            pool.wait_ge(units_ready, 1)
            code_rows = list_code.rearrange("(r e) a -> r (e a)", e=UNIT)
            dst_rows = list_dst.rearrange("(r e) a -> r (e a)", e=UNIT)
            for j in range(UJ):
                where = bass.IndirectOffsetOnAxis(ap=unit_row[:, j:j + 1], axis=0)
                pool.indirect_dma_start(got_i[:, j, :], None, code_rows, where).then_inc(rows_got, 16)
                pool.indirect_dma_start(got_i[:, UJ + j, :], None, dst_rows, where).then_inc(rows_got, 16)

            pool.dma_start(unit_tiles.rearrange("(j p) a -> p (j a)", p=UQ), unit_tile[:, :], allow_slow_non_contiguous=True).then_inc(unit_dma, 16)
            pool.wait_ge(unit_dma, 16)
            pool.dma_start(tile_at[:, :], unit_tiles.rearrange("n a -> a n")).then_inc(tiles_loaded, 16)

            def gathers(k, table, width, written, total):
                for s in written:
                    pool.wait_ge(s, total)

                def beat(u):
                    u = u(0)
                    pool.wait_ge(ix_ready, u.count(0, k))
                    pool.sem_inc(pace, 1)
                    for half in range(HALVES):
                        pool.indirect_dma_start(g[:, u.slot, half, 0:width], None, table,
                                                bass.IndirectOffsetOnAxis(ap=ix[:, u.slot, half:half + 1], axis=0))\
                            .then_inc(arrived[u.slot], 16)
                over_units(pool, beat, 0)

            gathers(0, typed_table, FEAT, typed_written[0], 16 * GROUPS)
            gathers(1, node_table, FEAT, [table_written[1]], 16 * GROUPS)
            gathers(2, node_table, FEAT, [table_written[2]], 16 * GROUPS)
            gathers(3, typed_table, FEAT, typed_written[1], 16 * GROUPS)
            gathers(4, gat_table, TROW, [table_written[4]], 16)

        @block.scalar
        def _(act):
            for n, w in ((W1i, W1), (W2i, W2), (C1L, c1l), (C1R, c1r), (C2L, c2l), (C2R, c2r), (L3i, L3W)):
                act.dma_start(wraw[:, n, :], w).then_inc(loaded_w, 16)
            for n, w in ((IH, w_ih), (HH, w_hh)):
                act.dma_start(wraw[:, n:n + 3, :], w.rearrange("(k p) d -> p k d", p=P)).then_inc(loaded_w, 16)
            act.dma_start(L0W_sb[:, :, :], L0W.rearrange("t h d -> h t d")).then_inc(loaded_w, 16)
            act.dma_start(L2W_sb[:, :, :], L2W.rearrange("t h d -> h t d")).then_inc(loaded_w, 16)
            act.dma_start(selfw[:, :], L2S).then_inc(loaded_w, 16)
            act.dma_start(L0b_raw[:, 0, :], L0b.rearrange("t d -> (t d)").partition_broadcast(96)).then_inc(loaded_w, 16)
            act.dma_start(L3b_bc[:, :], L3b.partition_broadcast(P)).then_inc(loaded_w, 16)
            for n, b in ((B_IH, b_ih), (B_HH, b_hh)):
                act.dma_start(bcol[:, n:n + 3], b.rearrange("(k p) -> p k", p=P), allow_slow_non_contiguous=True).then_inc(loaded_w, 16)
            for n, b in ((B1, b1), (B2, b2), (B_C1, c1b), (B_C2, c2b), (B_L2, L2b)):
                act.dma_start(bcol[:, n:n + 1], b.rearrange("(p a) -> p a", a=1), allow_slow_non_contiguous=True).then_inc(loaded_w, 16)
            act.wait_ge(att_zeroed, 1)
            for h in range(HEADS):
                for side in range(2):
                    act.dma_start(att[h * HEAD_F:(h + 1) * HEAD_F, side * HEADS + h:side * HEADS + h + 1],
                                  L3a[h, side * HEAD_F:(side + 1) * HEAD_F].rearrange("(p a) -> p a", a=1), allow_slow_non_contiguous=True).then_inc(loaded_w, 16)
            act.wait_ge(weights_turned, 1)
            act.activation(wT[:, :, :].rearrange("p k d -> p (k d)"), PS[:, 0:12 * FEAT], ACT.Copy).then_inc(weights_ready, 1)
            act.activation(w3a[:, :], bank(4, FEAT + 2 * HEADS), ACT.Copy).then_inc(weights_ready, 1)
            with act.Fori(0, GROUPS) as i:
                act.wait_ge(x_turned, i + 1)
                act.activation(xT[:, ds(i * GW, GW)], region(1), ACT.Copy).then_inc(xT_ready, 1)
            def typed(k):
                def unit(i, j, half, first):
                    u = 2 * j + half
                    act.wait_ge(typed_done[k], i * (2 * GROUP) + u + 1)
                    if not first and half == 0:
                        act.wait_ge(typed_written[k][j], i * 16)
                    act.activation(typed_out[:, j, 512 * half:512 * half + 512], bank(u % 5), ACT.Copy).then_inc(typed_evac[k], 1)
                for j in range(GROUP):
                    for half in range(2):
                        unit(0, j, half, True)
                with act.Fori(1, GROUPS) as i:
                    for j in range(GROUP):
                        for half in range(2):
                            unit(i, j, half, False)

            typed(0)
            act.wait_ge(rows_turned, 1)
            act.activation(chunk_code[:, :, :].rearrange("p a u -> p (a u)"), bank(0, HALVES * UNITS), ACT.Copy).then_inc(chunks_ready, 1)
            act.activation(chunk_dst[:, :, :].rearrange("p a u -> p (a u)"), bank(1, HALVES * UNITS), ACT.Copy).then_inc(chunks_ready, 1)

            def columns(k, cols):
                def beat(u):
                    u = u(0)
                    if u.after(SLOTS):
                        act.wait_ge(product, u.count(-SLOTS, k))
                    act.activation(ix[:, u.slot, :], cols[:, :, ds(u.n, 1)].rearrange("p a b -> p (a b)"), ACT.Copy).then_inc(ix_ready, 1)
                over_units(act, beat, 0)

            def norm(k, i):
                act.wait_ge(var_ready[k], i + 1)
                act.activation(sd[:, :], mv[:, :, 1], ACT.Sqrt, bias=epst[:, 0:1]).then_inc(std_ready[k], 1)

            act.wait_ge(chunks_ready, 3)
            columns(0, chunk_code)

            with act.Fori(0, GROUPS) as i:
                act.wait_ge(agg_turned[0], i + 1)
                act.activation(mT[:, :], region(0), ACT.Copy).then_inc(agg_T[0], 1)
                act.wait_ge(gates_done, i * 4 + 1)
                act.activation(gr[:, :], region(1), ACT.Sigmoid, bias=bcol[:, B_R:B_R + 1]).then_inc(gates_rz, 1)
                act.wait_ge(gates_done, i * 4 + 2)
                act.activation(gz[:, :], region(2), ACT.Sigmoid, bias=bcol[:, B_Z:B_Z + 1]).then_inc(gates_rz, 1)
                act.wait_ge(n_pre, i + 1)
                act.activation(gn[:, :], u2[:, :], ACT.Tanh, bias=bcol[:, B_IH + 2:B_IH + 3]).then_inc(n_ready, 1)
                norm(0, i)
                act.wait_ge(x_again[0], i + 1)
                act.activation(xT[:, ds(i * GW, GW)], region(2), ACT.Copy).then_inc(x_T[0], 1)
                act.wait_ge(linear_done[0], i + 1)
                act.activation(hT[:, ds(i * GW, GW)], region(3), ACT.Relu, bias=bcol[:, B1:B1 + 1]).then_inc(hidden_T[0], 1)
            columns(1, chunk_src)

            with act.Fori(0, GROUPS) as i:
                act.wait_ge(agg_turned[1], i + 1)
                act.activation(mT[:, :], region(0), ACT.Copy).then_inc(agg_T[1], 1)
                act.wait_ge(linear_done[1], i + 1)
                act.activation(cT[:, :], region(1), ACT.Relu, bias=bcol[:, B_C1:B_C1 + 1]).then_inc(hidden_T[1], 1)
                act.wait_ge(linear2_done[1], i + 1)
                act.activation(hT[:, ds(i * GW, GW)], region(2), ACT.Relu, bias=bcol[:, B2:B2 + 1]).then_inc(hidden2_T[1], 1)
            columns(2, chunk_src)

            with act.Fori(0, GROUPS) as i:
                act.wait_ge(agg_turned[2], i + 1)
                act.activation(mT[:, :], region(0), ACT.Copy).then_inc(agg_T[2], 1)
                act.wait_ge(linear_done[2], i + 1)
                act.activation(cT[:, :], region(1), ACT.Relu, bias=bcol[:, B_C2:B_C2 + 1]).then_inc(hidden_T[2], 1)
                norm(2, i)
                act.wait_ge(x_again[2], i + 1)
                act.activation(xT[:, ds(i * GW, GW)], region(3), ACT.Copy).then_inc(x_T[2], 1)
            typed(1)
            columns(3, chunk_code)

            with act.Fori(0, GROUPS) as i:
                act.wait_ge(linear_done[3], i + 1)
                act.activation(cT[:, :], region(0), ACT.Relu, bias=bcol[:, B_L2:B_L2 + 1]).then_inc(hidden_T[3], 1)
                norm(3, i)
                act.wait_ge(x_again[3], i + 1)
                act.activation(xT[:, ds(i * GW, GW)], region(2), ACT.Copy).then_inc(x_T[3], 1)

            def beat(at):
                w = at(LEAD + LAG_EXP)
                if w.within():
                    act.wait_ge(logits, w.count())
                    act.activation(rescale[:, w.slot, :], dm[:, w.slot, :], ACT.Exp)
                    act.activation(wm[:, w.slot, :, :, HEAD_F], wd[:, w.slot, :, :], ACT.Exp).then_inc(weights, 1)
                u = at(0)
                if u.within():
                    if u.after(SLOTS):
                        act.wait_ge(weighted, u.count(-SLOTS))
                    act.activation(ix[:, u.slot, :], chunk_src[:, :, ds(u.n, 1)].rearrange("p a b -> p (a b)"), ACT.Copy).then_inc(ix_ready, 1)
                o = at(LEAD)
                if o.within():
                    act.wait_ge(oh_ready, o.count(0, 4))
                    act.activation(oh[:, o.slot, :, :], ohm[:, o.slot, :, :], ACT.Copy, bias=1.0).then_inc(oh_float, 1)
                t = at(LEAD + LAG_TURN)
                if t.within():
                    act.wait_ge(turned, t.count())
                    act.activation(ohT[:, t.slot, :, :].rearrange("p a e -> p (a e)"), bank(0, UNIT), ACT.Identity, bias=onesf[:, 0:1])
                    act.activation(aT[:, t.slot, :, :].rearrange("p a e -> p (a e)"), PS[0:12, UNIT:2 * UNIT], ACT.Copy).then_inc(turned_sb, 1)
            over_units(act, beat, LEAD + LAG_LAST)

            with act.Fori(0, GROUPS) as i:
                norm(4, i)

        @block.tensor
        def _(pe):
            def turn_group(r, source, i):
                for j in range(GROUP):
                    last = pe.transpose(PS[:, 1024 * r + j * P:1024 * r + (j + 1) * P],
                                        source(i, j), identf[:, :])
                return last

            def linear(r, parts):
                for c0, n in ((0, 512), (512, GW - 512)):
                    for q, (w, feats) in enumerate(parts):
                        last = pe.matmul(PS[:, 1024 * r + c0:1024 * r + c0 + n], w, feats(c0, n),
                                         start=(q == 0), stop=(q == len(parts) - 1))
                return last

            def whole(tile):
                return lambda c0, n: tile[:, c0:c0 + n]

            def of(tile, i):
                return lambda c0, n: tile[:, ds(i * GW + c0, n)]

            def node_tile(i, j):
                return xn[:, ds(i * GW + j * P, P)]

            pe.wait_ge(const_ready, 1)
            pe.wait_ge(loaded_w, 16 * 29)
            for n in range(12):
                pe.transpose(PS[:, n * P:(n + 1) * P], wraw[:, n, :], identf[:, :])
            pe.transpose(PS[:, 2048:2048 + P], wraw[:, L3i, :], identf[:, :])
            pe.matmul(PS[:, 2048 + P:2048 + P + 2 * HEADS], wraw[:, L3i, :], att[:, :], start=True, stop=True).then_inc(weights_turned, 1)
            pe.wait_ge(weights_ready, 2)
            pe.wait_ge(loaded_x, 32)
            for i in range(GROUPS):
                turn_group(1, node_tile, i).then_inc(x_turned, 1)
                pe.wait_ge(xT_ready, i + 1)

            def buckets():
                pe.wait_ge(rowtot_ready, 1)
                pe.matmul(bank(6, TILES + 1), onesf[:, :], rowtot[:, :], start=True, stop=True).then_inc(bucket_sums, 1)
                pe.matmul(bank(7, TILES + 1), below[:, :], rowtot[:, :], start=True, stop=True).then_inc(bucket_base, 1)
                pe.wait_ge(bad_ready, 1)
                pe.matmul(bank(5, 1), onesf[:, :], bad[:, 0:1], start=True, stop=True).then_inc(bad_sum, 1)

            def typed(k, w):
                def unit(i, j, half, first):
                    u = 2 * j + half
                    if not (first and u < 5):
                        pe.wait_ge(typed_evac[k], i * (2 * GROUP) + u - 4)
                    last = pe.matmul(bank(u % 5), xT[:, ds(i * GW + j * P, P)],
                                     w[:, 4 * half:4 * half + 4, :].rearrange("p t d -> p (t d)"), start=True, stop=(k == 1))
                    if k == 0:
                        last = pe.matmul(bank(u % 5), onesb[:, :], L0b_parts[:, 512 * half:512 * half + 512], start=False, stop=True)
                    last.then_inc(typed_done[k], 1)
                for i in range(GROUPS):
                    for j in range(GROUP):
                        for half in range(2):
                            unit(i, j, half, i == 0)
                    if k == 0 and i == 2:
                        buckets()

            pe.wait_ge(xT_ready, GROUPS)
            pe.wait_ge(bias_split, 1)
            typed(0, L0W_sb)
            pe.wait_ge(typed_evac[0], 10 * GROUPS)
            pe.wait_ge(rows_float, 1)
            for q in range(2):
                for half in range(HALVES):
                    for j in range(UJ):
                        at = 512 * q + half * UNITS + j * UQ
                        last = pe.transpose(PS[:, at:at + UQ], got_f[:, q * UJ + j, half * P:(half + 1) * P], identf[0:UQ, 0:UQ])
            last.then_inc(rows_turned, 1)
            pe.wait_ge(chunks_ready, 2)

            def sums(k, width):
                def beat(u):
                    u = u(0)
                    pe.wait_ge(oh_ready, u.count(0, k))
                    if u.after(4):
                        pe.wait_ge(acc_done, u.count(-4, k))
                    pe.wait_ge(arrived[u.slot], (u.round + (1 + k * TURNS)) * (16 * HALVES))
                    for half in range(HALVES):
                        last = pe.matmul(bank(u.slot % 4, width), oh[:, u.slot, half, :], g[:, u.slot, half, 0:width],
                                         start=(half == 0), stop=(half == HALVES - 1))
                    last.then_inc(product, 1)
                over_units(pe, beat, 0)

            sums(0, FEAT + 1)

            pe.wait_ge(acc_done, 1 * UNITS)
            for i in range(GROUPS):
                turn_group(0, lambda i, j: acc[:, ds(i * (GROUP * AW) + j * AW, P)], i).then_inc(agg_turned[0], 1)
                pe.wait_ge(agg_T[0], i + 1)
                linear(1, [(wT[:, IH, :], whole(mT)), (wT[:, HH, :], of(xT, i))]).then_inc(gates_done, 1)
                linear(2, [(wT[:, IH + 1, :], whole(mT)), (wT[:, HH + 1, :], of(xT, i))]).then_inc(gates_done, 1)
                linear(3, [(wT[:, HH + 2, :], of(xT, i))]).then_inc(gates_done, 1)
                linear(0, [(wT[:, IH + 2, :], whole(mT))]).then_inc(gates_done, 1)
                pe.wait_ge(y_T[0], i + 1)
                turn_group(1, lambda i, j: u1[:, j * P:(j + 1) * P], i).then_inc(y_turned[0], 1)
                pe.wait_ge(x_ready[0], i + 1)
                turn_group(2, node_tile, i).then_inc(x_again[0], 1)
                pe.wait_ge(x_T[0], i + 1)
                linear(3, [(wT[:, W1i, :], of(xT, i))]).then_inc(linear_done[0], 1)
                pe.wait_ge(hidden_T[0], i + 1)
                turn_group(0, lambda i, j: hT[:, ds(i * GW + j * P, P)], i).then_inc(rows_turned_back[0], 1)
                pe.wait_ge(rows_ready[0], i + 1)
            sums(1, FEAT)

            pe.wait_ge(acc_done, 2 * UNITS)
            for i in range(GROUPS):
                pe.wait_ge(mean_ready[1], i + 1)
                turn_group(0, lambda i, j: mn[:, j * P:(j + 1) * P], i).then_inc(agg_turned[1], 1)
                pe.wait_ge(agg_T[1], i + 1)
                linear(1, [(wT[:, C1L, :], whole(mT)), (wT[:, C1R, :], of(hT, i))]).then_inc(linear_done[1], 1)
                pe.wait_ge(hidden_T[1], i + 1)
                linear(2, [(wT[:, W2i, :], whole(cT))]).then_inc(linear2_done[1], 1)
                pe.wait_ge(hidden2_T[1], i + 1)
                turn_group(3, lambda i, j: hT[:, ds(i * GW + j * P, P)], i).then_inc(rows_turned_back[1], 1)
                pe.wait_ge(rows_ready[1], i + 1)
            sums(2, FEAT)

            pe.wait_ge(acc_done, 3 * UNITS)
            for i in range(GROUPS):
                pe.wait_ge(mean_ready[2], i + 1)
                turn_group(0, lambda i, j: mn[:, j * P:(j + 1) * P], i).then_inc(agg_turned[2], 1)
                pe.wait_ge(agg_T[2], i + 1)
                linear(1, [(wT[:, C2L, :], whole(mT)), (wT[:, C2R, :], of(hT, i))]).then_inc(linear_done[2], 1)
                pe.wait_ge(y_T[2], i + 1)
                turn_group(2, lambda i, j: u1[:, j * P:(j + 1) * P], i).then_inc(y_turned[2], 1)
                pe.wait_ge(x_ready[2], i + 1)
                turn_group(3, node_tile, i).then_inc(x_again[2], 1)
                pe.wait_ge(x_T[2], i + 1)
            typed(1, L2W_sb)
            pe.wait_ge(typed_evac[1], 10 * GROUPS)
            sums(3, FEAT)

            pe.wait_ge(acc_done, 4 * UNITS)
            for i in range(GROUPS):
                for j in range(GROUP):
                    pe.matmul(PS[:, j * P:(j + 1) * P], selfw[:, :], xT[:, ds(i * GW + j * P, P)], start=True, stop=False)
                    last = pe.matmul(PS[:, j * P:(j + 1) * P], acc[:, ds(i * (GROUP * AW) + j * AW, P)], identf[:, :],
                                     start=False, stop=True)
                last.then_inc(linear_done[3], 1)
                pe.wait_ge(y_T[3], i + 1)
                turn_group(1, lambda i, j: u1[:, j * P:(j + 1) * P], i).then_inc(y_turned[3], 1)
                pe.wait_ge(x_ready[3], i + 1)
                turn_group(2, node_tile, i).then_inc(x_again[3], 1)
                pe.wait_ge(x_T[3], i + 1)
                WA = FEAT + 2 * HEADS
                for j in range(GROUP):
                    at = 3072 + (j * WA if j < 3 else 512 + (j - 3) * WA)
                    last = pe.matmul(PS[:, at:at + WA], xT[:, ds(i * GW + j * P, P)], w3a[:, :], start=True, stop=True)
                last.then_inc(rows_turned_back[3], 1)
                pe.wait_ge(rows_ready[3], i + 1)

            def beat(at):
                f = at(LAG_SPREAD)
                if f.within():
                    pe.wait_ge(seg_max, f.count())
                    if f.after(1):
                        pe.wait_ge(logits, f.count(-1))
                    for half in range(HALVES):
                        last = pe.matmul(PS[:, 2560 + 8 * half:2568 + 8 * half], ohT[:, f.slot, half, :], bm[:, f.slot, :], start=True, stop=True)
                    last.then_inc(spread, 1)
                s = at(LAG_SUM)
                if s.within():
                    pe.wait_ge(oh_float, s.count())
                    pe.wait_ge(weighted, s.count())
                    if s.after(2):
                        pe.wait_ge(acc_done, s.count(-2, 4))
                    for half in range(HALVES):
                        last = pe.matmul(bank(6 + s.slot % 2, AW), oh[:, s.slot, half, :], wm[:, s.slot, half, :, :].rearrange("p h f -> p (h f)"),
                                         start=(half == 0), stop=(half == HALVES - 1))
                    last.then_inc(product, 1)
                m = at(LAG_MASK)
                if m.within():
                    pe.wait_ge(turned_sb, m.count())
                    if m.after(2):
                        pe.wait_ge(seg_max, m.count(-2))
                    for half in range(HALVES):
                        b = 1 + 2 * (m.slot % 2) + half
                        pe.matmul(bank(b), ohm[:, m.slot, half, :], ident4[:, :, :].rearrange("p h e -> p (h e)"), start=True, stop=True)
                        for h in range(HEADS):
                            last = pe.matmul(PS[:, 512 * b + h * P:512 * b + (h + 1) * P], headsel[:, h, :], aT[:, m.slot, half, :],
                                             start=False, stop=True, skip_group_check=True)
                    last.then_inc(masked, 1)
                t = at(LAG_TURN)
                if t.within():
                    pe.wait_ge(oh_ready, t.count(0, 4))
                    if t.after(1):
                        pe.wait_ge(turned_sb, t.count(-1))
                    pe.wait_ge(arrived[t.slot], (t.round + (1 + 4 * TURNS)) * (16 * HALVES))
                    for half in range(HALVES):
                        pe.matmul(PS[:, half * P:(half + 1) * P], ohm[:, t.slot, half, :], identb[:, :], start=True, stop=True)
                    for half in range(HALVES):
                        last = pe.matmul(PS[0:12, UNIT + half * P:UNIT + (half + 1) * P],
                                         g[:, t.slot, half, FEAT + HEADS:TROW].bitcast(BF16), identb[:, :], start=True, stop=True)
                    last.then_inc(turned, 1)
            over_units(pe, beat, LAG_LAST)

        @block.vector
        def _(dve):
            steps = [0]

            def link(ins):
                steps[0] += 1
                ins.then_inc(dve_seq, 1)
                dve.wait_ge(dve_seq, steps[0])

            dve.memset(att[:, :], 0.0).then_inc(att_zeroed, 1)
            link(dve.memset(L0b_parts[:, :], 0.0))
            dve.wait_ge(const_ready, 1)
            dve.wait_ge(loaded_w, 16 * 29)
            for p0 in (0, 32, 64):
                here = slice(p0, p0 + 1)
                raw, rest = L0b_raw[here, 0, :], L0b_raw[here, 1, :]
                for _ in range(p0 // 32):
                    link(dve.tensor_copy(L0b_parts[here, :], raw))
                    link(dve.tensor_tensor(rest, raw, L0b_parts[here, :], ALU.subtract))
                    raw, rest = rest, raw
                ins = dve.tensor_copy(L0b_parts[here, :], raw)
                if p0 < 64:
                    link(ins)
            ins.then_inc(bias_split, 1)
            dve.wait_ge(loaded_e, 16 * 8)
            dve.scalar_tensor_tensor(out=e_code[:, :], in0=e_code[:, :], scalar=float(TYPES), in1=e_type[:, :],
                                     op0=ALU.mult, op1=ALU.add).then_inc(code_ready, 1)
            link(dve.tensor_single_scalar(e_bkt[:, :], e_dst[:, :], P_BITS, ALU.arith_shift_right))
            link(dve.tensor_single_scalar(e_next[:, :], e_next[:, :], P_BITS, ALU.arith_shift_right))
            link(dve.tensor_tensor(e_f[:, :], e_bkt[:, :], e_next[:, :], ALU.is_gt))
            dve.tensor_reduce(bad[:, 0:1], e_f[:, :], AX.X, ALU.max).then_inc(bad_ready, 1)
            link(dve.tensor_copy(e_g[:, :], e_bkt[:, :]))
            for b in range(TILES + 1):
                link(dve.tensor_scalar(e_f[:, :], e_g[:, :], float(b), None, ALU.is_equal))
                ins = dve.tensor_reduce(rowtot[:, b:b + 1], e_f[:, :], AX.X, ALU.add)
                if b < TILES:
                    link(ins)
            ins.then_inc(rowtot_ready, 1)
            dve.wait_ge(bad_sum, 1)
            dve.tensor_scalar(flag[:, :], bank(5, 1), 1.0, None, ALU.min).then_inc(order_known, 1)
            CNT, END, START, FIRST, LAST, NUM, PEND, PSTART, SHIFT, HAS, ZERO = range(11)
            dve.wait_ge(bucket_base, 1)
            link(dve.tensor_copy(bk[:, CNT, :], bank(6, TILES + 1)))
            link(dve.memset(bk[:, ZERO, :], 0.0))
            link(dve.tensor_tensor_scan(bk[:, END, :], bk[:, CNT, :], bk[:, ZERO, :], 0.0, ALU.add, ALU.add))
            link(dve.tensor_tensor(bk[:, START, :], bk[:, END, :], bk[:, CNT, :], ALU.subtract))
            link(dve.tensor_tensor(base[:, :], bank(7, TILES + 1), bk[:, START, :], ALU.add))
            link(dve.tensor_scalar(base[:, :], base[:, :], -1.0, None, ALU.add))
            link(dve.tensor_copy(bki[:, 0, :], bk[:, START, :]))
            link(dve.tensor_scalar(bki[:, 1, :], bk[:, END, :], -1.0, 0.0, ALU.add, ALU.max))
            link(dve.tensor_single_scalar(bki[:, 2, :], bki[:, 0, :], UNIT_BITS, ALU.arith_shift_right))
            link(dve.tensor_single_scalar(bki[:, 3, :], bki[:, 1, :], UNIT_BITS, ALU.arith_shift_right))
            link(dve.tensor_copy(bk[:, FIRST, :], bki[:, 2, :]))
            link(dve.tensor_copy(bk[:, LAST, :], bki[:, 3, :]))
            link(dve.tensor_scalar(bk[:, HAS, :], bk[:, CNT, :], 1.0, None, ALU.min))
            link(dve.tensor_tensor(bk[:, NUM, :], bk[:, LAST, :], bk[:, FIRST, :], ALU.subtract))
            link(dve.scalar_tensor_tensor(out=bk[:, NUM, :], in0=bk[:, NUM, :], scalar=1.0, in1=bk[:, HAS, :],
                                          op0=ALU.add, op1=ALU.mult))
            link(dve.tensor_tensor_scan(bk[:, PEND, :], bk[:, NUM, :], bk[:, ZERO, :], 0.0, ALU.add, ALU.add))
            link(dve.tensor_tensor(bk[:, PSTART, :], bk[:, PEND, :], bk[:, NUM, :], ALU.subtract))
            link(dve.tensor_tensor(bk[:, SHIFT, :], bk[:, FIRST, :], bk[:, PSTART, :], ALU.subtract))
            NO, TILE, ROW = range(3)
            link(dve.tensor_copy(pr[:, NO, :], unit_no[:, :]))
            shape = [UQ, UJ, TILES]

            def per_tile(ap):
                return ap.unsqueeze(1).broadcast_to(shape)

            def per_unit(ap):
                return ap.unsqueeze(2).broadcast_to(shape)

            link(dve.tensor_tensor(prc[:, :, :], per_unit(pr[:, NO, :]), per_tile(bk[0:UQ, PEND, 0:TILES]), ALU.is_ge))
            link(dve.tensor_reduce(pr[:, TILE, :], prc[:, :, :], AX.X, ALU.add))
            link(dve.tensor_tensor(prd[:, :, :], per_unit(pr[:, TILE, :]), per_tile(lane[0:UQ, 0:TILES]), ALU.is_equal))
            link(dve.tensor_tensor(prd[:, :, :], prd[:, :, :], per_tile(bk[0:UQ, SHIFT, 0:TILES]), ALU.mult))
            link(dve.tensor_reduce(pr[:, ROW, :], prd[:, :, :], AX.X, ALU.add))
            link(dve.tensor_tensor(pr[:, ROW, :], pr[:, ROW, :], pr[:, NO, :], ALU.add))
            link(dve.tensor_copy(unit_tile[:, :], pr[:, TILE, :]))
            dve.tensor_scalar(unit_row[:, :], pr[:, ROW, :], float(ROWS - 1), None, ALU.min).then_inc(units_ready, 1)

            disorder = dve.value_load(flag[0:1, 0:1], min_val=0, max_val=1)
            with dve.If(disorder > 0):
                dve.memset(e_pos[:, :], 0.0).then_inc(sort_seq, 1)
                dve.memset(e_zero[:, :], 0.0).then_inc(sort_seq, 1)
                dve.wait_ge(sort_seq, 2)
                with dve.Fori(0, TILES + 1) as b:
                    dve.tensor_scalar(e_f[:, :], e_g[:, :], lane[:, ds(b, 1)], None, ALU.is_equal).then_inc(sort_seq, 1)
                    dve.wait_ge(sort_seq, b * 4 + 3)
                    dve.tensor_tensor_scan(e_cum[:, :], e_f[:, :], e_zero[:, :], 0.0, ALU.add, ALU.add).then_inc(sort_seq, 1)
                    dve.wait_ge(sort_seq, b * 4 + 4)
                    dve.scalar_tensor_tensor(out=e_cum[:, :], in0=e_cum[:, :], scalar=base[:, ds(b, 1)], in1=e_f[:, :],
                                             op0=ALU.add, op1=ALU.mult).then_inc(sort_seq, 1)
                    dve.wait_ge(sort_seq, b * 4 + 5)
                    dve.tensor_tensor(e_pos[:, :], e_pos[:, :], e_cum[:, :], ALU.add).then_inc(sort_seq, 1)
                    dve.wait_ge(sort_seq, b * 4 + 6)
                dve.memset(bad[:, 1:2], 0.0).then_inc(place_ready, 1)
            with dve.Else():
                dve.memset(bad[:, 1:2], 0.0).then_inc(place_ready, 1)

            dve.wait_ge(loaded_w, 16 * 29)
            link(dve.tensor_tensor(bcol[:, B_R:B_R + 1], bcol[:, B_IH:B_IH + 1], bcol[:, B_HH:B_HH + 1], ALU.add))
            link(dve.tensor_tensor(bcol[:, B_Z:B_Z + 1], bcol[:, B_IH + 1:B_IH + 2], bcol[:, B_HH + 1:B_HH + 2], ALU.add))

            dve.wait_ge(rows_got, 16 * 2 * UJ)
            link(dve.tensor_copy(got_f[:, 0:UJ, :], got_i[:, 0:UJ, :]))
            link(dve.tensor_scalar(pr[:, TILE, :], pr[:, TILE, :], float(-P), None, ALU.mult))
            for j in range(UJ):
                ins = dve.tensor_scalar(got_f[:, UJ + j, :], got_i[:, UJ + j, :], pr[:, TILE, j:j + 1], None, ALU.add)
            ins.then_inc(rows_float, 1)
            dve.wait_ge(chunks_ready, 2)
            dve.tensor_single_scalar(chunk_src[:, :, :], chunk_code[:, :, :], TYPE_BITS, ALU.arith_shift_right).then_inc(chunks_ready, 1)
            dve.wait_ge(tiles_loaded, 16)

            def one_hot(k, u):
                if u.after(SLOTS):
                    dve.wait_ge(product, u.count(-SLOTS, k))
                for half in range(HALVES):
                    last = dve.tensor_scalar(oh[:, u.slot, half, :], lane[:, :], chunk_dst[:, half, ds(u.n, 1)], None, ALU.is_equal)
                last.then_inc(oh_ready, 1)

            def one_hot_less_one(u):
                if u.after(SLOTS):
                    dve.wait_ge(product, u.count(-SLOTS, 4))
                for half in range(HALVES):
                    last = dve.tensor_scalar(ohm[:, u.slot, half, :], laneb[:, :], chunk_dst[:, half, ds(u.n, 1)], 1.0,
                                             ALU.is_equal, ALU.subtract)
                last.then_inc(oh_ready, 1)

            def tile_of(u):
                return dve.value_load(tile_at[0:1, ds(u.n, 1)], min_val=0, max_val=TILES)

            def sums(k, width):
                dve.memset(acc[:, :], 0.0).then_inc(acc_zero, 1)
                dve.wait_ge(acc_zero, k + 1)

                def beat(at):
                    now, add = at(0), at(3)
                    if now.within():
                        one_hot(k, now)
                    if add.within():
                        tile = tile_of(add)
                        dve.wait_ge(product, add.count(0, k))
                        if add.after(1):
                            dve.wait_ge(acc_done, add.count(-1, k))
                        dve.tensor_tensor(acc_cols(tile, width), acc_cols(tile, width), bank(add.slot % 4, width),
                                          ALU.add).then_inc(acc_done, 1)
                over_units(dve, beat, 3)

            class Seq:

                def __init__(self, s, per):
                    self.s, self.per, self.i, self.n = s, per, 0, 0

                def begin(self, i):
                    self.i, self.n = i, 0

                def __call__(self, ins):
                    self.n += 1
                    ins.then_inc(self.s, 1)
                    dve.wait_ge(self.s, self.i * self.per + self.n)

                def end(self):
                    assert self.n == self.per, self.n

            def norm(k, i, seq, source, target):
                for j in range(GROUP):
                    ins = dve.bn_stats(stats[:, j, :], source(j))
                seq(ins)
                dve.sem_inc(dve_pace, 1)
                for j in range(GROUP):
                    ins = dve.bn_aggr(mv[:, j, :], stats[:, j, :])
                ins.then_inc(var_ready[k], 1)
                dve.wait_ge(std_ready[k], i + 1)
                seq(dve.reciprocal(rs[:, :], sd[:, :]))
                for j in range(GROUP):
                    ins = dve.tensor_scalar(target(i, j), source(j), mv[:, j, 0:1], rs[:, j:j + 1], ALU.subtract, ALU.mult)
                return ins

            def new_x(i, j):
                return xn[:, ds(i * GW + j * P, P)]

            sums(0, FEAT + 1)
            dve.wait_ge(acc_done, 1 * UNITS)
            degree = acc[:, :].rearrange("p (t a) -> p t a", a=AW)[:, 0:TILES, FEAT]
            link(dve.tensor_scalar(rdeg[:, :], degree, 1.0, None, ALU.max))
            link(dve.reciprocal(rdeg[:, :], rdeg[:, :]))
            seq = Seq(sem("dve_gru"), 6)
            with dve.Fori(0, GROUPS) as i:
                seq.begin(i)
                cols = ds(i * GW, GW)
                dve.wait_ge(gates_rz, i * 2 + 1)
                dve.wait_ge(gates_done, i * 4 + 3)
                seq(dve.scalar_tensor_tensor(out=u1[:, :], in0=region(3), scalar=bcol[:, B_HH + 2:B_HH + 3], in1=gr[:, :],
                                             op0=ALU.add, op1=ALU.mult))
                dve.wait_ge(gates_done, i * 4 + 4)
                dve.tensor_tensor(u2[:, :], u1[:, :], region(0), ALU.add).then_inc(n_pre, 1)
                dve.wait_ge(n_ready, i + 1)
                seq(dve.tensor_tensor(u1[:, :], xT[:, cols], gn[:, :], ALU.subtract))
                dve.wait_ge(gates_rz, i * 2 + 2)
                seq(dve.tensor_tensor(u1[:, :], u1[:, :], gz[:, :], ALU.mult))
                seq(dve.tensor_tensor(u1[:, :], u1[:, :], gn[:, :], ALU.add))
                dve.tensor_tensor(u1[:, :], u1[:, :], xT[:, cols], ALU.add).then_inc(y_T[0], 1)
                dve.wait_ge(y_turned[0], i + 1)
                norm(0, i, seq, lambda j: PS[:, 1024 + j * P:1024 + (j + 1) * P], new_x).then_inc(x_ready[0], 1)
                dve.wait_ge(rows_turned_back[0], i + 1)
                dve.tensor_copy(rows[:, cols], region(0)).then_inc(rows_ready[0], 1)
                seq.end()

            def mean(k, i):
                dve.tensor_tensor(mn[:, :].rearrange("p (j d) -> p j d", d=P),
                                  acc[:, ds(i * (GROUP * AW), GROUP * AW)].rearrange("p (j a) -> p j a", a=AW)[:, :, 0:P],
                                  rdeg[:, ds(i * GROUP, GROUP)].unsqueeze(2).broadcast_to([P, GROUP, P]), ALU.mult)\
                    .then_inc(mean_ready[k], 1)

            sums(1, FEAT)
            dve.wait_ge(acc_done, 2 * UNITS)
            with dve.Fori(0, GROUPS) as i:
                mean(1, i)
                dve.wait_ge(rows_turned_back[1], i + 1)
                dve.tensor_copy(rows[:, ds(i * GW, GW)], region(3)).then_inc(rows_ready[1], 1)
            sums(2, FEAT)
            dve.wait_ge(acc_done, 3 * UNITS)
            seq = Seq(sem("dve_sage"), 2)
            with dve.Fori(0, GROUPS) as i:
                seq.begin(i)
                mean(2, i)
                dve.wait_ge(hidden_T[2], i + 1)
                dve.tensor_tensor(u1[:, :], xT[:, ds(i * GW, GW)], cT[:, :], ALU.add).then_inc(y_T[2], 1)
                dve.wait_ge(y_turned[2], i + 1)
                norm(2, i, seq, lambda j: PS[:, 2048 + j * P:2048 + (j + 1) * P], new_x).then_inc(x_ready[2], 1)
                seq.end()

            sums(3, FEAT)
            dve.wait_ge(acc_done, 4 * UNITS)
            seq = Seq(sem("dve_rel"), 2)
            rows_t = rows[:, :].rearrange("p (t d) -> p t d", d=TROW)
            with dve.Fori(0, GROUPS) as i:
                seq.begin(i)
                dve.wait_ge(hidden_T[3], i + 1)
                dve.tensor_tensor(u1[:, :], xT[:, ds(i * GW, GW)], cT[:, :], ALU.add).then_inc(y_T[3], 1)
                dve.wait_ge(y_turned[3], i + 1)
                norm(3, i, seq, lambda j: PS[:, 1024 + j * P:1024 + (j + 1) * P], new_x).then_inc(x_ready[3], 1)
                dve.wait_ge(rows_turned_back[3], i + 1)
                WA = FEAT + 2 * HEADS
                for at, t0, n in ((3072, 0, 3), (3584, 3, 2)):
                    p = PS[:, at:at + n * WA].rearrange("p (t d) -> p t d", d=WA)
                    dve.tensor_copy(rows[:, ds(i * (GROUP * TROW) + t0 * TROW, n * TROW)].rearrange("p (t d) -> p t d", d=TROW)[:, :, 0:FEAT + HEADS],
                                    p[:, :, 0:FEAT + HEADS])
                    ins = dve.tensor_copy(state[:, ds(i * GROUP + t0, n), 0:HEADS], p[:, :, FEAT + HEADS:WA])
                ins.then_inc(rows_ready[3], 1)
                seq.end()

            dve.wait_ge(rows_ready[3], GROUPS)
            score = rows_t[:, :, FEAT:FEAT + HEADS]
            part = [rows[:, :].bitcast(BF16).rearrange("p (t d) -> p t d", d=2 * TROW)[:, :, 2 * (FEAT + HEADS) + j:2 * TROW:3] for j in range(3)]
            link(dve.tensor_copy(part[0], score))
            link(dve.tensor_tensor(spl[:, 0, :, :], score, part[0], ALU.subtract))
            link(dve.tensor_copy(part[1], spl[:, 0, :, :]))
            link(dve.tensor_tensor(spl[:, 1, :, :], spl[:, 0, :, :], part[1], ALU.subtract))
            dve.tensor_copy(part[2], spl[:, 1, :, :]).then_inc(gat_rows, 1)
            dve.memset(state[:, TILES, :], 0.0)
            link(dve.tensor_tensor(spl[:, 0, :, :], score, state[:, 0:TILES, 0:HEADS], ALU.add))
            link(dve.scalar_tensor_tensor(out=state[:, 0:TILES, HEADS:2 * HEADS], in0=spl[:, 0, :, :], scalar=0.2,
                                          in1=spl[:, 0, :, :], op0=ALU.mult, op1=ALU.max))
            dve.memset(acc[:, TILES * AW:], 0.0)
            acc_f = acc[:, 0:TILES * AW].rearrange("p (t h f) -> p t h f", t=TILES, h=HEADS)
            dve.memset(acc_f[:, :, :, HEAD_F:HEAD_F + 1].rearrange("p t h f -> p (t h) f"), 1.0)
            dve.tensor_copy(acc_f[:, :, :, 0:HEAD_F], rows_t[:, :, 0:FEAT].rearrange("p t (h f) -> p t h f", h=HEADS))\
                .then_inc(acc_zero, 1)
            dve.wait_ge(acc_zero, 5)

            max_step, max_kept, logit_step, rescaled = sem("max_step"), sem("max_kept"), sem("logit_step"), sem("rescaled")

            def beat(at):
                now, m, e, w, a = at(0), at(LAG_MAX), at(LAG_LOGIT), at(LAG_WEIGHT), at(LAG_ADD)
                do_now, do_m, do_e, do_w, do_a = (u.within() for u in (now, m, e, w, a))
                f = bank(5, 8 * HALVES).rearrange("p (a b) -> p a b", a=HALVES)
                if do_m:
                    s = m.slot
                    dve.wait_ge(masked, m.count())
                    dve.tensor_reduce(cm[:, s, 0:4], bank(1 + 2 * (s % 2), 1024).rearrange("p (a h e) -> p h a e", a=HALVES, h=HEADS),
                                      AX.XY, ALU.max).then_inc(max_step, 1)
                    tile_m = tile_of(m)
                    here = state[:, ds(tile_m, 1), :].rearrange("p a b -> p (a b)")
                if do_a:
                    tile_a = tile_of(a)
                    sums_here = acc_cols(tile_a, AW)
                    if a.after(1):
                        dve.wait_ge(acc_done, a.count(-1, 4))
                    dve.tensor_tensor(sums_here.rearrange("p (h f) -> p h f", h=HEADS), sums_here.rearrange("p (h f) -> p h f", h=HEADS),
                                      rescale[:, a.slot, :].unsqueeze(2).broadcast_to([P, HEADS, HEAD_F + 1]), ALU.mult)\
                        .then_inc(rescaled, 1)
                if do_m:
                    if m.after(1):
                        dve.wait_ge(max_kept, m.count(-1))
                    dve.wait_ge(max_step, m.n * 5 + 1)
                    dve.tensor_tensor(cm[:, s, 4:8], cm[:, s, 0:4], here[:, 0:4], ALU.add).then_inc(max_step, 1)
                if do_e:
                    dve.wait_ge(spread, e.count())
                    dve.tensor_tensor(lg[:, e.slot, 0, :, :], g[:, e.slot, :, FEAT:FEAT + HEADS], f[:, :, 0:4], ALU.add).then_inc(logit_step, 1)
                if do_m:
                    dve.wait_ge(max_step, m.n * 5 + 2)
                    dve.scalar_tensor_tensor(out=cm[:, s, 8:12], in0=cm[:, s, 4:8], scalar=0.2, in1=cm[:, s, 4:8],
                                             op0=ALU.mult, op1=ALU.max).then_inc(max_step, 1)
                if do_e:
                    dve.wait_ge(logit_step, e.n * 3 + 1)
                    dve.scalar_tensor_tensor(out=lg[:, e.slot, 1, :, :], in0=lg[:, e.slot, 0, :, :], scalar=0.2, in1=lg[:, e.slot, 0, :, :],
                                             op0=ALU.mult, op1=ALU.max).then_inc(logit_step, 1)
                if do_m:
                    dve.wait_ge(max_step, m.n * 5 + 3)
                    dve.tensor_tensor(bm[:, s, 4:8], cm[:, s, 8:12], here[:, 4:8], ALU.max).then_inc(max_step, 1)
                if do_e:
                    dve.wait_ge(logit_step, e.n * 3 + 2)
                    dve.tensor_tensor(lg[:, e.slot, 2, :, :], lg[:, e.slot, 1, :, :], f[:, :, 4:8], ALU.subtract).then_inc(logit_step, 1)
                if do_m:
                    dve.wait_ge(max_step, m.n * 5 + 4)
                    dve.tensor_scalar(bm[:, s, 0:4], here[:, 0:4], 1.0, None, ALU.mult).then_inc(seg_max, 1)
                    dve.tensor_tensor(dm[:, s, :], here[:, 4:8], bm[:, s, 4:8], ALU.subtract).then_inc(max_step, 1)
                if do_e:
                    dve.wait_ge(logit_step, e.n * 3 + 3)
                    dve.tensor_scalar(wd[:, e.slot, :, :], lg[:, e.slot, 2, :, :], 0.0, None, ALU.min).then_inc(logits, 1)
                if do_now:
                    one_hot_less_one(now)
                if do_m:
                    dve.wait_ge(max_step, m.n * 5 + 5)
                    dve.tensor_scalar(here[:, 4:8], bm[:, s, 4:8], 1.0, None, ALU.mult).then_inc(max_kept, 1)
                if do_a:
                    dve.wait_ge(rescaled, a.count())
                    dve.wait_ge(product, a.count(0, 4))
                    dve.tensor_tensor(sums_here, sums_here, bank(6 + a.slot % 2, AW), ALU.add).then_inc(acc_done, 1)
                if do_w:
                    dve.wait_ge(weights, w.count())
                    dve.tensor_tensor(wm[:, w.slot, :, :, 0:HEAD_F], g[:, w.slot, :, 0:FEAT].rearrange("p a (h f) -> p a h f", h=HEADS),
                                      wm[:, w.slot, :, :, HEAD_F:HEAD_F + 1].broadcast_to([P, HALVES, HEADS, HEAD_F]), ALU.mult)\
                        .then_inc(weighted, 1)
            over_units(dve, beat, LAG_LAST)

            dve.wait_ge(acc_done, 5 * UNITS)
            accv = acc[:, 0:TILES * AW].rearrange("p (t h f) -> p t h f", t=TILES, h=HEADS)
            link(dve.tensor_scalar(den[:, :, :], accv[:, :, :, HEAD_F], 1e-10, None, ALU.max))
            link(dve.reciprocal(den[:, :, :], den[:, :, :]))
            seq = Seq(sem("dve_out"), 5)
            with dve.Fori(0, GROUPS) as i:
                seq.begin(i)
                here = acc[:, ds(i * (GROUP * AW), GROUP * AW)].rearrange("p (q f) -> p q f", f=HEAD_F + 1)
                seq(dve.tensor_tensor(u1[:, :].rearrange("p (q f) -> p q f", f=HEAD_F), here[:, :, 0:HEAD_F],
                                      den[:, ds(i * GROUP, GROUP), :].rearrange("p t h -> p (t h)").unsqueeze(2)
                                      .broadcast_to([P, GROUP * HEADS, HEAD_F]), ALU.mult))
                seq(dve.tensor_tensor(u1[:, :].rearrange("p (j d) -> p j d", d=P), u1[:, :].rearrange("p (j d) -> p j d", d=P),
                                      L3b_bc[:, :].unsqueeze(1).broadcast_to([P, GROUP, P]), ALU.add))
                seq(dve.tensor_tensor(u1[:, :], u1[:, :], xn[:, ds(i * GW, GW)], ALU.add))
                norm(4, i, seq, lambda j: u1[:, j * P:(j + 1) * P],
                     lambda i, j: rows[:, ds(i * GW + j * P, P)]).then_inc(out_rows, 1)
                dve.wait_ge(out_rows, i + 1)
                seq.end()


_INS = ['x', 'src', 'dst', 'edge_type_8', 'L0_gnn_message_W', 'L0_gnn_message_b', 'L0_gnn_gru_w_ih', 'L0_gnn_gru_w_hh',
        'L0_gnn_gru_b_ih', 'L0_gnn_gru_b_hh', 'L1_gnn_W1', 'L1_gnn_b1', 'L1_gnn_W2', 'L1_gnn_b2', 'L1_gnn_c1_Wl',
        'L1_gnn_c1_bl', 'L1_gnn_c1_Wr', 'L1_gnn_c2_Wl', 'L1_gnn_c2_bl', 'L1_gnn_c2_Wr', 'L2_gnn_weight',
        'L2_gnn_self_loop_weight', 'L2_gnn_bias', 'L3_gnn_W', 'L3_gnn_att', 'L3_gnn_bias']


def kernel(**inputs):
    import numpy as _np
    import concourse.bacc as _bacc
    from concourse import mybir as _mybir
    from concourse.bass_utils import run_bass_kernel_spmd as _run

    nc = _bacc.Bacc("TRN2", target_bir_lowering=False, num_devices=1)
    arrays, args = {}, []
    for name in _INS:
        a = _np.ascontiguousarray(inputs[name])
        arrays[f"in_{name}_dram"] = a
        args.append(nc.dram_tensor(f"in_{name}_dram", a.shape, _mybir.dt.from_np(a.dtype), kind="ExternalInput").ap())
    args.append(nc.dram_tensor("out_0_dram", (NODES, FEAT), F32, kind="ExternalOutput").ap())
    build(nc, *args)
    r = _run(nc, [arrays], core_ids=[0])
    return r.results[0]["out_0_dram"]
```

```python
import concourse.bass as bass
from concourse import mybir
from concourse.alu_op_type import AluOpType as ALU
from contextlib import ExitStack

F32 = mybir.dt.float32
BF16 = mybir.dt.bfloat16
I32 = mybir.dt.int32
ACT = mybir.ActivationFunctionType
AX = mybir.AxisListType
ds = bass.ds

P = 128
NODES, EDGES, FEAT, TYPES = 3125, 53125, 128, 8
HEADS, HEAD_F = 4, 32
TILES = -(-NODES // P)
PADN = TILES * P
FULL = NODES // P
LASTN = NODES - FULL * P
HALVES = 2
UNIT = HALVES * P
PADE = -(-EDGES // UNIT) * UNIT
PER = PADE // P
LASTP = EDGES - (P - 1) * PER
P_BITS, TYPE_BITS = P.bit_length() - 1, TYPES.bit_length() - 1
SLOTS = 8
GROUP = 5
GROUPS = TILES // GROUP
GW = GROUP * P
AW = 132
TROW = FEAT + HEADS + 6
FAR = 2.0 ** 100
EPS = 1e-5
LAG_TURN, LAG_MASK, LAG_MAX, LAG_SPREAD, LAG_LOGIT, LAG_EXP, LAG_WEIGHT, LAG_SUM, LAG_ADD = 1, 2, 3, 4, 4, 5, 5, 6, 7
LAG_LAST = 7
LEAD = 2


class Cut:

    def __init__(self, halves, uj, skew):
        self.halves, self.edges, self.skew = halves, halves * P, skew
        self.bits = self.edges.bit_length() - 1
        self.rows = PADE // self.edges
        self.units = self.rows + TILES - 1
        self.turns = self.units // SLOTS
        self.uj, self.uq = uj, self.units // uj
        assert self.uq * uj == self.units and self.uq <= P and self.turns * SLOTS == self.units


CHUNKS = Cut(1, 4, 0)
PAIRS = Cut(HALVES, 2, LAG_MAX)
assert GROUPS * GROUP == TILES and 0 < LASTP <= PER


class Unit:

    def __init__(self, cut, turn, at):
        self.cut = cut
        self.n = turn * SLOTS + at
        self.at = at
        self.slot = at % SLOTS
        self.round = turn + at // SLOTS

    def count(self, more=0, k=0):
        return self.n + (1 + more + k * CHUNKS.units)

    def gathered(self, k):
        return self.round * (16 * self.cut.halves) + (self.cut.halves + k * CHUNKS.turns) * 16

    def within(self):
        return not isinstance(self.n, int) or 0 <= self.n < self.cut.units

    def loads(self):
        return not isinstance(self.n, int) or -self.cut.skew <= self.n < self.cut.units

    def after(self, n):
        return not isinstance(self.n, int) or self.n >= n


def over_units(eng, cut, step, lag):
    for b in range(SLOTS):
        step(lambda delay: Unit(cut, 0, b - delay))
    with eng.Fori(1, cut.turns) as turn:
        for b in range(SLOTS):
            step(lambda delay: Unit(cut, turn, b - delay))
    for b in range(lag):
        step(lambda delay: Unit(cut, cut.turns, b - delay))


def build(nc, x, src, dst, etype, L0W, L0b, w_ih, w_hh, b_ih, b_hh, W1, b1, W2, b2, c1l, c1b, c1r,
          c2l, c2b, c2r, L2W, L2S, L2b, L3W, L3a, L3b, out):
    with ExitStack() as ctx:
        def sb(name, shape, dt=F32):
            return ctx.enter_context(nc.sbuf_tensor(name, shape, dt))

        def sem(name):
            return ctx.enter_context(nc.semaphore(name))

        typed_table = nc.dram_tensor("typed_table", (PADN * TYPES, FEAT), F32, kind="Internal").ap()
        node_table = nc.dram_tensor("node_table", (PADN, FEAT), F32, kind="Internal").ap()
        gat_table = nc.dram_tensor("gat_table", (PADN, TROW), F32, kind="Internal").ap()
        list_code = nc.dram_tensor("list_code", (PADE, 1), I32, kind="Internal").ap()
        list_dst = nc.dram_tensor("list_dst", (PADE, 1), I32, kind="Internal").ap()
        unit_tiles = {cut: nc.dram_tensor(f"unit_tiles{cut.halves}", (cut.units, 1), I32, kind="Internal").ap() for cut in (CHUNKS, PAIRS)}

        PS = ctx.enter_context(nc.psum_tensor("PS", [P, 8 * 512], F32))

        xn = sb("xn", [P, PADN])
        xT = sb("xT", [P, PADN])
        hT = sb("hT", [P, PADN])
        rows = sb("rows", [P, TILES * TROW])
        acc = sb("acc", [P, (TILES + 1) * AW])
        work = sb("work", [P, GROUP * TYPES * FEAT])
        typed_out = work[:, :].rearrange("p (j n) -> p j n", j=GROUP)
        mT, cT, mn, gr, gz, gn, u1, u2 = (work[:, q * GW:(q + 1) * GW] for q in range(8))
        L0W_sb = sb("L0W_sb", [P, TYPES, FEAT])
        L2W_sb = sb("L2W_sb", [P, TYPES, FEAT])
        L0b_parts = sb("L0b_parts", [96, TYPES * FEAT], BF16)
        L0b_raw = rows[0:96, 0:2 * TYPES * FEAT].rearrange("p (a n) -> p a n", a=2)
        L3b_bc = sb("L3b_bc", [P, FEAT])
        wraw = sb("wraw", [P, 13, FEAT])
        wT = sb("wT", [P, 12, FEAT])
        w3a = sb("w3a", [P, FEAT + 2 * HEADS])
        att = sb("att", [P, 2 * HEADS])
        selfw = sb("selfw", [P, FEAT])
        bcol = sb("bcol", [P, 12])
        identf = sb("identf", [P, P])
        identb = sb("identb", [P, P], BF16)
        ident4 = sb("ident4", [P, HEADS, P], BF16)
        headsel = sb("headsel", [12, HEADS, P], BF16)
        onesf = sb("onesf", [P, P])
        onesb = sb("onesb", [96, P], BF16)
        below = sb("below", [P, P])
        lane_i = sb("lane_i", [P, P], I32)
        lane = sb("lane", [P, P])
        laneb = sb("laneb", [P, P], BF16)
        epst = sb("epst", [P, 1])
        rdeg = sb("rdeg", [P, TILES])

        e_dst = sb("e_dst", [P, PER], I32)
        e_next = sb("e_next", [P, PER], I32)
        e_code = sb("e_code", [P, PER], I32)
        e_type = sb("e_type", [P, PER], I32)
        e_bkt = sb("e_bkt", [P, PER], I32)
        e_f = sb("e_f", [P, PER])
        e_g = sb("e_g", [P, PER])
        e_pos = sb("e_pos", [P, PER])
        e_cum = sb("e_cum", [P, PER])
        e_zero = sb("e_zero", [P, PER])
        rowtot = sb("rowtot", [P, TILES + 1])
        bk = sb("bk", [P, 12, TILES + 1])
        bki = sb("bki", [P, 4, TILES + 1], I32)
        bad = sb("bad", [P, 2])
        flag = sb("flag", [P, 1], I32)
        base = sb("base", [P, TILES + 1])
        scat = sb("scat", [P, 3], I32)
        def of_cut(name, shape, dt=F32):
            return {cut: sb(f"{name}{cut.halves}", shape(cut), dt) for cut in (CHUNKS, PAIRS)}

        pr = of_cut("pr", lambda c: [c.uq, 3, c.uj])
        prc = of_cut("prc", lambda c: [c.uq, c.uj, TILES])
        prd = of_cut("prd", lambda c: [c.uq, c.uj, TILES])
        unit_no = of_cut("unit_no", lambda c: [c.uq, c.uj], I32)
        unit_row = of_cut("unit_row", lambda c: [c.uq, c.uj], I32)
        unit_tile = of_cut("unit_tile", lambda c: [c.uq, c.uj], I32)
        got_i = of_cut("got_i", lambda c: [c.uq, 2 * c.uj, c.edges], I32)
        got_f = of_cut("got_f", lambda c: [c.uq, 2 * c.uj, c.edges])
        unit_code = sb("unit_code", [P, 1, CHUNKS.units], I32)
        unit_src = of_cut("unit_src", lambda c: [P, c.halves, c.units], I32)
        unit_dst = of_cut("unit_dst", lambda c: [P, c.halves, c.units])
        tile_at = of_cut("tile_at", lambda c: [1, c.units + 4], I32)

        ix = sb("ix", [P, SLOTS, HALVES], I32)
        g = sb("g", [P, SLOTS, HALVES, TROW])
        oh = sb("oh", [P, SLOTS, HALVES, P])
        ohm = sb("ohm", [P, SLOTS, HALVES, P], BF16)
        ohT = sb("ohT", [P, SLOTS, HALVES, P], BF16)
        aT = sb("aT", [12, SLOTS, HALVES, P], BF16)
        cm = sb("cm", [P, SLOTS, 12])
        lg = sb("lg", [P, SLOTS, 3, HALVES, HEADS])
        bm = sb("bm", [P, SLOTS, 8])
        bmp = sb("bmp", [P, SLOTS, 3, 8], BF16)
        bmr = sb("bmr", [P, SLOTS, 8])
        zero8 = sb("zero8", [P, 8])
        fs = sb("fs", [P, SLOTS, HALVES, 8])
        state = sb("state", [P, TILES + 1, 8])
        wd = sb("wd", [P, SLOTS, HALVES, HEADS])
        dm = sb("dm", [P, SLOTS, HEADS])
        rescale = sb("rescale", [P, SLOTS, HEADS])
        wm = sb("wm", [P, SLOTS, HALVES, HEADS, HEAD_F + 1])

        stats = sb("stats", [P, GROUP, 6])
        mv = sb("mv", [P, GROUP, 2])
        sd = sb("sd", [P, GROUP])
        rs = sb("rs", [P, GROUP])
        den = sb("den", [P, TILES, HEADS])
        spl = sb("spl", [P, 2, TILES, HEADS])

        loaded_x, loaded_w, loaded_e = sem("loaded_x"), sem("loaded_w"), sem("loaded_e")
        pool_seq, const_ready = sem("pool_seq"), sem("const_ready")
        dve_seq, dve_pace = sem("dve_seq"), sem("dve_pace")
        code_ready, order_known = sem("code_ready"), sem("order_known")
        bucket_sums, bucket_base, bad_sum = sem("bucket_sums"), sem("bucket_base"), sem("bad_sum")
        compared, counted, bad_ready = sem("compared"), sem("counted"), sem("bad_ready")
        place_ready, scattered = sem("place_ready"), sem("scattered")
        units_ready, unit_dma = sem("units_ready"), sem("unit_dma")
        rows_got = {cut: sem(f"rows_got{cut.halves}") for cut in (CHUNKS, PAIRS)}
        rows_float, rows_turned, lists_ready = sem("rows_float"), sem("rows_turned"), sem("lists_ready")
        weights_turned, weights_ready, att_zeroed = sem("weights_turned"), sem("weights_ready"), sem("att_zeroed")
        tiles_loaded, sort_seq, bias_split, oh_float = sem("tiles_loaded"), sem("sort_seq"), sem("bias_split"), sem("oh_float")
        x_padded, x_turned, xT_ready = sem("x_padded"), sem("x_turned"), sem("xT_ready")
        pace = sem("pace")
        typed_done = [sem(f"typed_done{k}") for k in range(2)]
        typed_evac = [sem(f"typed_evac{k}") for k in range(2)]
        typed_written = [[sem(f"typed_written{k}_{j}") for j in range(GROUP)] for k in range(2)]
        table_written = {k: sem(f"table_written{k}") for k in (1, 2, 4,)}
        arrived = [sem(f"arrived{b}") for b in range(SLOTS)]
        ix_ready = sem("ix_ready")
        oh_ready = sem("oh_ready")
        product = sem("product")
        acc_done = sem("acc_done")
        acc_zero = sem("acc_zero")
        agg_turned = {k: sem(f"agg_turned{k}") for k in (0, 1, 2,)}
        agg_T = {k: sem(f"agg_T{k}") for k in (0, 1, 2,)}
        mean_ready = [sem(f"mean_ready{k}") for k in range(4)]
        linear_done = {k: sem(f"linear_done{k}") for k in (0, 1, 2, 3,)}
        hidden_T = {k: sem(f"hidden_T{k}") for k in (0, 1, 2, 3,)}
        linear2_done = {k: sem(f"linear2_done{k}") for k in (1,)}
        hidden2_T = {k: sem(f"hidden2_T{k}") for k in (1,)}
        rows_turned_back = {k: sem(f"rows_turned_back{k}") for k in (0, 1, 3,)}
        rows_ready = [sem(f"rows_ready{k}") for k in range(4)]
        gates_done, gates_rz, n_pre, n_ready = sem("gates_done"), sem("gates_rz"), sem("n_pre"), sem("n_ready")
        y_T = {k: sem(f"y_T{k}") for k in (0, 2, 3,)}
        y_turned = {k: sem(f"y_turned{k}") for k in (0, 2, 3,)}
        var_ready = [sem(f"var_ready{k}") for k in range(5)]
        std_ready = [sem(f"std_ready{k}") for k in range(5)]
        x_ready = [sem(f"x_ready{k}") for k in range(5)]
        x_again = {k: sem(f"x_again{k}") for k in (0, 2, 3,)}
        x_T = {k: sem(f"x_T{k}") for k in (0, 2, 3,)}
        gat_rows = sem("gat_rows")
        turned, turned_sb, masked, seg_max = sem("turned"), sem("turned_sb"), sem("masked"), sem("seg_max")
        split_ready = sem("split_ready")
        spread, logits, weights, weighted = sem("spread"), sem("logits"), sem("weights"), sem("weighted")
        out_rows, out_written = sem("out_rows"), sem("out_written")

        block = ctx.enter_context(nc.Block())

        IH, HH, W1i, W2i, C1L, C1R, C2L, C2R = 0, 3, 6, 7, 8, 9, 10, 11
        L3i = 12
        B_IH, B_HH, B1, B2, B_C1, B_C2, B_L2, B_R, B_Z = 0, 3, 6, 7, 8, 9, 10, 11, 0

        def region(r, width=GW):
            return PS[:, 1024 * r:1024 * r + width]

        def bank(b, n=512, p=P):
            return PS[0:p, 512 * b:512 * b + n]

        def acc_cols(tile, n):
            return acc[:, ds(tile * AW, n)]

        @block.sync
        def _(sp):
            sp.wait_ge(x_padded, 1)
            sp.dma_start(xn[:, 0:FULL * P].rearrange("p (t d) -> p t d", d=FEAT),
                         x[0:FULL * P, :].rearrange("(t p) d -> p t d", p=P)).then_inc(loaded_x, 16)
            sp.dma_start(xn[0:LASTN, FULL * P:PADN], x[FULL * P:NODES, :]).then_inc(loaded_x, 16)
            sp.wait_ge(x_padded, 2)
            for tile, arr in ((e_dst, dst), (e_code, src), (e_type, etype)):
                sp.dma_start(tile[0:P - 1, :], arr[0:(P - 1) * PER].rearrange("(p t) -> p t", t=PER)).then_inc(loaded_e, 16)
                sp.dma_start(tile[P - 1:P, 0:LASTP], arr[(P - 1) * PER:EDGES].rearrange("(a t) -> a t", a=1)).then_inc(loaded_e, 16)
            sp.dma_start(e_next[0:P - 1, :], dst[1:1 + (P - 1) * PER].rearrange("(p t) -> p t", t=PER)).then_inc(loaded_e, 16)
            sp.dma_start(e_next[P - 1:P, 0:LASTP - 1], dst[(P - 1) * PER + 1:EDGES].rearrange("(a t) -> a t", a=1)).then_inc(loaded_e, 16)

            def typed(k):
                with sp.Fori(0, GROUPS) as i:
                    for j in range(GROUP):
                        sp.wait_ge(typed_evac[k], i * (2 * GROUP) + 2 * j + 2)
                        sp.dma_start(typed_table[ds(i * (GW * TYPES) + j * P * TYPES, P * TYPES), :].rearrange("(p t) d -> p (t d)", t=TYPES),
                                     typed_out[:, j, :]).then_inc(typed_written[k][j], 16)

            def plain(k):
                with sp.Fori(0, GROUPS) as i:
                    sp.wait_ge(rows_ready[k], i + 1)
                    sp.dma_start(node_table[ds(i * GW, GW), :].rearrange("(j p) d -> p j d", p=P),
                                 rows[:, ds(i * GW, GW)].rearrange("p (j d) -> p j d", d=FEAT)).then_inc(table_written[k + 1], 16)

            typed(0)
            plain(0)
            plain(1)
            typed(1)
            sp.wait_ge(gat_rows, 1)
            sp.dma_start(gat_table.rearrange("(t p) d -> p t d", p=P),
                         rows[:, :].rearrange("p (t d) -> p t d", d=TROW)).then_inc(table_written[4], 16)
            with sp.Fori(0, GROUPS - 1) as i:
                sp.wait_ge(out_rows, i + 1)
                sp.dma_start(out[ds(i * GW, GW), :].rearrange("(j p) d -> p j d", p=P),
                             rows[:, ds(i * GW, GW)].rearrange("p (j d) -> p j d", d=FEAT)).then_inc(out_written, 16)
            sp.wait_ge(out_rows, GROUPS)
            sp.dma_start(out[(GROUPS - 1) * GW:FULL * P, :].rearrange("(j p) d -> p j d", p=P),
                         rows[:, (GROUPS - 1) * GW:FULL * P].rearrange("p (j d) -> p j d", d=FEAT)).then_inc(out_written, 16)
            sp.dma_start(out[FULL * P:NODES, :], rows[0:LASTN, FULL * P:PADN]).then_inc(out_written, 16)
            sp.wait_ge(out_written, 16 * (GROUPS + 1))

        @block.gpsimd
        def _(pool):
            steps = [0]

            def link(ins):
                steps[0] += 1
                ins.then_inc(pool_seq, 1)
                pool.wait_ge(pool_seq, steps[0])

            pool.memset(xn[:, FULL * P:PADN], 0.0).then_inc(x_padded, 1)
            pool.memset(e_dst[:, :], PADN)
            pool.memset(e_next[:, :], PADN)
            pool.memset(e_code[:, :], 0)
            pool.memset(e_type[:, :], 0).then_inc(x_padded, 1)
            link(pool.memset(identf[:, :], 0.0))
            link(pool.affine_select(out=identf[:, :], in_=identf[:, :], compare_op=ALU.not_equal, fill=1.0,
                                    base=0, pattern=[[-1, P]], channel_multiplier=1))
            link(pool.tensor_copy(identb[:, :], identf[:, :]))
            link(pool.memset(ident4[:, :, :], 0.0))
            link(pool.affine_select(out=ident4[:, :, :], in_=ident4[:, :, :], compare_op=ALU.not_equal, fill=FAR,
                                    base=0, pattern=[[0, HEADS], [-1, P]], channel_multiplier=1))
            link(pool.memset(onesf[:, :], 1.0))
            link(pool.affine_select(out=below[:, :], in_=onesf[:, :], compare_op=ALU.is_gt, fill=0.0,
                                    base=0, pattern=[[1, P]], channel_multiplier=-1))
            link(pool.memset(headsel[:, :, :], 1.0))
            link(pool.affine_select(out=headsel[:, :, :], in_=headsel[:, :, :], compare_op=ALU.is_ge, fill=0.0,
                                    base=0, pattern=[[-3, HEADS], [0, P]], channel_multiplier=1))
            link(pool.affine_select(out=headsel[:, :, :], in_=headsel[:, :, :], compare_op=ALU.is_ge, fill=0.0,
                                    base=2, pattern=[[3, HEADS], [0, P]], channel_multiplier=-1))
            link(pool.iota(lane_i[:, :], pattern=[[1, P]], base=0, channel_multiplier=0))
            link(pool.tensor_copy(lane[:, :], lane_i[:, :]))
            link(pool.tensor_copy(laneb[:, :], lane_i[:, :]))
            for cut in (CHUNKS, PAIRS):
                link(pool.iota(unit_no[cut][:, :], pattern=[[cut.uq, cut.uj]], base=0, channel_multiplier=1))
            link(pool.memset(epst[:, :], EPS))
            link(pool.memset(zero8[:, :], 0.0))
            for cut in (CHUNKS, PAIRS):
                link(pool.memset(tile_at[cut][:, :], 0))
            link(pool.memset(onesb[:, :], 1.0))
            pool.memset(g[:, :, :, :], 1.0).then_inc(const_ready, 1)

            pool.wait_ge(code_ready, 1)
            pool.wait_ge(order_known, 1)
            disorder = pool.value_load(flag[0:1, 0:1], min_val=0, max_val=1)
            with pool.If(disorder > 0):
                pool.wait_ge(place_ready, 1)
                with pool.Fori(0, PER) as t:
                    pool.tensor_copy(scat[:, 0:1], e_pos[:, ds(t, 1)])
                    pool.tensor_copy(scat[:, 1:2], e_code[:, ds(t, 1)])
                    pool.tensor_copy(scat[:, 2:3], e_dst[:, ds(t, 1)]).then_inc(place_ready, 1)
                    pool.wait_ge(place_ready, t + 2)
                    pool.sem_inc(pace, 1)
                    pool.indirect_dma_start(list_code, bass.IndirectOffsetOnAxis(ap=scat[:, 0:1], axis=0),
                                            scat[:, 1:2], None).then_inc(scattered, 16)
                    pool.indirect_dma_start(list_dst, bass.IndirectOffsetOnAxis(ap=scat[:, 0:1], axis=0),
                                            scat[:, 2:3], None).then_inc(scattered, 16)
                    pool.wait_ge(scattered, t * 32 + 32)
                    pool.sem_inc(pace, 1)
            with pool.Else():
                pool.dma_start(list_code.rearrange("(p t) a -> p (t a)", t=PER), e_code[:, :]).then_inc(scattered, 16)
                pool.dma_start(list_dst.rearrange("(p t) a -> p (t a)", t=PER), e_dst[:, :]).then_inc(scattered, 16)
                pool.wait_ge(scattered, 32)
                pool.sem_inc(pace, 1)

            for at, cut in enumerate((CHUNKS, PAIRS)):
                pool.wait_ge(units_ready, at + 1)
                pool.sem_inc(pace, 1)
                code_rows = list_code.rearrange("(r e) a -> r (e a)", e=cut.edges)
                dst_rows = list_dst.rearrange("(r e) a -> r (e a)", e=cut.edges)
                for j in range(cut.uj):
                    where = bass.IndirectOffsetOnAxis(ap=unit_row[cut][:, j:j + 1], axis=0)
                    pool.indirect_dma_start(got_i[cut][:, j, :], None, code_rows, where).then_inc(rows_got[cut], 16)
                    pool.indirect_dma_start(got_i[cut][:, cut.uj + j, :], None, dst_rows, where).then_inc(rows_got[cut], 16)
                pool.dma_start(unit_tiles[cut].rearrange("(j p) a -> p (j a)", p=cut.uq), unit_tile[cut][:, :],
                               allow_slow_non_contiguous=True).then_inc(unit_dma, 16)
            pool.wait_ge(unit_dma, 32)
            for cut in (CHUNKS, PAIRS):
                pool.dma_start(tile_at[cut][:, cut.skew:cut.skew + cut.units], unit_tiles[cut].rearrange("n a -> a n")).then_inc(tiles_loaded, 16)

            split_step = sem("split_step")

            def split(u):
                if not u.within():
                    return
                whole, left = bm[:, u.slot, :], bmr[:, u.slot, :]
                part = [bmp[:, u.slot, n, :] for n in range(3)]
                pool.wait_ge(seg_max, u.count())
                pool.tensor_tensor(part[0], whole, zero8[:, :], ALU.add).then_inc(split_step, 1)
                pool.wait_ge(split_step, u.n * 3 + 1)
                pool.tensor_tensor(left, whole, part[0], ALU.subtract).then_inc(split_step, 1)
                pool.wait_ge(split_step, u.n * 3 + 2)
                pool.tensor_tensor(part[1], left, zero8[:, :], ALU.add).then_inc(split_step, 1)
                pool.wait_ge(split_step, u.n * 3 + 3)
                pool.tensor_tensor(part[2], left, part[1], ALU.subtract).then_inc(split_ready, 1)

            def weigh(u):
                if not u.within():
                    return
                pool.wait_ge(weights, u.count())
                pool.tensor_tensor(wm[:, u.slot, :, :, 0:HEAD_F], g[:, u.slot, :, 0:FEAT].rearrange("p a (h f) -> p a h f", h=HEADS),
                                   wm[:, u.slot, :, :, HEAD_F:HEAD_F + 1].broadcast_to([P, HALVES, HEADS, HEAD_F]), ALU.mult)\
                    .then_inc(weighted, 1)

            def gathers(k, cut, table, width, written, total):
                for s in written:
                    pool.wait_ge(s, total)

                def gather(u):
                    pool.wait_ge(ix_ready, u.count(0, k))
                    pool.sem_inc(pace, 1)
                    for half in range(cut.halves):
                        pool.indirect_dma_start(g[:, u.slot, half, 0:width], None, table,
                                                bass.IndirectOffsetOnAxis(ap=ix[:, u.slot, half:half + 1], axis=0))\
                            .then_inc(arrived[u.slot], 16)

                def beat(at):
                    if k == 4:
                        split(at(LEAD + LAG_MAX))
                        weigh(at(LEAD + LAG_WEIGHT))
                    u = at(0)
                    if u.within():
                        gather(u)
                over_units(pool, cut, beat, LEAD + LAG_WEIGHT if k == 4 else 0)

            gathers(0, CHUNKS, typed_table, FEAT, typed_written[0], 16 * GROUPS)
            gathers(1, CHUNKS, node_table, FEAT, [table_written[1]], 16 * GROUPS)
            gathers(2, CHUNKS, node_table, FEAT, [table_written[2]], 16 * GROUPS)
            gathers(3, CHUNKS, typed_table, FEAT, typed_written[1], 16 * GROUPS)
            gathers(4, PAIRS, gat_table, TROW, [table_written[4]], 16)

        @block.scalar
        def _(act):
            for n, w in ((W1i, W1), (W2i, W2), (C1L, c1l), (C1R, c1r), (C2L, c2l), (C2R, c2r), (L3i, L3W)):
                act.dma_start(wraw[:, n, :], w).then_inc(loaded_w, 16)
            for n, w in ((IH, w_ih), (HH, w_hh)):
                act.dma_start(wraw[:, n:n + 3, :], w.rearrange("(k p) d -> p k d", p=P)).then_inc(loaded_w, 16)
            act.dma_start(L0W_sb[:, :, :], L0W.rearrange("t h d -> h t d")).then_inc(loaded_w, 16)
            act.dma_start(L2W_sb[:, :, :], L2W.rearrange("t h d -> h t d")).then_inc(loaded_w, 16)
            act.dma_start(selfw[:, :], L2S).then_inc(loaded_w, 16)
            act.dma_start(L0b_raw[:, 0, :], L0b.rearrange("t d -> (t d)").partition_broadcast(96)).then_inc(loaded_w, 16)
            act.dma_start(L3b_bc[:, :], L3b.partition_broadcast(P)).then_inc(loaded_w, 16)
            for n, b in ((B_IH, b_ih), (B_HH, b_hh)):
                act.dma_start(bcol[:, n:n + 3], b.rearrange("(k p) -> p k", p=P), allow_slow_non_contiguous=True).then_inc(loaded_w, 16)
            for n, b in ((B1, b1), (B2, b2), (B_C1, c1b), (B_C2, c2b), (B_L2, L2b)):
                act.dma_start(bcol[:, n:n + 1], b.rearrange("(p a) -> p a", a=1), allow_slow_non_contiguous=True).then_inc(loaded_w, 16)
            act.wait_ge(att_zeroed, 1)
            for h in range(HEADS):
                for side in range(2):
                    act.dma_start(att[h * HEAD_F:(h + 1) * HEAD_F, side * HEADS + h:side * HEADS + h + 1],
                                  L3a[h, side * HEAD_F:(side + 1) * HEAD_F].rearrange("(p a) -> p a", a=1), allow_slow_non_contiguous=True).then_inc(loaded_w, 16)
            act.wait_ge(weights_turned, 1)
            act.activation(wT[:, :, :].rearrange("p k d -> p (k d)"), PS[:, 0:12 * FEAT], ACT.Copy).then_inc(weights_ready, 1)
            act.activation(w3a[:, :], bank(4, FEAT + 2 * HEADS), ACT.Copy).then_inc(weights_ready, 1)
            with act.Fori(0, GROUPS) as i:
                act.wait_ge(x_turned, i + 1)
                act.activation(xT[:, ds(i * GW, GW)], region(1), ACT.Copy).then_inc(xT_ready, 1)
            def typed(k):
                def unit(i, j, half, first):
                    u = 2 * j + half
                    act.wait_ge(typed_done[k], i * (2 * GROUP) + u + 1)
                    if not first and half == 0:
                        act.wait_ge(typed_written[k][j], i * 16)
                    act.activation(typed_out[:, j, 512 * half:512 * half + 512], bank(u % 5), ACT.Copy).then_inc(typed_evac[k], 1)
                for j in range(GROUP):
                    for half in range(2):
                        unit(0, j, half, True)
                with act.Fori(1, GROUPS) as i:
                    for j in range(GROUP):
                        for half in range(2):
                            unit(i, j, half, False)

            typed(0)
            for at, (cut, codes) in enumerate(((CHUNKS, unit_code), (PAIRS, unit_src[PAIRS]))):
                act.wait_ge(rows_turned, at + 1)
                for q, cols in enumerate((codes, unit_dst[cut])):
                    act.activation(cols[:, :, :].rearrange("p a u -> p (a u)"), bank(2 * at + q, cut.halves * cut.units), ACT.Copy)\
                        .then_inc(lists_ready, 1)

            def columns(k, cols):
                def beat(u):
                    u = u(0)
                    if u.after(SLOTS):
                        act.wait_ge(product, u.count(-SLOTS, k))
                    act.activation(ix[:, u.slot, 0:1], cols[:, 0, ds(u.n, 1)], ACT.Copy).then_inc(ix_ready, 1)
                over_units(act, CHUNKS, beat, 0)

            def norm(k, i):
                act.wait_ge(var_ready[k], i + 1)
                act.activation(sd[:, :], mv[:, :, 1], ACT.Sqrt, bias=epst[:, 0:1]).then_inc(std_ready[k], 1)

            act.wait_ge(lists_ready, 4)
            columns(0, unit_code)

            def gru(i, first=False, last=False):
                if not last:
                    act.wait_ge(agg_turned[0], i + 1)
                    act.activation(mT[:, :], region(0), ACT.Copy).then_inc(agg_T[0], 1)
                if not first:
                    norm(0, i - 1)
                if not last:
                    act.wait_ge(gates_done, i * 4 + 1)
                    act.activation(gr[:, :], region(1), ACT.Sigmoid, bias=bcol[:, B_R:B_R + 1]).then_inc(gates_rz, 1)
                    act.wait_ge(gates_done, i * 4 + 2)
                    act.activation(gz[:, :], region(2), ACT.Sigmoid, bias=bcol[:, B_Z:B_Z + 1]).then_inc(gates_rz, 1)
                    act.wait_ge(n_pre, i + 1)
                    act.activation(gn[:, :], u2[:, :], ACT.Tanh, bias=bcol[:, B_IH + 2:B_IH + 3]).then_inc(n_ready, 1)
                if not first:
                    cols = ds(i * GW - GW, GW)
                    act.wait_ge(x_again[0], i)
                    act.activation(xT[:, cols], region(1), ACT.Copy).then_inc(x_T[0], 1)
                    act.wait_ge(linear_done[0], i)
                    act.activation(hT[:, cols], region(2), ACT.Relu, bias=bcol[:, B1:B1 + 1]).then_inc(hidden_T[0], 1)
            gru(0, first=True)
            with act.Fori(1, GROUPS) as i:
                gru(i)
            gru(GROUPS, last=True)
            act.wait_ge(lists_ready, 5)
            columns(1, unit_src[CHUNKS])

            def sage1(i, first=False, last=False):
                if not last:
                    act.wait_ge(agg_turned[1], i + 1)
                    act.activation(mT[:, :], region(0), ACT.Copy).then_inc(agg_T[1], 1)
                if not first:
                    act.wait_ge(linear2_done[1], i)
                    act.activation(hT[:, ds(i * GW - GW, GW)], region(2), ACT.Relu, bias=bcol[:, B2:B2 + 1]).then_inc(hidden2_T[1], 1)
                if not last:
                    act.wait_ge(linear_done[1], i + 1)
                    act.activation(cT[:, :], region(1), ACT.Relu, bias=bcol[:, B_C1:B_C1 + 1]).then_inc(hidden_T[1], 1)
            sage1(0, first=True)
            with act.Fori(1, GROUPS) as i:
                sage1(i)
            sage1(GROUPS, last=True)
            columns(2, unit_src[CHUNKS])

            def sage2(i, first=False, last=False):
                if not last:
                    act.wait_ge(agg_turned[2], i + 1)
                    act.activation(mT[:, :], region(0), ACT.Copy).then_inc(agg_T[2], 1)
                if not first:
                    norm(2, i - 1)
                if not last:
                    act.wait_ge(linear_done[2], i + 1)
                    act.activation(cT[:, :], region(1), ACT.Relu, bias=bcol[:, B_C2:B_C2 + 1]).then_inc(hidden_T[2], 1)
                if not first:
                    act.wait_ge(x_again[2], i)
                    act.activation(xT[:, ds(i * GW - GW, GW)], region(3), ACT.Copy).then_inc(x_T[2], 1)
            sage2(0, first=True)
            with act.Fori(1, GROUPS) as i:
                sage2(i)
            sage2(GROUPS, last=True)
            typed(1)
            columns(3, unit_code)

            def relational(i, first=False, last=False):
                if not last:
                    act.wait_ge(linear_done[3], i + 1)
                    act.activation(cT[:, :], region(0), ACT.Relu, bias=bcol[:, B_L2:B_L2 + 1]).then_inc(hidden_T[3], 1)
                if not first:
                    norm(3, i - 1)
                    act.wait_ge(x_again[3], i)
                    act.activation(xT[:, ds(i * GW - GW, GW)], region(2), ACT.Copy).then_inc(x_T[3], 1)
            relational(0, first=True)
            with act.Fori(1, GROUPS) as i:
                relational(i)
            relational(GROUPS, last=True)

            def beat(at):
                w = at(LEAD + LAG_EXP)
                if w.within():
                    act.wait_ge(logits, w.count())
                    act.activation(rescale[:, w.slot, :], dm[:, w.slot, :], ACT.Exp)
                    act.activation(wm[:, w.slot, :, :, HEAD_F], wd[:, w.slot, :, :], ACT.Exp).then_inc(weights, 1)
                u = at(0)
                if u.within():
                    if u.after(SLOTS):
                        act.wait_ge(weighted, u.count(-SLOTS))
                    act.activation(ix[:, u.slot, :], unit_src[PAIRS][:, :, ds(u.n, 1)].rearrange("p a b -> p (a b)"), ACT.Copy).then_inc(ix_ready, 1)
                o = at(LEAD)
                if o.within():
                    act.wait_ge(oh_ready, o.count(0, 4))
                    act.activation(oh[:, o.slot, :, :], ohm[:, o.slot, :, :], ACT.Copy, bias=1.0).then_inc(oh_float, 1)
                t = at(LEAD + LAG_TURN)
                if t.within():
                    act.wait_ge(turned, t.count())
                    act.activation(ohT[:, t.slot, :, :].rearrange("p a e -> p (a e)"), bank(0, UNIT), ACT.Identity, bias=onesf[:, 0:1])
                    act.activation(aT[:, t.slot, :, :].rearrange("p a e -> p (a e)"), PS[0:12, UNIT:2 * UNIT], ACT.Copy).then_inc(turned_sb, 1)
            over_units(act, PAIRS, beat, LEAD + LAG_LAST)

            with act.Fori(0, GROUPS) as i:
                norm(4, i)

        @block.tensor
        def _(pe):
            def turn_group(r, source, i):
                for j in range(GROUP):
                    last = pe.transpose(PS[:, 1024 * r + j * P:1024 * r + (j + 1) * P],
                                        source(i, j), identf[:, :])
                return last

            def linear(r, parts):
                for c0, n in ((0, 512), (512, GW - 512)):
                    for q, (w, feats) in enumerate(parts):
                        last = pe.matmul(PS[:, 1024 * r + c0:1024 * r + c0 + n], w, feats(c0, n),
                                         start=(q == 0), stop=(q == len(parts) - 1))
                return last

            def whole(tile):
                return lambda c0, n: tile[:, c0:c0 + n]

            def of(tile, i):
                return lambda c0, n: tile[:, ds(i * GW + c0, n)]

            def node_tile(i, j):
                return xn[:, ds(i * GW + j * P, P)]

            pe.wait_ge(const_ready, 1)
            pe.wait_ge(loaded_w, 16 * 29)
            for n in range(12):
                pe.transpose(PS[:, n * P:(n + 1) * P], wraw[:, n, :], identf[:, :])
            pe.transpose(PS[:, 2048:2048 + P], wraw[:, L3i, :], identf[:, :])
            pe.matmul(PS[:, 2048 + P:2048 + P + 2 * HEADS], wraw[:, L3i, :], att[:, :], start=True, stop=True).then_inc(weights_turned, 1)
            pe.wait_ge(weights_ready, 2)
            pe.wait_ge(loaded_x, 32)
            for i in range(GROUPS):
                turn_group(1, node_tile, i).then_inc(x_turned, 1)
                pe.wait_ge(xT_ready, i + 1)

            def buckets():
                pe.wait_ge(counted, TILES + 1)
                pe.matmul(bank(6, TILES + 1), onesf[:, :], rowtot[:, :], start=True, stop=True).then_inc(bucket_sums, 1)
                pe.matmul(bank(7, TILES + 1), below[:, :], rowtot[:, :], start=True, stop=True).then_inc(bucket_base, 1)
                pe.wait_ge(bad_ready, 1)
                pe.matmul(bank(5, 1), onesf[:, :], bad[:, 0:1], start=True, stop=True).then_inc(bad_sum, 1)

            def typed(k, w):
                def unit(i, j, half, first):
                    u = 2 * j + half
                    if not (first and u < 5):
                        pe.wait_ge(typed_evac[k], i * (2 * GROUP) + u - 4)
                    last = pe.matmul(bank(u % 5), xT[:, ds(i * GW + j * P, P)],
                                     w[:, 4 * half:4 * half + 4, :].rearrange("p t d -> p (t d)"), start=True, stop=(k == 1))
                    if k == 0:
                        last = pe.matmul(bank(u % 5), onesb[:, :], L0b_parts[:, 512 * half:512 * half + 512], start=False, stop=True)
                    last.then_inc(typed_done[k], 1)
                for i in range(GROUPS):
                    for j in range(GROUP):
                        for half in range(2):
                            unit(i, j, half, i == 0)
                    if k == 0 and i == 1:
                        buckets()

            pe.wait_ge(xT_ready, GROUPS)
            pe.wait_ge(bias_split, 1)
            typed(0, L0W_sb)
            pe.wait_ge(typed_evac[0], 10 * GROUPS)
            for at, cut in enumerate((CHUNKS, PAIRS)):
                pe.wait_ge(rows_float, at + 1)
                for q in range(2):
                    for half in range(cut.halves):
                        for j in range(cut.uj):
                            col = 512 * (2 * at + q) + half * cut.units + j * cut.uq
                            last = pe.transpose(PS[:, col:col + cut.uq], got_f[cut][:, q * cut.uj + j, half * P:(half + 1) * P],
                                                identf[0:cut.uq, 0:cut.uq])
                last.then_inc(rows_turned, 1)
            pe.wait_ge(lists_ready, 4)

            def sums(k, width):
                def beat(u):
                    u = u(0)
                    pe.wait_ge(oh_ready, u.count(0, k))
                    if u.after(4):
                        pe.wait_ge(acc_done, u.count(-4, k))
                    pe.wait_ge(arrived[u.slot], u.gathered(k))
                    pe.matmul(bank(u.slot % 4, width), oh[:, u.slot, 0, :], g[:, u.slot, 0, 0:width],
                              start=True, stop=True).then_inc(product, 1)
                over_units(pe, CHUNKS, beat, 0)

            sums(0, FEAT + 1)

            pe.wait_ge(acc_done, 1 * CHUNKS.units)
            for i in range(GROUPS + 1):
                if i > 0:
                    pe.wait_ge(y_T[0], i)
                    turn_group(3, lambda i, j: u1[:, j * P:(j + 1) * P], i - 1).then_inc(y_turned[0], 1)
                if i < GROUPS:
                    turn_group(0, lambda i, j: acc[:, ds(i * (GROUP * AW) + j * AW, P)], i).then_inc(agg_turned[0], 1)
                    pe.wait_ge(agg_T[0], i + 1)
                    if i > 1:
                        pe.wait_ge(rows_ready[0], i - 1)
                    linear(1, [(wT[:, IH, :], whole(mT)), (wT[:, HH, :], of(xT, i))]).then_inc(gates_done, 1)
                    linear(2, [(wT[:, IH + 1, :], whole(mT)), (wT[:, HH + 1, :], of(xT, i))]).then_inc(gates_done, 1)
                if i > 0:
                    pe.wait_ge(x_ready[0], i)
                if i < GROUPS:
                    linear(3, [(wT[:, HH + 2, :], of(xT, i))]).then_inc(gates_done, 1)
                    linear(0, [(wT[:, IH + 2, :], whole(mT))]).then_inc(gates_done, 1)
                    pe.wait_ge(gates_rz, 2 * i + 2)
                if i > 0:
                    if i == GROUPS:
                        pe.wait_ge(rows_ready[0], i - 1)
                    turn_group(1, node_tile, i - 1).then_inc(x_again[0], 1)
                    pe.wait_ge(x_T[0], i)
                    linear(2, [(wT[:, W1i, :], of(xT, i - 1))]).then_inc(linear_done[0], 1)
                    pe.wait_ge(hidden_T[0], i)
                    turn_group(1, lambda i, j: hT[:, ds(i * GW + j * P, P)], i - 1).then_inc(rows_turned_back[0], 1)
            pe.wait_ge(rows_ready[0], GROUPS)
            sums(1, FEAT)

            pe.wait_ge(acc_done, 2 * CHUNKS.units)
            for i in range(GROUPS + 1):
                if i < GROUPS:
                    pe.wait_ge(mean_ready[1], i + 1)
                    turn_group(0, lambda i, j: mn[:, j * P:(j + 1) * P], i).then_inc(agg_turned[1], 1)
                if i > 0:
                    pe.wait_ge(hidden_T[1], i)
                    linear(2, [(wT[:, W2i, :], whole(cT))]).then_inc(linear2_done[1], 1)
                if i < GROUPS:
                    pe.wait_ge(agg_T[1], i + 1)
                    linear(1, [(wT[:, C1L, :], whole(mT)), (wT[:, C1R, :], of(hT, i))]).then_inc(linear_done[1], 1)
                if i > 0:
                    pe.wait_ge(hidden2_T[1], i)
                    if i > 1:
                        pe.wait_ge(rows_ready[1], i - 1)
                    turn_group(3, lambda i, j: hT[:, ds(i * GW + j * P, P)], i - 1).then_inc(rows_turned_back[1], 1)
            pe.wait_ge(rows_ready[1], GROUPS)
            sums(2, FEAT)

            pe.wait_ge(acc_done, 3 * CHUNKS.units)
            for i in range(GROUPS + 1):
                if i > 0:
                    pe.wait_ge(y_T[2], i)
                    turn_group(2, lambda i, j: u1[:, j * P:(j + 1) * P], i - 1).then_inc(y_turned[2], 1)
                if i < GROUPS:
                    pe.wait_ge(mean_ready[2], i + 1)
                    turn_group(0, lambda i, j: mn[:, j * P:(j + 1) * P], i).then_inc(agg_turned[2], 1)
                    pe.wait_ge(agg_T[2], i + 1)
                    linear(1, [(wT[:, C2L, :], whole(mT)), (wT[:, C2R, :], of(hT, i))]).then_inc(linear_done[2], 1)
                if i > 0:
                    pe.wait_ge(x_ready[2], i)
                    if i > 1:
                        pe.wait_ge(x_T[2], i - 1)
                    turn_group(3, node_tile, i - 1).then_inc(x_again[2], 1)
            pe.wait_ge(x_T[2], GROUPS)
            typed(1, L2W_sb)
            pe.wait_ge(typed_evac[1], 10 * GROUPS)
            sums(3, FEAT)

            pe.wait_ge(acc_done, 4 * CHUNKS.units)
            for i in range(GROUPS + 1):
                if i > 0:
                    pe.wait_ge(y_T[3], i)
                    turn_group(1, lambda i, j: u1[:, j * P:(j + 1) * P], i - 1).then_inc(y_turned[3], 1)
                if i < GROUPS:
                    for j in range(GROUP):
                        pe.matmul(PS[:, j * P:(j + 1) * P], selfw[:, :], xT[:, ds(i * GW + j * P, P)], start=True, stop=False)
                        last = pe.matmul(PS[:, j * P:(j + 1) * P], acc[:, ds(i * (GROUP * AW) + j * AW, P)], identf[:, :],
                                         start=False, stop=True)
                    last.then_inc(linear_done[3], 1)
                if i > 0:
                    pe.wait_ge(x_ready[3], i)
                    turn_group(2, node_tile, i - 1).then_inc(x_again[3], 1)
                    pe.wait_ge(x_T[3], i)
                    if i > 1:
                        pe.wait_ge(rows_ready[3], i - 1)
                    WA = FEAT + 2 * HEADS
                    for j in range(GROUP):
                        at = 3072 + (j * WA if j < 3 else 512 + (j - 3) * WA)
                        last = pe.matmul(PS[:, at:at + WA], xT[:, ds(i * GW - GW + j * P, P)], w3a[:, :], start=True, stop=True)
                    last.then_inc(rows_turned_back[3], 1)
            pe.wait_ge(rows_ready[3], GROUPS)

            def beat(at):
                f = at(LAG_SPREAD)
                if f.within():
                    pe.wait_ge(split_ready, f.count())
                    if f.after(1):
                        pe.wait_ge(logits, f.count(-1))
                    for half in range(HALVES):
                        last = pe.matmul(PS[:, 2560 + 24 * half:2584 + 24 * half], ohT[:, f.slot, half, :],
                                         bmp[:, f.slot, :, :].rearrange("p k c -> p (k c)"), start=True, stop=True)
                    last.then_inc(spread, 1)
                s = at(LAG_SUM)
                if s.within():
                    pe.wait_ge(oh_float, s.count())
                    pe.wait_ge(weighted, s.count())
                    if s.after(2):
                        pe.wait_ge(acc_done, s.count(-2, 4))
                    for half in range(HALVES):
                        last = pe.matmul(bank(6 + s.slot % 2, AW), oh[:, s.slot, half, :], wm[:, s.slot, half, :, :].rearrange("p h f -> p (h f)"),
                                         start=(half == 0), stop=(half == HALVES - 1))
                    last.then_inc(product, 1)
                m = at(LAG_MASK)
                if m.within():
                    pe.wait_ge(turned_sb, m.count())
                    if m.after(2):
                        pe.wait_ge(seg_max, m.count(-2))
                    for half in range(HALVES):
                        b = 1 + 2 * (m.slot % 2) + half
                        pe.matmul(bank(b), ohm[:, m.slot, half, :], ident4[:, :, :].rearrange("p h e -> p (h e)"), start=True, stop=True)
                        for h in range(HEADS):
                            last = pe.matmul(PS[:, 512 * b + h * P:512 * b + (h + 1) * P], headsel[:, h, :], aT[:, m.slot, half, :],
                                             start=False, stop=True, skip_group_check=True)
                    last.then_inc(masked, 1)
                t = at(LAG_TURN)
                if t.within():
                    pe.wait_ge(oh_ready, t.count(0, 4))
                    if t.after(1):
                        pe.wait_ge(turned_sb, t.count(-1))
                    pe.wait_ge(arrived[t.slot], t.gathered(4))
                    for half in range(HALVES):
                        pe.matmul(PS[:, half * P:(half + 1) * P], ohm[:, t.slot, half, :], identb[:, :], start=True, stop=True)
                    for half in range(HALVES):
                        last = pe.matmul(PS[0:12, UNIT + half * P:UNIT + (half + 1) * P],
                                         g[:, t.slot, half, FEAT + HEADS:TROW].bitcast(BF16), identb[:, :], start=True, stop=True)
                    last.then_inc(turned, 1)
            over_units(pe, PAIRS, beat, LAG_LAST)

        @block.vector
        def _(dve):
            steps = [0]

            def link(ins):
                steps[0] += 1
                ins.then_inc(dve_seq, 1)
                dve.wait_ge(dve_seq, steps[0])

            dve.memset(att[:, :], 0.0).then_inc(att_zeroed, 1)
            link(dve.memset(L0b_parts[:, :], 0.0))
            dve.wait_ge(const_ready, 1)
            dve.wait_ge(loaded_w, 16 * 29)
            for p0 in (0, 32, 64):
                here = slice(p0, p0 + 1)
                raw, rest = L0b_raw[here, 0, :], L0b_raw[here, 1, :]
                for _ in range(p0 // 32):
                    link(dve.tensor_copy(L0b_parts[here, :], raw))
                    link(dve.tensor_tensor(rest, raw, L0b_parts[here, :], ALU.subtract))
                    raw, rest = rest, raw
                ins = dve.tensor_copy(L0b_parts[here, :], raw)
                if p0 < 64:
                    link(ins)
            ins.then_inc(bias_split, 1)
            dve.wait_ge(loaded_e, 16 * 8)
            dve.scalar_tensor_tensor(out=e_code[:, :], in0=e_code[:, :], scalar=float(TYPES), in1=e_type[:, :],
                                     op0=ALU.mult, op1=ALU.add).then_inc(code_ready, 1)
            link(dve.tensor_single_scalar(e_bkt[:, :], e_dst[:, :], P_BITS, ALU.arith_shift_right))
            link(dve.tensor_single_scalar(e_next[:, :], e_next[:, :], P_BITS, ALU.arith_shift_right))
            link(dve.tensor_tensor(e_f[:, :], e_bkt[:, :], e_next[:, :], ALU.is_gt))
            dve.tensor_reduce(bad[:, 0:1], e_f[:, :], AX.X, ALU.max).then_inc(bad_ready, 1)
            link(dve.tensor_copy(e_g[:, :], e_bkt[:, :]))
            dve.tensor_scalar(e_f[:, :], e_g[:, :], 0.0, None, ALU.is_equal).then_inc(compared, 1)
            for b in range(TILES + 1):
                now, other = (e_f, e_cum) if b % 2 == 0 else (e_cum, e_f)
                if b < TILES:
                    if b > 0:
                        dve.wait_ge(counted, b)
                    dve.tensor_scalar(other[:, :], e_g[:, :], float(b + 1), None, ALU.is_equal).then_inc(compared, 1)
                dve.wait_ge(compared, b + 1)
                dve.tensor_reduce(rowtot[:, b:b + 1], now[:, :], AX.X, ALU.add).then_inc(counted, 1)
            dve.wait_ge(bad_sum, 1)
            dve.tensor_scalar(flag[:, :], bank(5, 1), 1.0, None, ALU.min).then_inc(order_known, 1)
            CNT, END, START, FIRST, LAST, NUM, PEND, PSTART, SHIFT, HAS, ZERO = range(11)
            NO, TILE, ROW = range(3)

            def units_of(cut):
                link(dve.tensor_single_scalar(bki[:, 2, :], bki[:, 0, :], cut.bits, ALU.arith_shift_right))
                link(dve.tensor_single_scalar(bki[:, 3, :], bki[:, 1, :], cut.bits, ALU.arith_shift_right))
                link(dve.tensor_copy(bk[:, FIRST, :], bki[:, 2, :]))
                link(dve.tensor_copy(bk[:, LAST, :], bki[:, 3, :]))
                link(dve.tensor_scalar(bk[:, HAS, :], bk[:, CNT, :], 1.0, None, ALU.min))
                link(dve.tensor_tensor(bk[:, NUM, :], bk[:, LAST, :], bk[:, FIRST, :], ALU.subtract))
                link(dve.scalar_tensor_tensor(out=bk[:, NUM, :], in0=bk[:, NUM, :], scalar=1.0, in1=bk[:, HAS, :],
                                              op0=ALU.add, op1=ALU.mult))
                link(dve.tensor_tensor_scan(bk[:, PEND, :], bk[:, NUM, :], bk[:, ZERO, :], 0.0, ALU.add, ALU.add))
                link(dve.tensor_tensor(bk[:, PSTART, :], bk[:, PEND, :], bk[:, NUM, :], ALU.subtract))
                link(dve.tensor_tensor(bk[:, SHIFT, :], bk[:, FIRST, :], bk[:, PSTART, :], ALU.subtract))
                link(dve.tensor_copy(pr[cut][:, NO, :], unit_no[cut][:, :]))
                shape = [cut.uq, cut.uj, TILES]

                def per_tile(ap):
                    return ap.unsqueeze(1).broadcast_to(shape)

                def per_unit(ap):
                    return ap.unsqueeze(2).broadcast_to(shape)

                link(dve.tensor_tensor(prc[cut][:, :, :], per_unit(pr[cut][:, NO, :]), per_tile(bk[0:cut.uq, PEND, 0:TILES]), ALU.is_ge))
                link(dve.tensor_reduce(pr[cut][:, TILE, :], prc[cut][:, :, :], AX.X, ALU.add))
                link(dve.tensor_tensor(prd[cut][:, :, :], per_unit(pr[cut][:, TILE, :]), per_tile(lane[0:cut.uq, 0:TILES]), ALU.is_equal))
                link(dve.tensor_tensor(prd[cut][:, :, :], prd[cut][:, :, :], per_tile(bk[0:cut.uq, SHIFT, 0:TILES]), ALU.mult))
                link(dve.tensor_reduce(pr[cut][:, ROW, :], prd[cut][:, :, :], AX.X, ALU.add))
                link(dve.tensor_tensor(pr[cut][:, ROW, :], pr[cut][:, ROW, :], pr[cut][:, NO, :], ALU.add))
                link(dve.tensor_copy(unit_tile[cut][:, :], pr[cut][:, TILE, :]))
                return dve.tensor_scalar(unit_row[cut][:, :], pr[cut][:, ROW, :], float(cut.rows - 1), None, ALU.min)

            dve.wait_ge(bucket_base, 1)
            link(dve.tensor_copy(bk[:, CNT, :], bank(6, TILES + 1)))
            link(dve.memset(bk[:, ZERO, :], 0.0))
            link(dve.tensor_tensor_scan(bk[:, END, :], bk[:, CNT, :], bk[:, ZERO, :], 0.0, ALU.add, ALU.add))
            link(dve.tensor_tensor(bk[:, START, :], bk[:, END, :], bk[:, CNT, :], ALU.subtract))
            link(dve.tensor_tensor(base[:, :], bank(7, TILES + 1), bk[:, START, :], ALU.add))
            link(dve.tensor_scalar(base[:, :], base[:, :], -1.0, None, ALU.add))
            link(dve.tensor_copy(bki[:, 0, :], bk[:, START, :]))
            link(dve.tensor_scalar(bki[:, 1, :], bk[:, END, :], -1.0, 0.0, ALU.add, ALU.max))
            for cut in (CHUNKS, PAIRS):
                units_of(cut).then_inc(units_ready, 1)

            disorder = dve.value_load(flag[0:1, 0:1], min_val=0, max_val=1)
            with dve.If(disorder > 0):
                dve.memset(e_pos[:, :], 0.0).then_inc(sort_seq, 1)
                dve.memset(e_zero[:, :], 0.0).then_inc(sort_seq, 1)
                dve.wait_ge(sort_seq, 2)
                with dve.Fori(0, TILES + 1) as b:
                    dve.tensor_scalar(e_f[:, :], e_g[:, :], lane[:, ds(b, 1)], None, ALU.is_equal).then_inc(sort_seq, 1)
                    dve.wait_ge(sort_seq, b * 4 + 3)
                    dve.tensor_tensor_scan(e_cum[:, :], e_f[:, :], e_zero[:, :], 0.0, ALU.add, ALU.add).then_inc(sort_seq, 1)
                    dve.wait_ge(sort_seq, b * 4 + 4)
                    dve.scalar_tensor_tensor(out=e_cum[:, :], in0=e_cum[:, :], scalar=base[:, ds(b, 1)], in1=e_f[:, :],
                                             op0=ALU.add, op1=ALU.mult).then_inc(sort_seq, 1)
                    dve.wait_ge(sort_seq, b * 4 + 5)
                    dve.tensor_tensor(e_pos[:, :], e_pos[:, :], e_cum[:, :], ALU.add).then_inc(sort_seq, 1)
                    dve.wait_ge(sort_seq, b * 4 + 6)
                dve.memset(bad[:, 1:2], 0.0).then_inc(place_ready, 1)
            with dve.Else():
                dve.memset(bad[:, 1:2], 0.0).then_inc(place_ready, 1)

            dve.memset(acc[:, :], 0.0).then_inc(acc_zero, 1)

            dve.wait_ge(loaded_w, 16 * 29)
            link(dve.tensor_tensor(bcol[:, B_R:B_R + 1], bcol[:, B_IH:B_IH + 1], bcol[:, B_HH:B_HH + 1], ALU.add))
            link(dve.tensor_tensor(bcol[:, B_Z:B_Z + 1], bcol[:, B_IH + 1:B_IH + 2], bcol[:, B_HH + 1:B_HH + 2], ALU.add))

            for cut in (CHUNKS, PAIRS):
                dve.wait_ge(rows_got[cut], 16 * 2 * cut.uj)
                if cut is PAIRS:
                    link(dve.tensor_single_scalar(got_i[cut][:, 0:cut.uj, :], got_i[cut][:, 0:cut.uj, :], TYPE_BITS, ALU.arith_shift_right))
                link(dve.tensor_copy(got_f[cut][:, 0:cut.uj, :], got_i[cut][:, 0:cut.uj, :]))
                link(dve.tensor_scalar(pr[cut][:, TILE, :], pr[cut][:, TILE, :], float(-P), None, ALU.mult))
                for j in range(cut.uj):
                    ins = dve.tensor_scalar(got_f[cut][:, cut.uj + j, :], got_i[cut][:, cut.uj + j, :], pr[cut][:, TILE, j:j + 1], None, ALU.add)
                ins.then_inc(rows_float, 1)
            dve.wait_ge(lists_ready, 4)
            dve.tensor_single_scalar(unit_src[CHUNKS][:, :, :], unit_code[:, :, :], TYPE_BITS, ALU.arith_shift_right).then_inc(lists_ready, 1)
            dve.wait_ge(tiles_loaded, 32)

            def one_hot(k, u):
                if u.after(SLOTS):
                    dve.wait_ge(product, u.count(-SLOTS, k))
                dve.tensor_scalar(oh[:, u.slot, 0, :], lane[:, :], unit_dst[CHUNKS][:, 0, ds(u.n, 1)], None, ALU.is_equal).then_inc(oh_ready, 1)

            def one_hot_less_one(u):
                if u.after(SLOTS):
                    dve.wait_ge(product, u.count(-SLOTS, 4))
                for half in range(HALVES):
                    last = dve.tensor_scalar(ohm[:, u.slot, half, :], laneb[:, :], unit_dst[PAIRS][:, half, ds(u.n, 1)], 1.0,
                                             ALU.is_equal, ALU.subtract)
                last.then_inc(oh_ready, 1)

            tile_registers = [[dve.alloc_register(f"tile{q}_{n}") for n in range(4)] for q in range(2)]

            def tile_of(u, load):
                q, place = divmod((u.at + u.cut.skew) % 8, 4)
                if load and place == 0:
                    dve.load(tile_registers[q], tile_at[u.cut][0:1, ds(u.n + u.cut.skew, 4)])
                return dve.snap(tile_registers[q][place], min_val=0, max_val=TILES)

            def sums(k, width):
                if k > 0:
                    dve.memset(acc[:, :], 0.0).then_inc(acc_zero, 1)
                dve.wait_ge(acc_zero, k + 1)

                def beat(at):
                    now, add = at(0), at(4)
                    if now.within():
                        one_hot(k, now)
                    if add.within():
                        tile = tile_of(add, True)
                        dve.wait_ge(product, add.count(0, k))
                        if add.after(1):
                            dve.wait_ge(acc_done, add.count(-1, k))
                        dve.tensor_tensor(acc_cols(tile, width), acc_cols(tile, width), bank(add.slot % 4, width),
                                          ALU.add).then_inc(acc_done, 1)
                over_units(dve, CHUNKS, beat, 4)

            class Seq:

                def __init__(self, s, per):
                    self.s, self.per, self.i, self.n = s, per, 0, 0

                def begin(self, i):
                    self.i, self.n = i, 0

                def __call__(self, ins):
                    self.n += 1
                    ins.then_inc(self.s, 1)
                    dve.wait_ge(self.s, self.i * self.per + self.n)

                def end(self):
                    assert self.n == self.per, self.n

            def norm(k, i, seq, source, target):
                for j in range(GROUP):
                    ins = dve.bn_stats(stats[:, j, :], source(j))
                seq(ins)
                dve.sem_inc(dve_pace, 1)
                for j in range(GROUP):
                    ins = dve.bn_aggr(mv[:, j, :], stats[:, j, :])
                ins.then_inc(var_ready[k], 1)
                dve.wait_ge(std_ready[k], i + 1)
                seq(dve.reciprocal(rs[:, :], sd[:, :]))
                for j in range(GROUP):
                    ins = dve.tensor_scalar(target(i, j), source(j), mv[:, j, 0:1], rs[:, j:j + 1], ALU.subtract, ALU.mult)
                return ins

            def new_x(i, j):
                return xn[:, ds(i * GW + j * P, P)]

            sums(0, FEAT + 1)
            dve.wait_ge(acc_done, 1 * CHUNKS.units)
            degree = acc[:, :].rearrange("p (t a) -> p t a", a=AW)[:, 0:TILES, FEAT]
            link(dve.tensor_scalar(rdeg[:, :], degree, 1.0, None, ALU.max))
            link(dve.reciprocal(rdeg[:, :], rdeg[:, :]))
            seq_a, seq_b = Seq(sem("dve_gru"), 4), Seq(sem("dve_gru_norm"), 2)

            def gru(i, first=False, last=False):
                if not first:
                    seq_b.begin(i - 1)
                    dve.wait_ge(y_turned[0], i)
                    norm(0, i - 1, seq_b, lambda j: PS[:, 3072 + j * P:3072 + (j + 1) * P], new_x).then_inc(x_ready[0], 1)
                    seq_b.end()
                if not last:
                    seq_a.begin(i)
                    cols = ds(i * GW, GW)
                    dve.wait_ge(gates_rz, i * 2 + 1)
                    dve.wait_ge(gates_done, i * 4 + 3)
                    seq_a(dve.scalar_tensor_tensor(out=u1[:, :], in0=region(3), scalar=bcol[:, B_HH + 2:B_HH + 3], in1=gr[:, :],
                                                   op0=ALU.add, op1=ALU.mult))
                    dve.wait_ge(gates_done, i * 4 + 4)
                    dve.tensor_tensor(u2[:, :], u1[:, :], region(0), ALU.add).then_inc(n_pre, 1)
                    dve.wait_ge(n_ready, i + 1)
                    seq_a(dve.tensor_tensor(u1[:, :], xT[:, cols], gn[:, :], ALU.subtract))
                    dve.wait_ge(gates_rz, i * 2 + 2)
                    seq_a(dve.tensor_tensor(u1[:, :], u1[:, :], gz[:, :], ALU.mult))
                    seq_a(dve.tensor_tensor(u1[:, :], u1[:, :], gn[:, :], ALU.add))
                    dve.tensor_tensor(u1[:, :], u1[:, :], xT[:, cols], ALU.add).then_inc(y_T[0], 1)
                    seq_a.end()
                if not first:
                    dve.wait_ge(rows_turned_back[0], i)
                    dve.tensor_copy(rows[:, ds(i * GW - GW, GW)], region(1)).then_inc(rows_ready[0], 1)
            gru(0, first=True)
            with dve.Fori(1, GROUPS) as i:
                gru(i)
            gru(GROUPS, last=True)

            def mean(k, i):
                dve.tensor_tensor(mn[:, :].rearrange("p (j d) -> p j d", d=P),
                                  acc[:, ds(i * (GROUP * AW), GROUP * AW)].rearrange("p (j a) -> p j a", a=AW)[:, :, 0:P],
                                  rdeg[:, ds(i * GROUP, GROUP)].unsqueeze(2).broadcast_to([P, GROUP, P]), ALU.mult)\
                    .then_inc(mean_ready[k], 1)

            sums(1, FEAT)
            dve.wait_ge(acc_done, 2 * CHUNKS.units)
            def sage1(i, first=False, last=False):
                if not last:
                    if not first:
                        dve.wait_ge(agg_turned[1], i)
                    mean(1, i)
                if not first:
                    dve.wait_ge(rows_turned_back[1], i)
                    dve.tensor_copy(rows[:, ds(i * GW - GW, GW)], region(3)).then_inc(rows_ready[1], 1)
            sage1(0, first=True)
            with dve.Fori(1, GROUPS) as i:
                sage1(i)
            sage1(GROUPS, last=True)
            sums(2, FEAT)
            dve.wait_ge(acc_done, 3 * CHUNKS.units)
            seq_sage = Seq(sem("dve_sage"), 2)

            def sage2(i, first=False, last=False):
                if not last:
                    mean(2, i)
                if not first:
                    seq_sage.begin(i - 1)
                    dve.wait_ge(y_turned[2], i)
                    norm(2, i - 1, seq_sage, lambda j: PS[:, 2048 + j * P:2048 + (j + 1) * P], new_x).then_inc(x_ready[2], 1)
                    seq_sage.end()
                if not last:
                    dve.wait_ge(hidden_T[2], i + 1)
                    dve.tensor_tensor(u1[:, :], xT[:, ds(i * GW, GW)], cT[:, :], ALU.add).then_inc(y_T[2], 1)
            sage2(0, first=True)
            with dve.Fori(1, GROUPS) as i:
                sage2(i)
            sage2(GROUPS, last=True)

            sums(3, FEAT)
            dve.wait_ge(acc_done, 4 * CHUNKS.units)
            seq_rel = Seq(sem("dve_rel"), 2)
            rows_t = rows[:, :].rearrange("p (t d) -> p t d", d=TROW)

            def relational(i, first=False, last=False):
                if not first:
                    seq_rel.begin(i - 1)
                    dve.wait_ge(y_turned[3], i)
                    norm(3, i - 1, seq_rel, lambda j: PS[:, 1024 + j * P:1024 + (j + 1) * P], new_x).then_inc(x_ready[3], 1)
                    seq_rel.end()
                if not last:
                    dve.wait_ge(hidden_T[3], i + 1)
                    dve.tensor_tensor(u1[:, :], xT[:, ds(i * GW, GW)], cT[:, :], ALU.add).then_inc(y_T[3], 1)
                if not first:
                    dve.wait_ge(rows_turned_back[3], i)
                    WA = FEAT + 2 * HEADS
                    for at, t0, n in ((3072, 0, 3), (3584, 3, 2)):
                        p = PS[:, at:at + n * WA].rearrange("p (t d) -> p t d", d=WA)
                        dve.tensor_copy(rows[:, ds(i * (GROUP * TROW) + (t0 - GROUP) * TROW, n * TROW)].rearrange("p (t d) -> p t d", d=TROW)[:, :, 0:FEAT + HEADS],
                                        p[:, :, 0:FEAT + HEADS])
                        ins = dve.tensor_copy(state[:, ds(i * GROUP + (t0 - GROUP), n), 0:HEADS], p[:, :, FEAT + HEADS:WA])
                    ins.then_inc(rows_ready[3], 1)
            relational(0, first=True)
            with dve.Fori(1, GROUPS) as i:
                relational(i)
            relational(GROUPS, last=True)

            dve.wait_ge(rows_ready[3], GROUPS)
            score = rows_t[:, :, FEAT:FEAT + HEADS]
            part = [rows[:, :].bitcast(BF16).rearrange("p (t d) -> p t d", d=2 * TROW)[:, :, 2 * (FEAT + HEADS) + j:2 * TROW:3] for j in range(3)]
            link(dve.tensor_copy(part[0], score))
            link(dve.tensor_tensor(spl[:, 0, :, :], score, part[0], ALU.subtract))
            link(dve.tensor_copy(part[1], spl[:, 0, :, :]))
            link(dve.tensor_tensor(spl[:, 1, :, :], spl[:, 0, :, :], part[1], ALU.subtract))
            dve.tensor_copy(part[2], spl[:, 1, :, :]).then_inc(gat_rows, 1)
            dve.memset(state[:, TILES, :], 0.0)
            link(dve.tensor_tensor(spl[:, 0, :, :], score, state[:, 0:TILES, 0:HEADS], ALU.add))
            link(dve.scalar_tensor_tensor(out=state[:, 0:TILES, HEADS:2 * HEADS], in0=spl[:, 0, :, :], scalar=0.2,
                                          in1=spl[:, 0, :, :], op0=ALU.mult, op1=ALU.max))
            dve.memset(acc[:, TILES * AW:], 0.0)
            acc_f = acc[:, 0:TILES * AW].rearrange("p (t h f) -> p t h f", t=TILES, h=HEADS)
            dve.memset(acc_f[:, :, :, HEAD_F:HEAD_F + 1].rearrange("p t h f -> p (t h) f"), 1.0)
            dve.tensor_copy(acc_f[:, :, :, 0:HEAD_F], rows_t[:, :, 0:FEAT].rearrange("p t (h f) -> p t h f", h=HEADS))\
                .then_inc(acc_zero, 1)
            dve.wait_ge(acc_zero, 5)

            max_step, max_kept, logit_step, rescaled = sem("max_step"), sem("max_kept"), sem("logit_step"), sem("rescaled")

            def beat(at):
                now, m, e, a = at(0), at(LAG_MAX), at(LAG_LOGIT), at(LAG_ADD)
                do_now, do_m, do_e, do_a = (u.within() for u in (now, m, e, a))
                f = fs[:, e.slot, :, :]
                if do_m:
                    s = m.slot
                    dve.wait_ge(masked, m.count())
                    dve.tensor_reduce(cm[:, s, 0:4], bank(1 + 2 * (s % 2), 1024).rearrange("p (a h e) -> p h a e", a=HALVES, h=HEADS),
                                      AX.XY, ALU.max).then_inc(max_step, 1)
                if m.loads():
                    tile_m = tile_of(m, True)
                if do_m:
                    here = state[:, ds(tile_m, 1), :].rearrange("p a b -> p (a b)")
                if do_a:
                    tile_a = tile_of(a, False)
                    sums_here = acc_cols(tile_a, AW)
                    dve.wait_ge(weights, a.count())
                    if a.after(1):
                        dve.wait_ge(acc_done, a.count(-1, 4))
                    dve.tensor_tensor(sums_here.rearrange("p (h f) -> p h f", h=HEADS), sums_here.rearrange("p (h f) -> p h f", h=HEADS),
                                      rescale[:, a.slot, :].unsqueeze(2).broadcast_to([P, HEADS, HEAD_F + 1]), ALU.mult)\
                        .then_inc(rescaled, 1)
                if do_e:
                    dve.wait_ge(spread, e.count())
                    dve.tensor_reduce(f, bank(5, 24 * HALVES).rearrange("p (a k c) -> p a c k", a=HALVES, k=3), AX.X, ALU.add)\
                        .then_inc(logit_step, 1)
                if do_m:
                    if m.after(1):
                        dve.wait_ge(max_kept, m.count(-1))
                    dve.wait_ge(max_step, m.n * 5 + 1)
                    dve.tensor_tensor(cm[:, s, 4:8], cm[:, s, 0:4], here[:, 0:4], ALU.add).then_inc(max_step, 1)
                if do_e:
                    dve.wait_ge(logit_step, e.n * 4 + 1)
                    dve.tensor_tensor(lg[:, e.slot, 0, :, :], g[:, e.slot, :, FEAT:FEAT + HEADS], f[:, :, 0:4], ALU.add).then_inc(logit_step, 1)
                if do_m:
                    dve.wait_ge(max_step, m.n * 5 + 2)
                    dve.scalar_tensor_tensor(out=cm[:, s, 8:12], in0=cm[:, s, 4:8], scalar=0.2, in1=cm[:, s, 4:8],
                                             op0=ALU.mult, op1=ALU.max).then_inc(max_step, 1)
                if do_e:
                    dve.wait_ge(logit_step, e.n * 4 + 2)
                    dve.scalar_tensor_tensor(out=lg[:, e.slot, 1, :, :], in0=lg[:, e.slot, 0, :, :], scalar=0.2, in1=lg[:, e.slot, 0, :, :],
                                             op0=ALU.mult, op1=ALU.max).then_inc(logit_step, 1)
                if do_m:
                    dve.wait_ge(max_step, m.n * 5 + 3)
                    dve.tensor_tensor(bm[:, s, 4:8], cm[:, s, 8:12], here[:, 4:8], ALU.max).then_inc(max_step, 1)
                if do_e:
                    dve.wait_ge(logit_step, e.n * 4 + 3)
                    dve.tensor_tensor(lg[:, e.slot, 2, :, :], lg[:, e.slot, 1, :, :], f[:, :, 4:8], ALU.subtract).then_inc(logit_step, 1)
                if do_m:
                    dve.wait_ge(max_step, m.n * 5 + 4)
                    dve.tensor_scalar(bm[:, s, 0:4], here[:, 0:4], 1.0, None, ALU.mult).then_inc(seg_max, 1)
                    dve.tensor_tensor(dm[:, s, :], here[:, 4:8], bm[:, s, 4:8], ALU.subtract).then_inc(max_step, 1)
                if do_e:
                    dve.wait_ge(logit_step, e.n * 4 + 4)
                    dve.tensor_scalar(wd[:, e.slot, :, :], lg[:, e.slot, 2, :, :], 0.0, None, ALU.min).then_inc(logits, 1)
                if do_now:
                    one_hot_less_one(now)
                if do_m:
                    dve.wait_ge(max_step, m.n * 5 + 5)
                    dve.tensor_scalar(here[:, 4:8], bm[:, s, 4:8], 1.0, None, ALU.mult).then_inc(max_kept, 1)
                if do_a:
                    dve.wait_ge(rescaled, a.count())
                    dve.wait_ge(product, a.count(0, 4))
                    dve.tensor_tensor(sums_here, sums_here, bank(6 + a.slot % 2, AW), ALU.add).then_inc(acc_done, 1)
            over_units(dve, PAIRS, beat, LAG_LAST)

            dve.wait_ge(acc_done, 4 * CHUNKS.units + PAIRS.units)
            accv = acc[:, 0:TILES * AW].rearrange("p (t h f) -> p t h f", t=TILES, h=HEADS)
            link(dve.tensor_scalar(den[:, :, :], accv[:, :, :, HEAD_F], 1e-10, None, ALU.max))
            link(dve.reciprocal(den[:, :, :], den[:, :, :]))
            seq = Seq(sem("dve_out"), 5)
            with dve.Fori(0, GROUPS) as i:
                seq.begin(i)
                here = acc[:, ds(i * (GROUP * AW), GROUP * AW)].rearrange("p (q f) -> p q f", f=HEAD_F + 1)
                seq(dve.tensor_tensor(u1[:, :].rearrange("p (q f) -> p q f", f=HEAD_F), here[:, :, 0:HEAD_F],
                                      den[:, ds(i * GROUP, GROUP), :].rearrange("p t h -> p (t h)").unsqueeze(2)
                                      .broadcast_to([P, GROUP * HEADS, HEAD_F]), ALU.mult))
                seq(dve.tensor_tensor(u1[:, :].rearrange("p (j d) -> p j d", d=P), u1[:, :].rearrange("p (j d) -> p j d", d=P),
                                      L3b_bc[:, :].unsqueeze(1).broadcast_to([P, GROUP, P]), ALU.add))
                seq(dve.tensor_tensor(u1[:, :], u1[:, :], xn[:, ds(i * GW, GW)], ALU.add))
                norm(4, i, seq, lambda j: u1[:, j * P:(j + 1) * P],
                     lambda i, j: rows[:, ds(i * GW + j * P, P)]).then_inc(out_rows, 1)
                dve.wait_ge(out_rows, i + 1)
                seq.end()


_INS = ['x', 'src', 'dst', 'edge_type_8', 'L0_gnn_message_W', 'L0_gnn_message_b', 'L0_gnn_gru_w_ih', 'L0_gnn_gru_w_hh',
        'L0_gnn_gru_b_ih', 'L0_gnn_gru_b_hh', 'L1_gnn_W1', 'L1_gnn_b1', 'L1_gnn_W2', 'L1_gnn_b2', 'L1_gnn_c1_Wl',
        'L1_gnn_c1_bl', 'L1_gnn_c1_Wr', 'L1_gnn_c2_Wl', 'L1_gnn_c2_bl', 'L1_gnn_c2_Wr', 'L2_gnn_weight',
        'L2_gnn_self_loop_weight', 'L2_gnn_bias', 'L3_gnn_W', 'L3_gnn_att', 'L3_gnn_bias']


def kernel(**inputs):
    import numpy as _np
    import concourse.bacc as _bacc
    from concourse import mybir as _mybir
    from concourse.bass_utils import run_bass_kernel_spmd as _run

    nc = _bacc.Bacc("TRN2", target_bir_lowering=False, num_devices=1)
    arrays, args = {}, []
    for name in _INS:
        a = _np.ascontiguousarray(inputs[name])
        arrays[f"in_{name}_dram"] = a
        args.append(nc.dram_tensor(f"in_{name}_dram", a.shape, _mybir.dt.from_np(a.dtype), kind="ExternalInput").ap())
    args.append(nc.dram_tensor("out_0_dram", (NODES, FEAT), F32, kind="ExternalOutput").ap())
    build(nc, *args)
    r = _run(nc, [arrays], core_ids=[0])
    return r.results[0]["out_0_dram"]
```
